# Optimizing a Trainium2 kernel written in Bass

```python
import numpy as np
import jax
import jax.numpy as jnp

def _softmax(x, axis=-1):
    return jax.nn.softmax(x, axis=axis)

def _gelu(x):
    return jax.nn.gelu(x, approximate=True)

def _silu(x):
    return jax.nn.silu(x)

def _sigmoid(x):
    return jax.nn.sigmoid(x)

def _layernorm(x, axis=-1, eps=1e-05):
    m = jnp.mean(x, axis=axis, keepdims=True)
    v = jnp.var(x, axis=axis, keepdims=True)
    return (x - m) / jnp.sqrt(v + eps)

def _scatter_add(tgt, idx, src, axis=0):
    return tgt.at[idx].add(src)

def _segment_sum(src, seg, n):
    return jax.ops.segment_sum(src, seg, n)
kernel_name = 'mk_pixart_seq_d4_seqx_r4_fccd5d'

def setup_inputs(seed: int=0):
    np.random.seed(seed)
    _w = jnp.asarray

    def _rec_inputs():
        import jax
        import jax.numpy as jnp
        _rk = jax.random.key(seed)
        x = -0.0003929 + 0.9999 * jax.random.normal(jax.random.fold_in(_rk, 1), (16, 256, 256), jnp.float32)
        _lenS = 256 - jax.random.randint(jax.random.fold_in(_rk, 7), (16,), 0, max(1, 256 // 4) + 1, jnp.int32)
        _lenS2 = 77 - jax.random.randint(jax.random.fold_in(_rk, 8), (16,), 0, max(1, 77 // 4) + 1, jnp.int32)
        cond_1024 = 0.00782532 + 1.00527 * jax.random.normal(jax.random.fold_in(_rk, 11), (16, 256), jnp.float32)
        _ctx_1024P = jax.random.normal(jax.random.fold_in(_rk, 12), (16, 16, 256), jnp.float32)
        _ctx_1024c = jax.random.dirichlet(jax.random.fold_in(_rk, 512), 0.3 * jnp.ones((16,), jnp.float32), (16, 77))
        _ctx_1024t = jnp.einsum('bsk,bkd->bsd', _ctx_1024c, _ctx_1024P)
        _ctx_1024t = _ctx_1024t * jax.lax.rsqrt(jnp.mean(jnp.square(_ctx_1024t)) + 1e-12) * 0.953939
        ctx_1024 = -0.000761806 + 0.999296 * (_ctx_1024t + 0.3 * jax.random.normal(jax.random.fold_in(_rk, 612), (16, 77, 256), jnp.float32))
        return (x, cond_1024, ctx_1024)
    x, cond_1024, ctx_1024 = _rec_inputs()

    def _L0_xcond_setup():
        import jax, jax.numpy as jnp
        import numpy as np
        H = 256
        RH = 2 * H
        E = 3
        B, T, P = (8, 512, 64)
        LN_EPS = 1e-05

        def _layer_norm(x, gamma, beta):
            mu = jnp.mean(x, axis=-1, keepdims=True)
            var = jnp.mean(jnp.square(x - mu), axis=-1, keepdims=True)
            return (x - mu) * jax.lax.rsqrt(var + LN_EPS) * gamma + beta
        key = jax.random.key(seed)
        ks = jax.random.split(key, 24)
        s = lambda fan_in: 1.0 / np.sqrt(fan_in)
        inp = {'mix_hidden_states': jax.random.normal(ks[0], (B, T, H), jnp.float32), 'global_anchor': jax.random.normal(ks[1], (B, H), jnp.float32), 'prototype_bank': jax.random.normal(ks[2], (B, P, H), jnp.float32), 'ln_gamma': jnp.ones((H,), jnp.float32), 'ln_beta': jnp.zeros((H,), jnp.float32), 'Wq': jax.random.normal(ks[3], (H, H), jnp.float32) * s(H), 'Wk': jax.random.normal(ks[4], (H, H), jnp.float32) * s(H), 'Wv': jax.random.normal(ks[5], (H, H), jnp.float32) * s(H), 'router_W': jax.random.normal(ks[6], (3 * H, E), jnp.float32) * s(3 * H), 'router_b': jnp.zeros((E,), jnp.float32), 'e_w1': jax.random.normal(ks[7], (E, 3 * H, RH), jnp.float32) * s(3 * H), 'e_b1': jnp.zeros((E, RH), jnp.float32), 'e_w2': jax.random.normal(ks[8], (E, RH, H), jnp.float32) * s(RH), 'e_b2': jnp.zeros((E, H), jnp.float32), 'gate_w1': jax.random.normal(ks[9], (3 * H, H), jnp.float32) * s(3 * H), 'gate_b1': jnp.zeros((H,), jnp.float32), 'gate_w2': jax.random.normal(ks[10], (H, H), jnp.float32) * s(H), 'gate_b2': jnp.zeros((H,), jnp.float32), 'out_w': jax.random.normal(ks[11], (H, H), jnp.float32) * s(H), 'out_b': jnp.zeros((H,), jnp.float32)}
        return inp
    _L0_xcond_all = _L0_xcond_setup()
    _L0_xcond_in = {k: v for k, v in _L0_xcond_all.items() if k in ('ln_gamma', 'ln_beta', 'Wq', 'Wk', 'Wv', 'router_W', 'router_b', 'e_w1', 'e_b1', 'e_w2', 'e_b2', 'gate_w1', 'gate_b1', 'gate_w2', 'gate_b2', 'out_w', 'out_b')}
    del _L0_xcond_all

    def _L1_xcond_setup():
        import jax, jax.numpy as jnp
        import numpy as np
        LN_EPS = 1e-06

        def _ln(x):
            mu = jnp.mean(x, axis=-1, keepdims=True)
            var = jnp.var(x, axis=-1, keepdims=True)
            return (x - mu) * jax.lax.rsqrt(var + LN_EPS)
        key = jax.random.key(seed)
        H, NH = (256, 16)
        B, N, S = (4, 256, 77)
        MLP = int(H * 4.0)
        ks = jax.random.split(key, 20)
        s = 1.0 / np.sqrt(H)
        return {'x': jax.random.normal(ks[0], (B, N, H), jnp.float32), 'c': jax.random.normal(ks[1], (B, H), jnp.float32), 'context': jax.random.normal(ks[2], (B, S, H), jnp.float32), 'W_mod': jax.random.normal(ks[3], (H, 6 * H), jnp.float32) * s, 'b_mod': jnp.zeros((6 * H,), jnp.float32), 'W_qkv': jax.random.normal(ks[4], (H, 3 * H), jnp.float32) * s, 'b_qkv': jnp.zeros((3 * H,), jnp.float32), 'W_proj': jax.random.normal(ks[5], (H, H), jnp.float32) * s, 'b_proj': jnp.zeros((H,), jnp.float32), 'W_qc': jax.random.normal(ks[6], (H, H), jnp.float32) * s, 'b_qc': jnp.zeros((H,), jnp.float32), 'W_kvc': jax.random.normal(ks[7], (H, 2 * H), jnp.float32) * s, 'b_kvc': jnp.zeros((2 * H,), jnp.float32), 'W_cproj': jax.random.normal(ks[8], (H, H), jnp.float32) * s, 'b_cproj': jnp.zeros((H,), jnp.float32), 'W_mlp1': jax.random.normal(ks[9], (H, MLP), jnp.float32) * s, 'b_mlp1': jnp.zeros((MLP,), jnp.float32), 'W_mlp2': jax.random.normal(ks[10], (MLP, H), jnp.float32) * (1.0 / np.sqrt(MLP)), 'b_mlp2': jnp.zeros((H,), jnp.float32)}
    _L1_xcond_all = _L1_xcond_setup()
    _L1_xcond_in = {k: v for k, v in _L1_xcond_all.items() if k in ('W_mod', 'b_mod', 'W_qkv', 'b_qkv', 'W_proj', 'b_proj', 'W_qc', 'b_qc', 'W_kvc', 'b_kvc', 'W_cproj', 'b_cproj', 'W_mlp1', 'b_mlp1', 'W_mlp2', 'b_mlp2')}
    del _L1_xcond_all

    def _L2_xcond_setup():
        import jax, jax.numpy as jnp
        import numpy as np
        D = 256
        H = 16
        HD = D // H
        MLP = 4 * D
        EPS = 1e-06
        SCALE = HD ** (-0.5)

        def _p(key, shape, s=0.02):
            return jax.random.normal(key, shape, dtype=jnp.float32) * s

        def _ln(x):
            mu = jnp.mean(x, axis=-1, keepdims=True)
            var = jnp.var(x, axis=-1, keepdims=True)
            return (x - mu) * jax.lax.rsqrt(var + EPS)

        def _heads(t):
            B, L, _ = t.shape
            return t.reshape(B, L, H, HD).transpose(0, 2, 1, 3)

        def _attend(q, k, v):
            attn = jnp.einsum('bhnd,bhsd->bhns', q, k) * SCALE
            attn = jax.nn.softmax(attn, axis=-1)
            o = jnp.einsum('bhns,bhsd->bhnd', attn, v)
            B, _, N, _ = q.shape
            return o.transpose(0, 2, 1, 3).reshape(B, N, D)
        key = jax.random.key(seed)
        ks = jax.random.split(key, 24)
        B, N, S = (4, 256, 77)
        return {'x': jax.random.normal(ks[0], (B, N, D), dtype=jnp.float32), 't_emb': jax.random.normal(ks[1], (B, D), dtype=jnp.float32), 'context': jax.random.normal(ks[2], (B, S, D), dtype=jnp.float32), 'adaln_w': _p(ks[3], (D, 6 * D)), 'adaln_b': _p(ks[4], (6 * D,)), 'qkv_w': _p(ks[5], (D, 3 * D)), 'qkv_b': _p(ks[6], (3 * D,)), 'sa_proj_w': _p(ks[7], (D, D)), 'sa_proj_b': _p(ks[8], (D,)), 'q_w': _p(ks[9], (D, D)), 'q_b': _p(ks[10], (D,)), 'kv_w': _p(ks[11], (D, 2 * D)), 'kv_b': _p(ks[12], (2 * D,)), 'ca_proj_w': _p(ks[13], (D, D)), 'ca_proj_b': _p(ks[14], (D,)), 'fc1_w': _p(ks[15], (D, MLP)), 'fc1_b': _p(ks[16], (MLP,)), 'fc2_w': _p(ks[17], (MLP, D)), 'fc2_b': _p(ks[18], (D,))}
    _L2_xcond_all = _L2_xcond_setup()
    _L2_xcond_in = {k: v for k, v in _L2_xcond_all.items() if k in ('adaln_w', 'adaln_b', 'qkv_w', 'qkv_b', 'sa_proj_w', 'sa_proj_b', 'q_w', 'q_b', 'kv_w', 'kv_b', 'ca_proj_w', 'ca_proj_b', 'fc1_w', 'fc1_b', 'fc2_w', 'fc2_b')}
    del _L2_xcond_all

    def _L3_xcond_setup():
        import jax, jax.numpy as jnp
        import numpy as np
        D = 256
        H = 16
        DH = D // H
        DFF = 1024
        B = 2
        L = 512
        EPS = 1e-05

        def layer_norm(x, g, b):
            mu = jnp.mean(x, axis=-1, keepdims=True)
            var = jnp.mean(jnp.square(x - mu), axis=-1, keepdims=True)
            return (x - mu) * jax.lax.rsqrt(var + EPS) * g + b

        def ada_ln(x, t_emb, ln_g, ln_b, aff_w, aff_b):
            normed = layer_norm(x, ln_g, ln_b)
            affine = t_emb @ aff_w + aff_b
            gamma, beta = jnp.split(affine, 2, axis=-1)
            return gamma[:, None, :] * normed + beta[:, None, :]

        def mha(q_in, k_in, v_in, qw, qb, kw, kb, vw, vb, ow, ob):
            Bq, Lq, _ = q_in.shape
            Lk = k_in.shape[1]
            Q = (q_in @ qw + qb).reshape(Bq, Lq, H, DH)
            K = (k_in @ kw + kb).reshape(Bq, Lk, H, DH)
            V = (v_in @ vw + vb).reshape(Bq, Lk, H, DH)
            scores = jnp.einsum('bqhd,bkhd->bhqk', Q, K) / np.sqrt(DH).astype(np.float32)
            attn = jax.nn.softmax(scores, axis=-1)
            out = jnp.einsum('bhqk,bkhd->bqhd', attn, V).reshape(Bq, Lq, D)
            return out @ ow + ob
        key = jax.random.key(seed)
        ks = jax.random.split(key, 32)
        s = lambda k, shape, scale=0.02: jax.random.normal(k, shape, dtype=jnp.float32) * scale
        inp = {'x': jax.random.normal(ks[0], (B, L, D), dtype=jnp.float32), 'u': jax.random.normal(ks[1], (B, L, D), dtype=jnp.float32), 't_emb': jax.random.normal(ks[2], (B, D), dtype=jnp.float32), 'ln1_g': jnp.ones((D,), jnp.float32), 'ln1_b': jnp.zeros((D,), jnp.float32), 'aff1_w': s(ks[3], (D, 2 * D)), 'aff1_b': jnp.zeros((2 * D,), jnp.float32), 'ln2_g': jnp.ones((D,), jnp.float32), 'ln2_b': jnp.zeros((D,), jnp.float32), 'aff2_w': s(ks[4], (D, 2 * D)), 'aff2_b': jnp.zeros((2 * D,), jnp.float32), 'sa_qw': s(ks[5], (D, D)), 'sa_qb': jnp.zeros((D,), jnp.float32), 'sa_kw': s(ks[6], (D, D)), 'sa_kb': jnp.zeros((D,), jnp.float32), 'sa_vw': s(ks[7], (D, D)), 'sa_vb': jnp.zeros((D,), jnp.float32), 'sa_ow': s(ks[8], (D, D)), 'sa_ob': jnp.zeros((D,), jnp.float32), 'ca_qw': s(ks[9], (D, D)), 'ca_qb': jnp.zeros((D,), jnp.float32), 'ca_kw': s(ks[10], (D, D)), 'ca_kb': jnp.zeros((D,), jnp.float32), 'ca_vw': s(ks[11], (D, D)), 'ca_vb': jnp.zeros((D,), jnp.float32), 'ca_ow': s(ks[12], (D, D)), 'ca_ob': jnp.zeros((D,), jnp.float32), 'ffn_w1': s(ks[13], (D, DFF)), 'ffn_b1': jnp.zeros((DFF,), jnp.float32), 'ffn_w2': s(ks[14], (DFF, D)), 'ffn_b2': jnp.zeros((D,), jnp.float32)}
        return inp
    _L3_xcond_all = _L3_xcond_setup()
    _L3_xcond_in = {k: v for k, v in _L3_xcond_all.items() if k in ('ln1_g', 'ln1_b', 'aff1_w', 'aff1_b', 'ln2_g', 'ln2_b', 'aff2_w', 'aff2_b', 'sa_qw', 'sa_qb', 'sa_kw', 'sa_kb', 'sa_vw', 'sa_vb', 'sa_ow', 'sa_ob', 'ca_qw', 'ca_qb', 'ca_kw', 'ca_kb', 'ca_vw', 'ca_vb', 'ca_ow', 'ca_ob', 'ffn_w1', 'ffn_b1', 'ffn_w2', 'ffn_b2')}
    del _L3_xcond_all
    return {'x': x, 'cond_1024': cond_1024, 'ctx_1024': ctx_1024, 'L0_xcond_ln_gamma': _L0_xcond_in['ln_gamma'], 'L0_xcond_ln_beta': _L0_xcond_in['ln_beta'], 'L0_xcond_Wq': _L0_xcond_in['Wq'], 'L0_xcond_Wk': _L0_xcond_in['Wk'], 'L0_xcond_Wv': _L0_xcond_in['Wv'], 'L0_xcond_router_W': _L0_xcond_in['router_W'], 'L0_xcond_router_b': _L0_xcond_in['router_b'], 'L0_xcond_e_w1': _L0_xcond_in['e_w1'], 'L0_xcond_e_b1': _L0_xcond_in['e_b1'], 'L0_xcond_e_w2': _L0_xcond_in['e_w2'], 'L0_xcond_e_b2': _L0_xcond_in['e_b2'], 'L0_xcond_gate_w1': _L0_xcond_in['gate_w1'], 'L0_xcond_gate_b1': _L0_xcond_in['gate_b1'], 'L0_xcond_gate_w2': _L0_xcond_in['gate_w2'], 'L0_xcond_gate_b2': _L0_xcond_in['gate_b2'], 'L0_xcond_out_w': _L0_xcond_in['out_w'], 'L0_xcond_out_b': _L0_xcond_in['out_b'], 'L1_xcond_W_mod': _L1_xcond_in['W_mod'], 'L1_xcond_b_mod': _L1_xcond_in['b_mod'], 'L1_xcond_W_qkv': _L1_xcond_in['W_qkv'], 'L1_xcond_b_qkv': _L1_xcond_in['b_qkv'], 'L1_xcond_W_proj': _L1_xcond_in['W_proj'], 'L1_xcond_b_proj': _L1_xcond_in['b_proj'], 'L1_xcond_W_qc': _L1_xcond_in['W_qc'], 'L1_xcond_b_qc': _L1_xcond_in['b_qc'], 'L1_xcond_W_kvc': _L1_xcond_in['W_kvc'], 'L1_xcond_b_kvc': _L1_xcond_in['b_kvc'], 'L1_xcond_W_cproj': _L1_xcond_in['W_cproj'], 'L1_xcond_b_cproj': _L1_xcond_in['b_cproj'], 'L1_xcond_W_mlp1': _L1_xcond_in['W_mlp1'], 'L1_xcond_b_mlp1': _L1_xcond_in['b_mlp1'], 'L1_xcond_W_mlp2': _L1_xcond_in['W_mlp2'], 'L1_xcond_b_mlp2': _L1_xcond_in['b_mlp2'], 'L2_xcond_adaln_w': _L2_xcond_in['adaln_w'], 'L2_xcond_adaln_b': _L2_xcond_in['adaln_b'], 'L2_xcond_qkv_w': _L2_xcond_in['qkv_w'], 'L2_xcond_qkv_b': _L2_xcond_in['qkv_b'], 'L2_xcond_sa_proj_w': _L2_xcond_in['sa_proj_w'], 'L2_xcond_sa_proj_b': _L2_xcond_in['sa_proj_b'], 'L2_xcond_q_w': _L2_xcond_in['q_w'], 'L2_xcond_q_b': _L2_xcond_in['q_b'], 'L2_xcond_kv_w': _L2_xcond_in['kv_w'], 'L2_xcond_kv_b': _L2_xcond_in['kv_b'], 'L2_xcond_ca_proj_w': _L2_xcond_in['ca_proj_w'], 'L2_xcond_ca_proj_b': _L2_xcond_in['ca_proj_b'], 'L2_xcond_fc1_w': _L2_xcond_in['fc1_w'], 'L2_xcond_fc1_b': _L2_xcond_in['fc1_b'], 'L2_xcond_fc2_w': _L2_xcond_in['fc2_w'], 'L2_xcond_fc2_b': _L2_xcond_in['fc2_b'], 'L3_xcond_ln1_g': _L3_xcond_in['ln1_g'], 'L3_xcond_ln1_b': _L3_xcond_in['ln1_b'], 'L3_xcond_aff1_w': _L3_xcond_in['aff1_w'], 'L3_xcond_aff1_b': _L3_xcond_in['aff1_b'], 'L3_xcond_ln2_g': _L3_xcond_in['ln2_g'], 'L3_xcond_ln2_b': _L3_xcond_in['ln2_b'], 'L3_xcond_aff2_w': _L3_xcond_in['aff2_w'], 'L3_xcond_aff2_b': _L3_xcond_in['aff2_b'], 'L3_xcond_sa_qw': _L3_xcond_in['sa_qw'], 'L3_xcond_sa_qb': _L3_xcond_in['sa_qb'], 'L3_xcond_sa_kw': _L3_xcond_in['sa_kw'], 'L3_xcond_sa_kb': _L3_xcond_in['sa_kb'], 'L3_xcond_sa_vw': _L3_xcond_in['sa_vw'], 'L3_xcond_sa_vb': _L3_xcond_in['sa_vb'], 'L3_xcond_sa_ow': _L3_xcond_in['sa_ow'], 'L3_xcond_sa_ob': _L3_xcond_in['sa_ob'], 'L3_xcond_ca_qw': _L3_xcond_in['ca_qw'], 'L3_xcond_ca_qb': _L3_xcond_in['ca_qb'], 'L3_xcond_ca_kw': _L3_xcond_in['ca_kw'], 'L3_xcond_ca_kb': _L3_xcond_in['ca_kb'], 'L3_xcond_ca_vw': _L3_xcond_in['ca_vw'], 'L3_xcond_ca_vb': _L3_xcond_in['ca_vb'], 'L3_xcond_ca_ow': _L3_xcond_in['ca_ow'], 'L3_xcond_ca_ob': _L3_xcond_in['ca_ob'], 'L3_xcond_ffn_w1': _L3_xcond_in['ffn_w1'], 'L3_xcond_ffn_b1': _L3_xcond_in['ffn_b1'], 'L3_xcond_ffn_w2': _L3_xcond_in['ffn_w2'], 'L3_xcond_ffn_b2': _L3_xcond_in['ffn_b2']}

def reference(x, cond_1024, ctx_1024, L0_xcond_ln_gamma, L0_xcond_ln_beta, L0_xcond_Wq, L0_xcond_Wk, L0_xcond_Wv, L0_xcond_router_W, L0_xcond_router_b, L0_xcond_e_w1, L0_xcond_e_b1, L0_xcond_e_w2, L0_xcond_e_b2, L0_xcond_gate_w1, L0_xcond_gate_b1, L0_xcond_gate_w2, L0_xcond_gate_b2, L0_xcond_out_w, L0_xcond_out_b, L1_xcond_W_mod, L1_xcond_b_mod, L1_xcond_W_qkv, L1_xcond_b_qkv, L1_xcond_W_proj, L1_xcond_b_proj, L1_xcond_W_qc, L1_xcond_b_qc, L1_xcond_W_kvc, L1_xcond_b_kvc, L1_xcond_W_cproj, L1_xcond_b_cproj, L1_xcond_W_mlp1, L1_xcond_b_mlp1, L1_xcond_W_mlp2, L1_xcond_b_mlp2, L2_xcond_adaln_w, L2_xcond_adaln_b, L2_xcond_qkv_w, L2_xcond_qkv_b, L2_xcond_sa_proj_w, L2_xcond_sa_proj_b, L2_xcond_q_w, L2_xcond_q_b, L2_xcond_kv_w, L2_xcond_kv_b, L2_xcond_ca_proj_w, L2_xcond_ca_proj_b, L2_xcond_fc1_w, L2_xcond_fc1_b, L2_xcond_fc2_w, L2_xcond_fc2_b, L3_xcond_ln1_g, L3_xcond_ln1_b, L3_xcond_aff1_w, L3_xcond_aff1_b, L3_xcond_ln2_g, L3_xcond_ln2_b, L3_xcond_aff2_w, L3_xcond_aff2_b, L3_xcond_sa_qw, L3_xcond_sa_qb, L3_xcond_sa_kw, L3_xcond_sa_kb, L3_xcond_sa_vw, L3_xcond_sa_vb, L3_xcond_sa_ow, L3_xcond_sa_ob, L3_xcond_ca_qw, L3_xcond_ca_qb, L3_xcond_ca_kw, L3_xcond_ca_kb, L3_xcond_ca_vw, L3_xcond_ca_vb, L3_xcond_ca_ow, L3_xcond_ca_ob, L3_xcond_ffn_w1, L3_xcond_ffn_b1, L3_xcond_ffn_w2, L3_xcond_ffn_b2):
    import jax
    import jax.numpy as jnp

    def _L0_xcond_ref(mix_hidden_states, global_anchor, prototype_bank, ln_gamma, ln_beta, Wq, Wk, Wv, router_W, router_b, e_w1, e_b1, e_w2, e_b2, gate_w1, gate_b1, gate_w2, gate_b2, out_w, out_b):
        import jax, jax.numpy as jnp
        import numpy as np
        H = 256
        RH = 2 * H
        E = 3
        B, T, P = (8, 512, 64)
        LN_EPS = 1e-05

        def _layer_norm(x, gamma, beta):
            mu = jnp.mean(x, axis=-1, keepdims=True)
            var = jnp.mean(jnp.square(x - mu), axis=-1, keepdims=True)
            return (x - mu) * jax.lax.rsqrt(var + LN_EPS) * gamma + beta
        x = mix_hidden_states
        nx = _layer_norm(x, ln_gamma, ln_beta)
        q = nx @ Wq
        k = prototype_bank @ Wk
        v = prototype_bank @ Wv
        scores = jnp.einsum('bth,bph->btp', q, k) * H ** (-0.5)
        weights = jax.nn.softmax(scores, axis=-1)
        evidence = jnp.einsum('btp,bph->bth', weights, v)
        anchor = jnp.broadcast_to(global_anchor[:, None, :], nx.shape)
        combined = jnp.concatenate([nx, evidence, anchor], axis=-1)
        router_logits = combined @ router_W + router_b
        router_probs = jax.nn.softmax(router_logits, axis=-1)
        h = jax.nn.silu(jnp.einsum('btc,ecr->bter', combined, e_w1) + e_b1)
        expert_out = jnp.einsum('bter,erh->bteh', h, e_w2) + e_b2
        routed = jnp.sum(expert_out * router_probs[..., None], axis=-2)
        g = jax.nn.sigmoid(jax.nn.silu(combined @ gate_w1 + gate_b1) @ gate_w2 + gate_b2)
        refined_delta = g * (routed @ out_w + out_b)
        return x + refined_delta

    def _L1_xcond_ref(x, c, context, W_mod, b_mod, W_qkv, b_qkv, W_proj, b_proj, W_qc, b_qc, W_kvc, b_kvc, W_cproj, b_cproj, W_mlp1, b_mlp1, W_mlp2, b_mlp2):
        import jax, jax.numpy as jnp
        import numpy as np
        LN_EPS = 1e-06

        def _ln(x):
            mu = jnp.mean(x, axis=-1, keepdims=True)
            var = jnp.var(x, axis=-1, keepdims=True)
            return (x - mu) * jax.lax.rsqrt(var + LN_EPS)
        B, N, H = x.shape
        NH = 16
        hd = H // NH
        scale = hd ** (-0.5)
        c_proj = jax.nn.silu(c) @ W_mod + b_mod
        shift_a, scale_a, gate_a, shift_m, scale_m, gate_m = jnp.split(c_proj, 6, axis=-1)

        def modulate(t, shift, sc):
            return t * (1 + sc[:, None]) + shift[:, None]
        x_norm = modulate(_ln(x), shift_a, scale_a)
        qkv = x_norm @ W_qkv + b_qkv
        q, k, v = jnp.split(qkv, 3, axis=-1)
        q = q.reshape(B, N, NH, hd).transpose(0, 2, 1, 3)
        k = k.reshape(B, N, NH, hd).transpose(0, 2, 1, 3)
        v = v.reshape(B, N, NH, hd).transpose(0, 2, 1, 3)
        attn_w = jax.nn.softmax(jnp.einsum('bhqd,bhkd->bhqk', q, k) * scale, axis=-1)
        attn_out = jnp.einsum('bhqk,bhkd->bhqd', attn_w, v)
        attn_out = attn_out.transpose(0, 2, 1, 3).reshape(B, N, H)
        attn_out = attn_out @ W_proj + b_proj
        x = x + gate_a[:, None] * attn_out
        S = context.shape[1]
        q_c = _ln(x) @ W_qc + b_qc
        kv_c = _ln(context) @ W_kvc + b_kvc
        k_c, v_c = jnp.split(kv_c, 2, axis=-1)
        q_c = q_c.reshape(B, N, NH, hd).transpose(0, 2, 1, 3)
        k_c = k_c.reshape(B, S, NH, hd).transpose(0, 2, 1, 3)
        v_c = v_c.reshape(B, S, NH, hd).transpose(0, 2, 1, 3)
        c_attn_w = jax.nn.softmax(jnp.einsum('bhqd,bhsd->bhqs', q_c, k_c) * scale, axis=-1)
        c_attn_out = jnp.einsum('bhqs,bhsd->bhqd', c_attn_w, v_c)
        c_attn_out = c_attn_out.transpose(0, 2, 1, 3).reshape(B, N, H)
        c_attn_out = c_attn_out @ W_cproj + b_cproj
        x = x + c_attn_out
        x_norm2 = modulate(_ln(x), shift_m, scale_m)
        h = jax.nn.gelu(x_norm2 @ W_mlp1 + b_mlp1)
        h = h @ W_mlp2 + b_mlp2
        x = x + gate_m[:, None] * h
        return x

    def _L2_xcond_ref(x, t_emb, context, adaln_w, adaln_b, qkv_w, qkv_b, sa_proj_w, sa_proj_b, q_w, q_b, kv_w, kv_b, ca_proj_w, ca_proj_b, fc1_w, fc1_b, fc2_w, fc2_b):
        import jax, jax.numpy as jnp
        import numpy as np
        D = 256
        H = 16
        HD = D // H
        MLP = 4 * D
        EPS = 1e-06
        SCALE = HD ** (-0.5)

        def _p(key, shape, s=0.02):
            return jax.random.normal(key, shape, dtype=jnp.float32) * s

        def _ln(x):
            mu = jnp.mean(x, axis=-1, keepdims=True)
            var = jnp.var(x, axis=-1, keepdims=True)
            return (x - mu) * jax.lax.rsqrt(var + EPS)

        def _heads(t):
            B, L, _ = t.shape
            return t.reshape(B, L, H, HD).transpose(0, 2, 1, 3)

        def _attend(q, k, v):
            attn = jnp.einsum('bhnd,bhsd->bhns', q, k) * SCALE
            attn = jax.nn.softmax(attn, axis=-1)
            o = jnp.einsum('bhns,bhsd->bhnd', attn, v)
            B, _, N, _ = q.shape
            return o.transpose(0, 2, 1, 3).reshape(B, N, D)
        B, N, _ = x.shape
        S = context.shape[1]
        mod = jax.nn.silu(t_emb) @ adaln_w + adaln_b
        sh_sa, sc_sa, g_sa, sh_ff, sc_ff, g_ff = jnp.split(mod[:, None, :], 6, axis=-1)
        xm = _ln(x) * (1.0 + sc_sa) + sh_sa
        qkv = (xm @ qkv_w + qkv_b).reshape(B, N, 3, H, HD)
        q = qkv[:, :, 0].transpose(0, 2, 1, 3)
        k = qkv[:, :, 1].transpose(0, 2, 1, 3)
        v = qkv[:, :, 2].transpose(0, 2, 1, 3)
        x_sa = _attend(q, k, v) @ sa_proj_w + sa_proj_b
        x = x + g_sa * x_sa
        xn = _ln(x)
        q = _heads(xn @ q_w + q_b)
        kv = (context @ kv_w + kv_b).reshape(B, S, 2, H, HD)
        k = kv[:, :, 0].transpose(0, 2, 1, 3)
        v = kv[:, :, 1].transpose(0, 2, 1, 3)
        x_ca = _attend(q, k, v) @ ca_proj_w + ca_proj_b
        x = x + x_ca
        xm = _ln(x) * (1.0 + sc_ff) + sh_ff
        h = jax.nn.gelu(xm @ fc1_w + fc1_b, approximate=True)
        x_ff = h @ fc2_w + fc2_b
        x = x + g_ff * x_ff
        return x

    def _L3_xcond_ref(x, u, t_emb, ln1_g, ln1_b, aff1_w, aff1_b, ln2_g, ln2_b, aff2_w, aff2_b, sa_qw, sa_qb, sa_kw, sa_kb, sa_vw, sa_vb, sa_ow, sa_ob, ca_qw, ca_qb, ca_kw, ca_kb, ca_vw, ca_vb, ca_ow, ca_ob, ffn_w1, ffn_b1, ffn_w2, ffn_b2):
        import jax, jax.numpy as jnp
        import numpy as np
        D = 256
        H = 16
        DH = D // H
        DFF = 1024
        B = 2
        L = 512
        EPS = 1e-05

        def layer_norm(x, g, b):
            mu = jnp.mean(x, axis=-1, keepdims=True)
            var = jnp.mean(jnp.square(x - mu), axis=-1, keepdims=True)
            return (x - mu) * jax.lax.rsqrt(var + EPS) * g + b

        def ada_ln(x, t_emb, ln_g, ln_b, aff_w, aff_b):
            normed = layer_norm(x, ln_g, ln_b)
            affine = t_emb @ aff_w + aff_b
            gamma, beta = jnp.split(affine, 2, axis=-1)
            return gamma[:, None, :] * normed + beta[:, None, :]

        def mha(q_in, k_in, v_in, qw, qb, kw, kb, vw, vb, ow, ob):
            Bq, Lq, _ = q_in.shape
            Lk = k_in.shape[1]
            Q = (q_in @ qw + qb).reshape(Bq, Lq, H, DH)
            K = (k_in @ kw + kb).reshape(Bq, Lk, H, DH)
            V = (v_in @ vw + vb).reshape(Bq, Lk, H, DH)
            scores = jnp.einsum('bqhd,bkhd->bhqk', Q, K) / np.sqrt(DH).astype(np.float32)
            attn = jax.nn.softmax(scores, axis=-1)
            out = jnp.einsum('bhqk,bkhd->bqhd', attn, V).reshape(Bq, Lq, D)
            return out @ ow + ob
        xn = ada_ln(x, t_emb, ln1_g, ln1_b, aff1_w, aff1_b)
        x = x + mha(xn, xn, xn, sa_qw, sa_qb, sa_kw, sa_kb, sa_vw, sa_vb, sa_ow, sa_ob)
        x = x + mha(x, u, u, ca_qw, ca_qb, ca_kw, ca_kb, ca_vw, ca_vb, ca_ow, ca_ob)
        xn = ada_ln(x, t_emb, ln2_g, ln2_b, aff2_w, aff2_b)
        h = jax.nn.gelu(xn @ ffn_w1 + ffn_b1, approximate=False)
        x = x + (h @ ffn_w2 + ffn_b2)
        return x
    x = _L0_xcond_ref(x, cond_1024, ctx_1024, L0_xcond_ln_gamma, L0_xcond_ln_beta, L0_xcond_Wq, L0_xcond_Wk, L0_xcond_Wv, L0_xcond_router_W, L0_xcond_router_b, L0_xcond_e_w1, L0_xcond_e_b1, L0_xcond_e_w2, L0_xcond_e_b2, L0_xcond_gate_w1, L0_xcond_gate_b1, L0_xcond_gate_w2, L0_xcond_gate_b2, L0_xcond_out_w, L0_xcond_out_b)
    x = _L1_xcond_ref(x, cond_1024, ctx_1024, L1_xcond_W_mod, L1_xcond_b_mod, L1_xcond_W_qkv, L1_xcond_b_qkv, L1_xcond_W_proj, L1_xcond_b_proj, L1_xcond_W_qc, L1_xcond_b_qc, L1_xcond_W_kvc, L1_xcond_b_kvc, L1_xcond_W_cproj, L1_xcond_b_cproj, L1_xcond_W_mlp1, L1_xcond_b_mlp1, L1_xcond_W_mlp2, L1_xcond_b_mlp2)
    x = _L2_xcond_ref(x, cond_1024, ctx_1024, L2_xcond_adaln_w, L2_xcond_adaln_b, L2_xcond_qkv_w, L2_xcond_qkv_b, L2_xcond_sa_proj_w, L2_xcond_sa_proj_b, L2_xcond_q_w, L2_xcond_q_b, L2_xcond_kv_w, L2_xcond_kv_b, L2_xcond_ca_proj_w, L2_xcond_ca_proj_b, L2_xcond_fc1_w, L2_xcond_fc1_b, L2_xcond_fc2_w, L2_xcond_fc2_b)
    x = _L3_xcond_ref(x, ctx_1024, cond_1024, L3_xcond_ln1_g, L3_xcond_ln1_b, L3_xcond_aff1_w, L3_xcond_aff1_b, L3_xcond_ln2_g, L3_xcond_ln2_b, L3_xcond_aff2_w, L3_xcond_aff2_b, L3_xcond_sa_qw, L3_xcond_sa_qb, L3_xcond_sa_kw, L3_xcond_sa_kb, L3_xcond_sa_vw, L3_xcond_sa_vb, L3_xcond_sa_ow, L3_xcond_sa_ob, L3_xcond_ca_qw, L3_xcond_ca_qb, L3_xcond_ca_kw, L3_xcond_ca_kb, L3_xcond_ca_vw, L3_xcond_ca_vb, L3_xcond_ca_ow, L3_xcond_ca_ob, L3_xcond_ffn_w1, L3_xcond_ffn_b1, L3_xcond_ffn_w2, L3_xcond_ffn_b2)
    return x

_drawn_inputs = setup_inputs


def setup_inputs(seed=0):
    import zlib

    import numpy as np

    out = dict(_drawn_inputs(seed))
    spreads = {'L0_xcond_ln_gamma': (1.0, 0.6),
     'L0_xcond_ln_beta': (0.0, 0.635),
     'L0_xcond_router_b': (0.0, 0.8),
     'L0_xcond_e_b1': (0.0, 0.41),
     'L0_xcond_e_b2': (0.0, 0.1),
     'L0_xcond_gate_b1': (0.0, 0.8),
     'L0_xcond_gate_b2': (0.0, 0.8),
     'L0_xcond_out_b': (0.0, 0.1),
     'L1_xcond_b_mod': (0.0, 0.1),
     'L1_xcond_b_qkv': (0.0, 0.1),
     'L1_xcond_b_proj': (0.0, 0.1),
     'L1_xcond_b_qc': (0.0, 0.47),
     'L1_xcond_b_kvc': (0.0, 0.1),
     'L1_xcond_b_cproj': (0.0, 0.1),
     'L1_xcond_b_mlp1': (0.0, 0.1),
     'L1_xcond_b_mlp2': (0.0, 0.1),
     'L3_xcond_ln1_g': (1.0, 0.6),
     'L3_xcond_ln1_b': (0.0, 2.0),
     'L3_xcond_aff1_b': (0.0, 0.8),
     'L3_xcond_ln2_g': (1.0, 0.6),
     'L3_xcond_ln2_b': (0.0, 2.0),
     'L3_xcond_aff2_b': (0.0, 0.745),
     'L3_xcond_sa_qb': (0.0, 2.0),
     'L3_xcond_sa_kb': (0.0, 2.0),
     'L3_xcond_sa_vb': (0.0, 0.332),
     'L3_xcond_sa_ob': (0.0, 0.269),
     'L3_xcond_ca_qb': (0.0, 2.0),
     'L3_xcond_ca_kb': (0.0, 2.0),
     'L3_xcond_ca_vb': (0.0, 0.358),
     'L3_xcond_ca_ob': (0.0, 0.268),
     'L3_xcond_ffn_b1': (0.0, 0.324),
     'L3_xcond_ffn_b2': (0.0, 0.275)}
    factors = {'L2_xcond_adaln_w': 3.051,
     'L2_xcond_adaln_b': 8.0,
     'L2_xcond_qkv_w': 6.216,
     'L2_xcond_qkv_b': 8.0,
     'L2_xcond_sa_proj_w': 6.159,
     'L2_xcond_sa_proj_b': 8.0,
     'L2_xcond_q_w': 64.0,
     'L2_xcond_q_b': 64.0,
     'L2_xcond_kv_b': 28.029,
     'L2_xcond_ca_proj_b': 3.992,
     'L2_xcond_fc1_w': 3.68,
     'L2_xcond_fc1_b': 8.0,
     'L2_xcond_fc2_w': 3.576,
     'L2_xcond_fc2_b': 8.0,
     'L3_xcond_sa_qw': 8.0,
     'L3_xcond_sa_kw': 8.0,
     'L3_xcond_ca_qw': 8.0,
     'L3_xcond_ca_kw': 8.0,
     'L2_xcond_kv_w': 3.247}
    for name, (base, spread) in spreads.items():
        noise = np.random.default_rng([zlib.crc32(name.encode()), seed]).standard_normal(out[name].shape)
        drawn = base * np.exp(spread * noise) if base else spread * noise
        out[name] = jnp.asarray(drawn.astype(out[name].dtype))
    for name, factor in factors.items():
        out[name] = (out[name] * factor).astype(out[name].dtype)
    return out
```

```python
import numpy as np

NB, NT, D, NC_TOK = 16, 256, 256, 77
NH, HD = 16, 16
P = 128
TT, CC = NT // P, D // P
MLP = 1024
MC = MLP // P
NE, RH = 3, 512
EC = NE * RH // P
VP, VW = 3, HD + 1
VC = VP * VW
NPAIR = NH // 2
QROWS = 3 * HD
CPAD = NC_TOK + 1
PSCALE = 2.0 ** 15


class Mark:

    def __init__(self, group, place, count, dma):
        self.group, self.place, self.count, self.dma = group, place, count, dma


class Op:
    def __init__(self, engine, phase, emit, after, mark, alone):
        self.engine, self.phase, self.emit, self.after = engine, phase, emit, after
        self.mark, self.alone = mark, alone


class Bank:

    def __init__(self, ap):
        self.ap, self.emptied, self.when = ap, None, 0


class Pipeline:

    def __init__(self, nc, name, lags, n_seq, stack):
        self.nc, self.name, self.lags, self.n_seq, self.stack = nc, name, lags, n_seq, stack
        self.marks, self.per_seq, self.sems = {}, {}, {}
        self.segments, self.shared = [], []

    def begin(self, active):
        self.active, self.ops, self.seen, self.counts = active, [], set(), {}
        self.group_of = {}

    def op(self, engine, phase, emit, after=(), mark=None, dma=0, group=None, alone=False):
        if phase not in self.active:
            return
        if mark:
            name = f"{phase}.{mark}"
            if name not in self.seen:
                self.seen.add(name)
                g = f"{name}" if dma else f"{engine}_{group or phase}"
                place = self.counts.get(g, 0)
                self.counts[g] = place + 1
                m = Mark(g, place, dma or 1, bool(dma))
                old = self.marks.setdefault(name, m)
                assert (old.group, old.place, old.count) == (m.group, m.place, m.count), name
            mark = name
        self.ops.append(Op(engine, phase, emit, list(after), mark, alone))

    def take(self, bank, phase):
        if phase not in self.active or bank.emptied is None:
            return []
        other = bank.emptied.split(".")[0]
        off = bank.when - self.iteration + self.lags[other] * -1 + self.lags[phase]
        return [f"{bank.emptied}@{off}"] if off else [bank.emptied]

    def empties(self, bank, phase, mark):
        if phase in self.active:
            bank.emptied, bank.when = f"{phase}.{mark}", self.iteration

    def end(self, lo, hi):
        for g, n in self.counts.items():
            assert self.per_seq.setdefault(g, n) == n, g
        for b in self.shared:
            if b.when == lo:
                b.when = hi - 1
        self.segments.append((lo, hi, self.ops))

    def sem(self, group):
        if group not in self.sems:
            name = f"{self.name}_{group}".replace(".", "_")
            self.sems[group] = self.stack.enter_context(self.nc.semaphore(name))
        return self.sems[group]

    def value(self, mark, seq):
        m = self.marks[mark]
        if m.dma:
            return seq * (16 * m.count) + 16 * m.count
        return seq * self.per_seq[m.group] + (m.place + 1)

    def emit(self, engine, eng):
        for lo, hi, ops in self.segments:
            mine = [o for o in ops if o.engine == engine]
            if not mine:
                continue
            if hi == lo + 1:
                self._body(eng, mine, lo, False)
            else:
                with eng.Fori(lo, hi) as n:
                    self._body(eng, mine, n, True)

    def _body(self, eng, ops, n, loop):
        waited = {}
        for o in ops:
            seq = n - self.lags[o.phase]
            waits = []
            for w in o.after:
                name, _, off = w.partition("@")
                off = int(off or 0)
                m = self.marks[name]
                lag = self.lags[o.phase]
                reach = (off - lag, m.place)
                if waited.get(m.group, (-99, 0)) >= reach:
                    continue
                waited[m.group] = reach
                if loop:
                    val = self.value(name, seq + off)
                else:
                    at = min(seq + off, self.n_seq - 1)
                    if at < 0:
                        continue
                    val = self.value(name, at)
                waits.append((self.sem(m.group), val))
            for s, v in waits:
                eng.wait_ge(s, v)
                if loop and (o.alone or o.engine == "sp"):
                    eng.sem_inc(self.sem("holder"), 1)
            ins = o.emit(eng, seq)
            if o.mark:
                m = self.marks[o.mark]
                ins.then_inc(self.sem(m.group), 16 if m.dma else 1)


def build(nc, t):
    import concourse.bass as bass
    from concourse import mybir
    from contextlib import ExitStack

    F32, F32R = mybir.dt.float32, mybir.dt.float32r
    BF16, F16 = mybir.dt.bfloat16, mybir.dt.float16
    ALU, ACT, AX = mybir.AluOpType, mybir.ActivationFunctionType, mybir.AxisListType

    root = ExitStack()

    def buffers(stack):
        def sb(name, shape, dt=F32):
            return stack.enter_context(nc.sbuf_tensor(name, shape, dt))
        return sb

    def scratch(name, shape):
        return nc.dram_tensor(name, shape, F32, kind="Internal").ap()

    xs = [scratch(f"x_after_L{i}", (NB, NT, D)) for i in range(3)] + [t["out"]]
    cols = [scratch("cols_L0", (P, NB * 14))] + [scratch(f"cols_L{i}", (P, NB * 8)) for i in (1, 2, 3)]
    rows = [scratch("rows_L0", (NB, NE))] + [scratch(f"rows_L{i}", (NB, 4 * D)) for i in (1, 2, 3)]

    def chunks(w):
        return w.rearrange("(k p) n -> p k n", p=P)

    def column(v):
        return v.rearrange("(k p) -> p k", p=P)

    def spread(v, n=P):
        return v.unsqueeze(0).to_broadcast([n, v.shape[0]])

    def by_tile(x):
        return x.rearrange("(t p) f -> p t f", p=P)

    with root, nc.allow_non_contiguous_dma(reason="bias vectors as columns, a few KB"):
        sbr = buffers(root)
        ident = sbr("ident", [P, P])
        half = sbr("minus_half", [P, 2])
        eps5 = sbr("eps5", [P, 2])
        eps6 = sbr("eps6", [P, 2])
        WT = []
        for s in range(2):
            WT.append(dict(
                qkv=sbr(f"w_qkv{s}", [P, CC, 3 * D]), o=sbr(f"w_o{s}", [P, CC, D]),
                qc=sbr(f"w_qc{s}", [P, CC, D]), kvc=sbr(f"w_kvc{s}", [P, CC, 2 * D]),
                oc=sbr(f"w_oc{s}", [P, CC, D]), w1=sbr(f"w_1{s}", [P, CC, MLP]),
                w2=sbr(f"w_2{s}", [P, MC, D]),
                bcol=sbr(f"b_col{s}", [P, 16]),
                bv=sbr(f"b_v{s}", [P, D]), bvc=sbr(f"b_vc{s}", [P, D]), boc=sbr(f"b_oc{s}", [P, D])))
        s_w = [root.enter_context(nc.semaphore(f"weights_L{L}")) for L in range(4)]
        n_w = [0] * 4

        def layer_parts(L):
            if L == 1:
                g = lambda k: t["L1_xcond_" + k]
                return dict(qkv=[g("W_qkv")], o=g("W_proj"), qc=g("W_qc"), kvc=[g("W_kvc")], oc=g("W_cproj"),
                            w1=g("W_mlp1"), w2=g("W_mlp2"), bqkv=g("b_qkv"), bqc=g("b_qc"), bkvc=g("b_kvc"),
                            boc=g("b_cproj"), b1=g("b_mlp1"))
            if L == 2:
                g = lambda k: t["L2_xcond_" + k]
                return dict(qkv=[g("qkv_w")], o=g("sa_proj_w"), qc=g("q_w"), kvc=[g("kv_w")], oc=g("ca_proj_w"),
                            w1=g("fc1_w"), w2=g("fc2_w"), bqkv=g("qkv_b"), bqc=g("q_b"), bkvc=g("kv_b"),
                            boc=g("ca_proj_b"), b1=g("fc1_b"))
            g = lambda k: t["L3_xcond_" + k]
            return dict(qkv=[g("sa_qw"), g("sa_kw"), g("sa_vw")], o=g("sa_ow"), qc=g("ca_qw"),
                        kvc=[g("ca_kw"), g("ca_vw")], oc=g("ca_ow"), w1=g("ffn_w1"), w2=g("ffn_w2"),
                        bq=g("sa_qb"), bk=g("sa_kb"), bv=g("sa_vb"), bqc=g("ca_qb"), bkc=g("ca_kb"),
                        bvc=g("ca_vb"), boc=g("ca_ob"), b1=g("ffn_b1"))

        def load_layer(eng, L):
            w, p = WT[L % 2], layer_parts(L)

            def go(dst, src):
                eng.dma_start(dst, src).then_inc(s_w[L], 16)
                n_w[L] += 16

            def side_by_side(dst, parts):
                at = 0
                for x in parts:
                    go(dst[:, :, at:at + x.shape[1]], chunks(x))
                    at += x.shape[1]

            side_by_side(w["qkv"], p["qkv"])
            if L < 3:
                bq, bk, bv = (p["bqkv"][i * D:(i + 1) * D] for i in range(3))
                bkc, bvc = (p["bkvc"][i * D:(i + 1) * D] for i in range(2))
            else:
                bq, bk, bv, bkc, bvc = p["bq"], p["bk"], p["bv"], p["bkc"], p["bvc"]
            for i, b in enumerate((bq, bk, p["bqc"], bkc)):
                go(w["bcol"][:, 2 * i:2 * i + 2], column(b))
            go(w["bcol"][:, 8:16], column(p["b1"]))
            go(w["bv"][:, :], spread(bv))
            go(w["bvc"][:, :], spread(bvc))
            go(w["boc"][:, :], spread(p["boc"]))
            side_by_side(w["kvc"], p["kvc"])
            for k in ("o", "qc", "oc", "w1", "w2"):
                go(w[k][:, :, :], chunks(p[k]))

        tables(nc, t, cols, rows, ident, half, eps5, eps6, chunks, column, spread, buffers)
        mixture(nc, t, xs[0], cols[0], rows[0], ident, half, eps5, chunks, column, spread, by_tile, buffers,
                lambda eng: (load_layer(eng, 1), load_layer(eng, 2)))
        blocks(nc, t, xs, cols, rows, ident, half, eps5, eps6, WT, s_w, n_w, load_layer, by_tile, buffers)


def tables(nc, t, cols, rows, ident, half, eps5, eps6, chunks, column, spread, buffers):
    from concourse import mybir
    from contextlib import ExitStack
    F32 = mybir.dt.float32
    ALU, ACT = mybir.AluOpType, mybir.ActivationFunctionType

    with ExitStack() as stack:
        sb = buffers(stack)
        cond = sb("cond", [NB, D])
        cond_silu = sb("cond_silu", [NB, D])
        condT = sb("condT", [P, CC, NB])
        cond_siluT = sb("cond_siluT", [P, CC, NB])
        w_mod = [sb("w_mod1", [P, CC, 6 * D]), sb("w_mod2", [P, CC, 6 * D])]
        w_aff = [sb("w_aff1", [P, CC, 2 * D]), sb("w_aff2", [P, CC, 2 * D])]
        w_anchor = sb("w_anchor", [P, CC, EC + 2, P])
        w_router = sb("w_router", [P, CC, NE])
        b_mod = sb("b_mod", [P, 2, 12])
        b_aff = sb("b_aff", [P, 2, 4])
        ln_gb = sb("ln_gb", [P, 2, 4])
        b_anchor = sb("b_anchor", [P, EC + 2])
        b_router = sb("b_router", [NB, NE])
        g_row = sb("g_row", [NB, 2, 2, D])
        o_row = sb("o_row", [NB, 3, 2, D])
        tab0 = sb("tab0", [P, NB, EC + 2])
        tab = [sb(f"tab{i}", [P, NB, 8]) for i in (1, 2, 3)]
        tr0 = sb("tr0", [NB, NE])
        tr = [sb(f"tr{i}", [NB, 4, D]) for i in (1, 2, 3)]
        ps = [stack.enter_context(nc.psum_tensor(f"t_ps{i}", [P, 512], F32)) for i in range(8)]
        sem = lambda n: stack.enter_context(nc.semaphore(n))
        s_cond, s_in, s_idm, s_id = sem("t_cond"), sem("t_in"), sem("t_idm"), sem("t_id")
        s_silu, s_T, s_cT, s_mm = sem("t_silu"), sem("t_T"), sem("t_cT"), sem("t_mm")
        s_dve, s_out = sem("t_dve"), sem("t_out")
        loads = []

        def load(dst, src):
            loads.append((dst, src))

        W1, W2, G0 = t["L1_xcond_W_mod"], t["L2_xcond_adaln_w"], t["L0_xcond_gate_w1"]
        load(w_mod[0][:, :, :], chunks(W1))
        load(w_mod[1][:, :, :], chunks(W2))
        load(w_aff[0][:, :, :], chunks(t["L3_xcond_aff1_w"]))
        load(w_aff[1][:, :, :], chunks(t["L3_xcond_aff2_w"]))
        for e in range(NE):
            for k in range(CC):
                load(w_anchor[:, k, 4 * e:4 * e + 4, :].rearrange("p m n -> p (m n)"),
                     t["L0_xcond_e_w1"][e, 2 * D + k * P:2 * D + (k + 1) * P, :])
        for k in range(CC):
            load(w_anchor[:, k, EC:EC + 2, :].rearrange("p m n -> p (m n)"), G0[2 * D + k * P:2 * D + (k + 1) * P, :])
        load(w_router[:, :, :], chunks(t["L0_xcond_router_W"][2 * D:3 * D, :]))
        for i, b in enumerate((t["L1_xcond_b_mod"], t["L2_xcond_adaln_b"])):
            load(b_mod[:, i, :], column(b))
            for j, at in enumerate((2 * D, 5 * D)):
                load(g_row[:, i, j, :], spread(b[at:at + D], NB))
        for i in range(2):
            load(b_aff[:, i, :], column(t[f"L3_xcond_aff{i + 1}_b"]))
            load(ln_gb[:, i, 0:2], column(t[f"L3_xcond_ln{i + 1}_g"]))
            load(ln_gb[:, i, 2:4], column(t[f"L3_xcond_ln{i + 1}_b"]))
        load(b_anchor[:, 0:EC], t["L0_xcond_e_b1"].rearrange("e (k p) -> p (e k)", p=P))
        load(b_anchor[:, EC:EC + 2], column(t["L0_xcond_gate_b1"]))
        load(b_router[:, :], spread(t["L0_xcond_router_b"], NB))
        for i, (a, m) in enumerate((("L1_xcond_b_proj", "L1_xcond_b_mlp2"), ("L2_xcond_sa_proj_b", "L2_xcond_fc2_b"),
                                    ("L3_xcond_sa_ob", "L3_xcond_ffn_b2"))):
            load(o_row[:, i, 0, :], spread(t[a], NB))
            load(o_row[:, i, 1, :], spread(t[m], NB))
        ALL = 16 * len(loads)

        block = stack.enter_context(nc.Block())

        @block.sync
        def _(eng):
            eng.dma_start(cond[:, :], t["cond_1024"]).then_inc(s_cond, 16)
            for dst, src in loads:
                eng.dma_start(dst, src).then_inc(s_in, 16)
            eng.wait_ge(s_dve, DVE_DONE)
            outs = [(cols[0], tab0[:, :, :].rearrange("p b m -> p (b m)")), (rows[0], tr0[:, :])]
            for i in range(3):
                outs.append((cols[i + 1], tab[i][:, :, :].rearrange("p b m -> p (b m)")))
                outs.append((rows[i + 1], tr[i][:, :, :].rearrange("b g f -> b (g f)")))
            for dst, src in outs:
                eng.dma_start(dst, src).then_inc(s_out, 16)
            eng.wait_ge(s_out, 16 * len(outs))

        @block.gpsimd
        def _(eng):
            eng.memset(half[:, :], -0.5)
            eng.memset(eps5[:, :], 1e-5)
            eng.memset(eps6[:, :], 1e-6)
            eng.memset(ident[:, :], 0.0).then_inc(s_idm, 1)
            eng.wait_ge(s_idm, 1)
            eng.affine_select(out=ident[:, :], in_=ident[:, :], compare_op=ALU.not_equal, fill=1.0,
                              base=0, pattern=[[-1, P]], channel_multiplier=1).then_inc(s_id, 1)

        @block.scalar
        def _(eng):
            eng.wait_ge(s_cond, 16)
            eng.activation(cond_silu[:, :], cond[:, :], ACT.Silu).then_inc(s_silu, 1)

        @block.tensor
        def _(eng):
            eng.wait_ge(s_id, 1)
            eng.wait_ge(s_cond, 16)
            for c in range(CC):
                eng.transpose(ps[0][:, c * NB:(c + 1) * NB], cond[:, c * P:(c + 1) * P], ident[0:NB, 0:NB])
            eng.wait_ge(s_silu, 1)
            for c in range(CC):
                mm = eng.transpose(ps[0][:, (CC + c) * NB:(CC + c + 1) * NB], cond_silu[:, c * P:(c + 1) * P],
                                   ident[0:NB, 0:NB])
            mm.then_inc(s_T, 1)
            eng.wait_ge(s_cT, 1)
            eng.wait_ge(s_in, ALL)

            def columns(out, lhs, m, rhs):
                for k in range(CC):
                    mm = eng.matmul(out, lhs(k, m), rhs[:, k, :], start=(k == 0), stop=(k == CC - 1))
                return mm

            for m in range(EC + 2):
                columns(ps[1][:, m * NB:(m + 1) * NB], lambda k, m: w_anchor[:, k, m, :], m, condT)
            for i in range(2):
                for j, m in enumerate((0, 1, 2, 3, 6, 7, 8, 9)):
                    columns(ps[2][:, (8 * i + j) * NB:(8 * i + j + 1) * NB],
                            lambda k, m: w_mod[i][:, k, m * P:(m + 1) * P], m, cond_siluT)
                for j in range(4):
                    columns(ps[3][:, (4 * i + j) * NB:(4 * i + j + 1) * NB],
                            lambda k, m: w_aff[i][:, k, m * P:(m + 1) * P], j, condT)
                for j, at in enumerate((2 * D, 5 * D)):
                    for k in range(CC):
                        eng.matmul(ps[4 + i][0:NB, j * D:(j + 1) * D], cond_siluT[:, k, :],
                                   w_mod[i][:, k, at:at + D], start=(k == 0), stop=(k == CC - 1))
            for k in range(CC):
                mm = eng.matmul(ps[6][0:NB, 0:NE], condT[:, k, :], w_router[:, k, :],
                                start=(k == 0), stop=(k == CC - 1))
            mm.then_inc(s_mm, 1)

        dve_marks = [0]

        @block.vector
        def _(eng):
            def done(ins, wait=True):
                ins.then_inc(s_dve, 1)
                dve_marks[0] += 1
                if wait:
                    eng.wait_ge(s_dve, dve_marks[0])

            eng.wait_ge(s_T, 1)
            eng.tensor_copy(condT[:, :, :], ps[0][:, 0:CC * NB].rearrange("p (c b) -> p c b", b=NB))
            eng.tensor_copy(cond_siluT[:, :, :],
                            ps[0][:, CC * NB:2 * CC * NB].rearrange("p (c b) -> p c b", b=NB)).then_inc(s_cT, 1)
            eng.wait_ge(s_in, ALL)
            eng.wait_ge(s_mm, 1)

            def flip(tile, a, b):
                return tile[:, :, a:b].rearrange("p b m -> p m b")

            def over_b(cols_):
                return cols_.unsqueeze(2).to_broadcast([P, cols_.shape[1], NB])

            def ps_cols(i, a, b):
                return ps[i][:, a * NB:b * NB].rearrange("p (m b) -> p m b", b=NB)

            done(eng.tensor_tensor(flip(tab0, 0, EC + 2), ps_cols(1, 0, EC + 2), over_b(b_anchor[:, :]), ALU.add))
            done(eng.tensor_tensor(tr0[:, :], ps[6][0:NB, 0:NE], b_router[:, :], ALU.add))
            for i in range(2):
                done(eng.tensor_tensor(flip(tab[i], 0, 4), ps_cols(2, 8 * i, 8 * i + 4),
                                       over_b(b_mod[:, i, 0:4]), ALU.add))
                done(eng.tensor_tensor(flip(tab[i], 4, 8), ps_cols(2, 8 * i + 4, 8 * i + 8),
                                       over_b(b_mod[:, i, 6:10]), ALU.add))
                for a in (2, 6):
                    done(eng.tensor_scalar(tab[i][:, :, a:a + 2], tab[i][:, :, a:a + 2], 1.0, None, ALU.add))
                for j in range(2):
                    done(eng.tensor_tensor(tr[i][:, 2 * j, :], ps[4 + i][0:NB, j * D:(j + 1) * D],
                                           g_row[:, i, j, :], ALU.add))
                    done(eng.tensor_tensor(tr[i][:, 2 * j + 1, :], tr[i][:, 2 * j, :], o_row[:, i, j, :], ALU.mult))
            for j in range(2):
                at = 4 * j
                done(eng.tensor_tensor(flip(tab[2], at + 2, at + 4), ps_cols(3, at, at + 2),
                                       over_b(b_aff[:, j, 0:2]), ALU.add))
                done(eng.tensor_tensor(flip(tab[2], at, at + 2), flip(tab[2], at + 2, at + 4),
                                       over_b(ln_gb[:, j, 2:4]), ALU.mult))
                done(eng.tensor_tensor(flip(tab[2], at, at + 2), flip(tab[2], at, at + 2),
                                       over_b(b_aff[:, j, 2:4]), ALU.add))
                done(eng.tensor_tensor(flip(tab[2], at, at + 2), ps_cols(3, at + 2, at + 4),
                                       flip(tab[2], at, at + 2), ALU.add))
                done(eng.tensor_tensor(flip(tab[2], at + 2, at + 4), flip(tab[2], at + 2, at + 4),
                                       over_b(ln_gb[:, j, 0:2]), ALU.mult))
                done(eng.memset(tr[2][:, 2 * j, :], 1.0))
                done(eng.tensor_copy(tr[2][:, 2 * j + 1, :], o_row[:, 2, j, :]))
            assert dve_marks[0] == DVE_DONE


DVE_DONE = 2 + 2 * (4 + 4) + 2 * 7


def norm_ops(pl, ph, pre, x, st, mv, rstd, eps, half, out, parts, after, wait_out, group=None, first=()):
    from concourse import mybir
    ALU = mybir.AluOpType
    n, tiles = parts
    G = dict(group=group)
    for i in range(tiles):
        pl.op("dve", ph, lambda e, s, i=i: e.bn_stats(st[0:n, i, :], x[0:n, i, :]),
              after=(list(after) + [f"{ph}.{pre}rstd@-1"] * 0 if i == 0 else []), mark=f"{pre}st{i}", **G)
    for i in range(tiles):
        pl.op("dve", ph, lambda e, s, i=i: e.bn_aggr(mv[0:n, i, :], st[0:n, i, :]),
              after=[f"{ph}.{pre}st{i}"] + ([f"{ph}.{pre}ve@-1"] if i == 0 else []),
              mark=f"{pre}mv{i}", alone=True, **G)
    pl.op("pool", ph, lambda e, s: e.tensor_tensor(rstd[0:n, 0:tiles], mv[0:n, 0:tiles, 1], eps[0:n, 0:tiles], ALU.add),
          after=[f"{ph}.{pre}mv{tiles - 1}", f"{ph}.{pre}xn{tiles - 1}@-1"], mark=f"{pre}ve", **G)
    pl.op("pool", ph, lambda e, s: e.tensor_tensor(rstd[0:n, 0:tiles], rstd[0:n, 0:tiles], half[0:n, 0:tiles], ALU.pow),
          after=[f"{ph}.{pre}ve"], mark=f"{pre}rstd", **G)
    for i in range(tiles):
        pl.op("dve", ph, lambda e, s, i=i: e.tensor_scalar(out[0:n, i, :], x[0:n, i, :], mv[0:n, i, 0:1],
                                                          rstd[0:n, i:i + 1], ALU.subtract, ALU.mult),
              after=([f"{ph}.{pre}rstd"] + list(wait_out)) if i == 0 else [], mark=f"{pre}xn{i}", **G)


def mixture(nc, t, x_out, cols0, rows0, ident, half, eps5, chunks, column, spread, by_tile, buffers, prefetch):
    from concourse import mybir
    from contextlib import ExitStack
    F32 = mybir.dt.float32
    ALU, ACT, AX = mybir.AluOpType, mybir.ActivationFunctionType, mybir.AxisListType
    g = lambda k: t["L0_xcond_" + k]

    with ExitStack() as stack:
        sb = buffers(stack)
        wq, wk, wv = (sb(f"m_{k}", [P, CC, D]) for k in ("wq", "wk", "wv"))
        rw = sb("m_rw", [P, 4, NE])
        w1 = sb("m_w1", [P, 4, EC, P])
        w2 = sb("m_w2", [P, EC, D])
        g1 = sb("m_g1", [P, 4, D])
        g2 = sb("m_g2", [P, CC, D])
        wo = sb("m_wo", [P, CC, D])
        lng = sb("m_lng", [P, 4])
        b2 = sb("m_b2", [P, NE, D])
        bg2 = sb("m_bg2", [P, D])
        bo = sb("m_bo", [P, D])
        x, xn, nx = sb("m_x", [P, TT, D]), sb("m_xn", [P, TT, D]), sb("m_nx", [P, CC, NT])
        st, mv, rstd = sb("m_st", [P, TT, 6]), sb("m_mv", [P, TT, 2]), sb("m_rstd", [P, TT])
        ctx, ctxT = sb("m_ctx", [NC_TOK, D]), sb("m_ctxT", [P, CC, NC_TOK])
        qT, kT, v = sb("m_qT", [P, CC, NT]), sb("m_kT", [P, CC, NC_TOK]), sb("m_v", [NC_TOK, D])
        mx, sm, rs = sb("m_mx", [P, TT]), sb("m_sm", [P, TT]), sb("m_rs", [P, TT])
        wgt, wgtT = sb("m_wgt", [P, TT, NC_TOK]), sb("m_wgtT", [NC_TOK, NT])
        ar, lg = sb("m_ar", [P, NE]), sb("m_lg", [P, TT, NE])
        rmx, rsm, rrs = sb("m_rmx", [P, TT]), sb("m_rsm", [P, TT]), sb("m_rrs", [P, TT])
        rex, prob = sb("m_rex", [P, TT, NE]), sb("m_prob", [P, TT, NE])
        evT = sb("m_evT", [P, CC, NT])
        comb = sb("m_comb", [P, 4, NT])
        xg = sb("m_xg", [P, TT, D])
        acol = sb("m_acol", [P, EC + 2])
        h = sb("m_h", [P, EC, NT])
        gT = sb("m_gT", [P, CC, NT])
        gp, th = sb("m_gp", [P, TT, D]), sb("m_th", [P, TT, D])
        r, rT = sb("m_r", [P, TT, D]), sb("m_rT", [P, CC, NT])
        y = sb("m_y", [P, TT, D])
        ps = [stack.enter_context(nc.psum_tensor(f"m_ps{i}", [P, 2, 256], F32)) for i in range(8)]
        banks = [Bank(p) for p in ps]
        fb, hb, eb, gb = banks[0:2], banks[2:5], banks[5:7], banks[7]
        s_w0 = stack.enter_context(nc.semaphore("m_weights"))
        loads = [(wq, g("Wq")), (wk, g("Wk")), (wv, g("Wv"))]
        loads = [(d[:, :, :], chunks(s_)) for d, s_ in loads]
        loads.append((lng[:, 0:2], column(g("ln_gamma"))))
        loads.append((lng[:, 2:4], column(g("ln_beta"))))
        loads.append((rw[:, :, :], chunks(g("router_W")[0:2 * D, :])))
        for e in range(NE):
            for k in range(4):
                loads.append((w1[:, k, 4 * e:4 * e + 4, :].rearrange("p m n -> p (m n)"),
                              g("e_w1")[e, k * P:(k + 1) * P, :]))
        loads.append((g1[:, :, :], chunks(g("gate_w1")[0:2 * D, :])))
        for e in range(NE):
            loads.append((w2[:, 4 * e:4 * e + 4, :], chunks(g("e_w2")[e, :, :])))
            loads.append((b2[:, e, :], spread(g("e_b2")[e, :])))
        loads.append((g2[:, :, :], chunks(g("gate_w2"))))
        loads.append((wo[:, :, :], chunks(g("out_w"))))
        loads.append((bg2[:, :], spread(g("gate_b2"))))
        loads.append((bo[:, :], spread(g("out_b"))))

        pl = Pipeline(nc, "m", dict(F=0, G=1), NB, stack)
        pl.shared = banks
        op, take, empties = pl.op, pl.take, pl.empties

        def f_load():
            op("sp", "F", lambda e, s: e.dma_start(x[:, :, :], by_tile(t["x"][s, :, :])),
               after=["F.xcopy@-1"], mark="x", dma=1)
            op("sp", "F", lambda e, s: e.dma_start(ctx[:, :], t["ctx_1024"][s, :, :]),
               after=["F.ctxt@-1"], mark="ctx", dma=1)
            op("sp", "F", lambda e, s: e.dma_start(ar[:, :], rows0[s, :].unsqueeze(0).to_broadcast([P, NE])),
               after=["F.lg@-1"], mark="ar", dma=1)

        def f_norm():
            norm_ops(pl, "F", "", x, st, mv, rstd, eps5, half, xn, (P, TT), ["F.x"], ["F.xt@-1"])

        def f_transpose():
            b = fb[0]
            for tt in range(TT):
                for c in range(CC):
                    op("pe", "F", lambda e, s, tt=tt, c=c: e.transpose(
                        b.ap[:, c, tt * P:(tt + 1) * P], xn[:, tt, c * P:(c + 1) * P], ident[:, :]),
                       after=(["F.xn1"] + take(b, "F")) if tt + c == 0 else [],
                       mark="xt" if tt + c == 2 else None)
            for c in range(CC):
                op("dve", "F", lambda e, s, c=c: e.tensor_scalar(nx[:, c, :], b.ap[:, c, :], lng[:, c:c + 1],
                                                                lng[:, 2 + c:3 + c], ALU.mult, ALU.add),
                   after=["F.xt", "F.nxcopy@-1", "F.q@-1", "F.lgp@-1"] if c == 0 else [], mark=f"nx{c}")
            empties(b, "F", "nx1")
            b2_ = fb[1]
            for c in range(CC):
                op("pe", "F", lambda e, s, c=c: e.transpose(b2_.ap[:, 0, c * NC_TOK:(c + 1) * NC_TOK],
                                                           ctx[:, c * P:(c + 1) * P], ident[0:NC_TOK, 0:NC_TOK]),
                   after=(["F.ctx"] + take(b2_, "F")) if c == 0 else [], mark="ctxt" if c else None)
            op("act", "F", lambda e, s: e.activation(
                ctxT[:, :, :], b2_.ap[:, 0, 0:CC * NC_TOK].rearrange("p (c k) -> p c k", c=CC), ACT.Copy),
               after=["F.ctxt", "F.v@-1"], mark="ctxT")
            empties(b2_, "F", "ctxT")

        def f_qkv():
            b = fb[0]
            for m in range(CC):
                for k in range(CC):
                    op("pe", "F", lambda e, s, m=m, k=k: e.matmul(b.ap[:, m, :], wq[:, k, m * P:(m + 1) * P],
                                                                 nx[:, k, :], start=(k == 0), stop=(k == CC - 1)),
                       after=(["F.nx1"] + take(b, "F")) if m + k == 0 else [], mark="q" if m + k == 2 else None)
            op("act", "F", lambda e, s: e.activation(qT[:, :, :], b.ap[:, :, :], ACT.Copy),
               after=["F.q", "F.sc@-1"], mark="qT")
            empties(b, "F", "qT")
            b2_ = fb[1]
            first = take(b2_, "F")
            for m in range(CC):
                for k in range(CC):
                    op("pe", "F", lambda e, s, m=m, k=k: e.matmul(
                        b2_.ap[:, 0, m * NC_TOK:(m + 1) * NC_TOK], wk[:, k, m * P:(m + 1) * P], ctxT[:, k, :],
                        start=(k == 0), stop=(k == CC - 1)),
                       after=(["F.ctxT"] + first) if m + k == 0 else [])
            for k in range(CC):
                op("pe", "F", lambda e, s, k=k: e.matmul(b2_.ap[0:NC_TOK, 1, :], ctxT[:, k, :], wv[:, k, :],
                                                        start=(k == 0), stop=(k == CC - 1)),
                   mark="v" if k else None)
            op("act", "F", lambda e, s: e.activation(
                kT[:, :, :], b2_.ap[:, 0, 0:CC * NC_TOK].rearrange("p (c k) -> p c k", c=CC), ACT.Copy),
               after=["F.v", "F.sc@-1"], mark="kT")
            op("act", "F", lambda e, s: e.activation(v[:, :], b2_.ap[0:NC_TOK, 1, :], ACT.Copy),
               after=["F.ev@-1"], mark="vS")
            empties(b2_, "F", "vS")

        def f_scores():
            b = fb[0]
            for tt in range(TT):
                for k in range(CC):
                    op("pe", "F", lambda e, s, tt=tt, k=k: e.matmul(
                        b.ap[:, 0, tt * P:tt * P + NC_TOK], qT[:, k, tt * P:(tt + 1) * P], kT[:, k, :],
                        start=(k == 0), stop=(k == CC - 1)),
                       after=(["F.qT", "F.kT"] + take(b, "F")) if tt + k == 0 else [],
                       mark="sc" if tt + k == 2 else None)
            view = b.ap[:, 0, :].rearrange("p (t k) -> p t k", t=TT)[:, :, 0:NC_TOK]
            op("dve", "F", lambda e, s: e.tensor_reduce(mx[:, :], view, AX.X, ALU.max, negate=True),
               after=["F.sc"] , mark="mx0")
            op("dve", "F", lambda e, s: e.tensor_scalar(mx[:, :], mx[:, :], D ** -0.5, None, ALU.mult),
               after=["F.mx0", "F.exp1@-1"], mark="mx")
            for tt in range(TT):
                op("act", "F", lambda e, s, tt=tt: e.activation(
                    wgt[:, tt, :], b.ap[:, 0, tt * P:tt * P + NC_TOK], ACT.Exp, bias=mx[:, tt:tt + 1],
                    scale=D ** -0.5, accum_out=sm[:, tt:tt + 1]),
                   after=["F.mx", "F.wn1@-1", "F.rs@-1", "F.wt@-1"] if tt == 0 else [], mark=f"exp{tt}")
            empties(b, "F", "exp1")
            op("dve", "F", lambda e, s: e.reciprocal(rs[:, :], sm[:, :]), after=["F.exp1", "F.wn1@-1"], mark="rs")
            for tt in range(TT):
                op("dve", "F", lambda e, s, tt=tt: e.tensor_scalar(wgt[:, tt, :], wgt[:, tt, :], rs[:, tt:tt + 1],
                                                                  None, ALU.mult),
                   after=["F.rs"] if tt == 0 else [], mark=f"wn{tt}")

        def f_evidence():
            b = fb[1]
            for tt in range(TT):
                op("pe", "F", lambda e, s, tt=tt: e.transpose(b.ap[0:NC_TOK, 0, tt * P:(tt + 1) * P], wgt[:, tt, :],
                                                             ident[:, :]),
                   after=(["F.wn1"] + take(b, "F")) if tt == 0 else [], mark="wt" if tt else None)
            op("act", "F", lambda e, s: e.activation(wgtT[:, :], b.ap[0:NC_TOK, 0, :], ACT.Copy),
               after=["F.wt", "F.ev@-1"], mark="wgtT")
            empties(b, "F", "wgtT")
            b2_ = fb[0]
            for m in range(CC):
                op("pe", "F", lambda e, s, m=m: e.matmul(b2_.ap[:, m, :], v[:, m * P:(m + 1) * P], wgtT[:, :],
                                                        start=True, stop=True),
                   after=(["F.wgtT", "F.vS"] + take(b2_, "F")) if m == 0 else [], mark="ev" if m else None)
            op("act", "F", lambda e, s: e.activation(evT[:, :, :], b2_.ap[:, :, :], ACT.Copy),
               after=["F.ev", "F.evcopy@-1", "F.lgp@-1"], mark="evT")
            empties(b2_, "F", "evT")

        def f_router():
            b = fb[1]
            for tt in range(TT):
                for k in range(4):
                    src = (nx, evT)[k // CC]
                    op("pe", "F", lambda e, s, tt=tt, k=k, src=src: e.matmul(
                        b.ap[:, 0, tt * NE:(tt + 1) * NE], src[:, k % CC, tt * P:(tt + 1) * P], rw[:, k, :],
                        start=(k == 0), stop=(k == 3)),
                       after=(["F.evT", "F.nx1"] + take(b, "F")) if tt + k == 0 else [],
                       mark="lgp" if tt + k == 4 else None)
            op("dve", "F", lambda e, s: e.tensor_tensor(
                lg[:, :, :], b.ap[:, 0, 0:TT * NE].rearrange("p (t e) -> p t e", t=TT),
                ar[:, :].unsqueeze(1).to_broadcast([P, TT, NE]), ALU.add),
               after=["F.lgp", "F.ar", "F.rexp1@-1"], mark="lg")
            empties(b, "F", "lg")
            op("dve", "F", lambda e, s: e.tensor_reduce(rmx[:, :], lg[:, :, :], AX.X, ALU.max, negate=True),
               after=["F.lg"], mark="rmx")
            for tt in range(TT):
                op("act", "F", lambda e, s, tt=tt: e.activation(rex[:, tt, :], lg[:, tt, :], ACT.Exp,
                                                               bias=rmx[:, tt:tt + 1],
                                                               accum_out=rsm[:, tt:tt + 1]),
                   after=["F.rmx", "F.prob1@-1"] if tt == 0 else [], mark=f"rexp{tt}")
            op("dve", "F", lambda e, s: e.reciprocal(rrs[:, :], rsm[:, :]), after=["F.rexp1"], mark="rrs")

        def f_hand_over():
            for tt in range(TT):
                op("dve", "F", lambda e, s, tt=tt: e.tensor_scalar(prob[:, tt, :], rex[:, tt, :], rrs[:, tt:tt + 1],
                                                                  None, ALU.mult),
                   after=["F.rrs", "G.r_last@-1"] if tt == 0 else [], mark=f"prob{tt}")
            op("act", "F", lambda e, s: e.activation(comb[:, 0:2, :], nx[:, :, :], ACT.Copy),
               after=["F.nx1", "G.g1p@-1"], mark="nxcopy")
            op("act", "F", lambda e, s: e.activation(comb[:, 2:4, :], evT[:, :, :], ACT.Copy),
               after=["F.evT"], mark="evcopy")
            op("act", "F", lambda e, s: e.activation(xg[:, :, :], x[:, :, :], ACT.Copy),
               after=["F.x", "G.y3@-1"], mark="xcopy")

        def g_load():
            op("sp", "G", lambda e, s: e.dma_start(
                acol[:, :], cols0.rearrange("p (b m) -> b p m", b=NB)[s, :, :]),
               after=["G.g1s1@-1", f"G.h{EC - 1}@-1"], mark="acol", dma=1)

        def g_h(i):
            b = hb[i % 3]
            for m2 in range(2):
                m = 2 * i + m2
                for k in range(4):
                    op("pe", "G", lambda e, s, m=m, m2=m2, k=k: e.matmul(
                        b.ap[:, m2, :], w1[:, k, m, :], comb[:, k, :], start=(k == 0), stop=(k == 3)),
                       after=(["F.nxcopy", "F.evcopy"] + take(b, "G")) if m2 + k == 0 else [],
                       mark=f"hp{i}" if m2 * 4 + k == 7 else None)
            for m2 in range(2):
                m = 2 * i + m2
                op("act", "G", lambda e, s, m=m, m2=m2: e.activation(h[:, m, :], b.ap[:, m2, :], ACT.Silu,
                                                                    bias=acol[:, m:m + 1]),
                   after=[f"G.hp{i}", "G.acol", f"G.ep{m // 4}@-1"] if m2 == 0 else [], mark=f"h{m}")
            empties(b, "G", f"h{2 * i + 1}")

        def g_e2(ex):
            b = eb[ex % 2]
            for tt in range(TT):
                for k in range(4):
                    op("pe", "G", lambda e, s, tt=tt, k=k: e.matmul(
                        b.ap[:, tt, :], h[:, 4 * ex + k, tt * P:(tt + 1) * P], w2[:, 4 * ex + k, :],
                        start=(k == 0), stop=(k == 3)),
                       after=([f"G.h{4 * ex + 3}"] + take(b, "G")) if tt + k == 0 else [],
                       mark=f"ep{ex}" if tt * 4 + k == 7 else None)
            for tt in range(TT):
                sc = lambda tt=tt: prob[:, tt, ex:ex + 1]
                last = "r_last" if ex == NE - 1 and tt == TT - 1 else f"r{ex}{tt}"
                if ex == 0:
                    op("dve", "G", lambda e, s, tt=tt: e.tensor_scalar(r[:, tt, :], b.ap[:, tt, :],
                                                                      prob[:, tt, 0:1], None, ALU.mult),
                       after=["G.ep0", "F.prob1", "G.rt@-1"], mark=f"r{ex}{tt}")
                else:
                    op("dve", "G", lambda e, s, tt=tt: e.scalar_tensor_tensor(
                        r[:, tt, :], b.ap[:, tt, :], prob[:, tt, ex:ex + 1], r[:, tt, :], ALU.mult, ALU.add),
                       after=[f"G.ep{ex}", f"G.b{ex - 1}{tt}"], mark=f"r{ex}{tt}")
                bl = "r_last" if ex == NE - 1 and tt == TT - 1 else f"b{ex}{tt}"
                op("dve", "G", lambda e, s, tt=tt: e.scalar_tensor_tensor(
                    r[:, tt, :], b2[:, ex, :], prob[:, tt, ex:ex + 1], r[:, tt, :], ALU.mult, ALU.add),
                   after=[f"G.r{ex}{tt}"], mark=bl)
            empties(b, "G", f"r{ex}1")

        def g_gate1():
            b = gb
            for m in range(CC):
                for k in range(4):
                    op("pe", "G", lambda e, s, m=m, k=k: e.matmul(b.ap[:, m, :], g1[:, k, m * P:(m + 1) * P],
                                                                 comb[:, k, :], start=(k == 0), stop=(k == 3)),
                       after=(["F.nxcopy", "F.evcopy"] + take(b, "G")) if m + k == 0 else [],
                       mark="g1p" if m * 4 + k == 7 else None)
            for m in range(CC):
                op("act", "G", lambda e, s, m=m: e.activation(gT[:, m, :], b.ap[:, m, :], ACT.Silu,
                                                             bias=acol[:, EC + m:EC + m + 1]),
                   after=["G.g1p", "G.acol", "G.g2p@-1"] if m == 0 else [], mark=f"g1s{m}")
            empties(b, "G", "g1s1")

        def g_gate2():
            b = gb
            for tt in range(TT):
                for k in range(CC):
                    op("pe", "G", lambda e, s, tt=tt, k=k: e.matmul(b.ap[:, tt, :], gT[:, k, tt * P:(tt + 1) * P],
                                                                   g2[:, k, :], start=(k == 0), stop=(k == 1)),
                       after=(["G.g1s1"] + take(b, "G")) if tt + k == 0 else [],
                       mark="g2p" if tt + k == 2 else None)
            op("dve", "G", lambda e, s: e.tensor_tensor(gp[:, :, :], b.ap[:, :, :],
                                                       bg2[:, :].unsqueeze(1).to_broadcast([P, TT, D]), ALU.add),
               after=["G.g2p", "G.th@-1"], mark="gp")
            empties(b, "G", "gp")
            op("act", "G", lambda e, s: e.activation(th[:, :, :], gp[:, :, :], ACT.Tanh, scale=0.5),
               after=["G.gp", "G.y2@-1"], mark="th")
            op("dve", "G", lambda e, s: e.tensor_scalar(th[:, :, :], th[:, :, :], 0.5, 0.5, ALU.mult, ALU.add),
               after=["G.th"], mark="gate")

        def g_out():
            b = gb
            for tt in range(TT):
                for c in range(CC):
                    op("pe", "G", lambda e, s, tt=tt, c=c: e.transpose(
                        b.ap[:, c, tt * P:(tt + 1) * P], r[:, tt, c * P:(c + 1) * P], ident[:, :]),
                       after=(["G.r_last", f"G.b{NE - 1}0"] + take(b, "G")) if tt + c == 0 else [],
                       mark="rt" if tt + c == 2 else None)
            op("act", "G", lambda e, s: e.activation(rT[:, :, :], b.ap[:, :, :], ACT.Copy),
               after=["G.rt", "G.yp@-1"], mark="rT")
            empties(b, "G", "rT")
            b2_ = eb[1]
            for tt in range(TT):
                for k in range(CC):
                    op("pe", "G", lambda e, s, tt=tt, k=k: e.matmul(b2_.ap[:, tt, :], rT[:, k, tt * P:(tt + 1) * P],
                                                                   wo[:, k, :], start=(k == 0), stop=(k == 1)),
                       after=(["G.rT"] + take(b2_, "G")) if tt + k == 0 else [],
                       mark="yp" if tt + k == 2 else None)
            op("dve", "G", lambda e, s: e.tensor_tensor(y[:, :, :], b2_.ap[:, :, :],
                                                       bo[:, :].unsqueeze(1).to_broadcast([P, TT, D]), ALU.add),
               after=["G.yp", "G.store@-1"], mark="y1")
            empties(b2_, "G", "y1")
            op("dve", "G", lambda e, s: e.tensor_tensor(y[:, :, :], y[:, :, :], th[:, :, :], ALU.mult),
               after=["G.y1", "G.gate"], mark="y2")
            op("dve", "G", lambda e, s: e.tensor_tensor(y[:, :, :], y[:, :, :], xg[:, :, :], ALU.add),
               after=["G.y2", "F.xcopy"], mark="y3")
            op("sp", "G", lambda e, s: e.dma_start(by_tile(x_out[s, :, :]), y[:, :, :]),
               after=["G.y3"], mark="store", dma=1)

        def iteration(n, hi, active):
            pl.iteration = n
            pl.begin(active)
            f_load()
            g_load()
            g_h(0)
            f_norm()
            g_h(1)
            f_transpose()
            g_e2(0)
            f_qkv()
            g_h(2)
            f_scores()
            g_h(3)
            g_e2(1)
            f_evidence()
            g_gate1()
            f_router()
            g_h(4)
            g_h(5)
            g_gate2()
            g_e2(2)
            g_out()
            f_hand_over()
            pl.end(n, hi)

        iteration(0, 1, "F")
        iteration(1, 2, "FG")
        iteration(2, NB, "FG")
        iteration(NB, NB + 1, "G")

        block = stack.enter_context(nc.Block())

        @block.sync
        def _(eng):
            for dst, src in loads:
                eng.dma_start(dst, src).then_inc(s_w0, 16)
            prefetch(eng)
            pl.emit("sp", eng)
            eng.wait_ge(pl.sem("G.store"), 16 * NB)

        @block.gpsimd
        def _(eng):
            pl.emit("pool", eng)

        @block.scalar
        def _(eng):
            pl.emit("act", eng)

        @block.vector
        def _(eng):
            eng.wait_ge(s_w0, 16 * len(loads))
            pl.emit("dve", eng)

        @block.tensor
        def _(eng):
            eng.wait_ge(s_w0, 16 * len(loads))
            pl.emit("pe", eng)


def blocks(nc, t, xs, cols, rows, ident, half, eps5, eps6, WT, s_w, n_w, load_layer, by_tile, buffers):
    from concourse import mybir
    from contextlib import ExitStack
    F32, F32R = mybir.dt.float32, mybir.dt.float32r
    BF16, F16 = mybir.dt.bfloat16, mybir.dt.float16
    ALU, ACT, AX = mybir.AluOpType, mybir.ActivationFunctionType, mybir.AxisListType
    LAYERS, SCALE = (1, 2, 3), HD ** -0.5

    with ExitStack() as stack:
        sb = buffers(stack)
        tile = lambda n: sb(n, [P, 2, 256])

        def stats(n):
            return sb(n + "_st", [P, TT, 6]), sb(n + "_mv", [P, TT, 2]), sb(n + "_rstd", [P, TT])

        x_in, xn_a, xT_a, res_a = tile("x_in"), tile("xn_a"), tile("xT_a"), tile("res_a")
        st_p, st_a, st_b, st_c = stats("p"), stats("a"), stats("b"), stats("c")
        col_a, row_a = sb("col_a", [P, 4]), sb("row_a", [P, 2, D])
        q_hl, k_hl = sb("q_hl", [P, 2, CC, NT], F32R), sb("k_hl", [P, 2, CC, NT], F32R)
        v_f = tile("v_f")
        v_cat = sb("v_cat", [P, TT, NH, VC], BF16)
        q_cat = sb("q_cat", [P, NPAIR, NT], F32R)
        k_cat = sb("k_cat", [P, NPAIR, NT], F32R)
        m_a, mT_a = sb("m_a", [P, TT, NH]), sb("mT_a", [NH, 2, NT], F32R)
        o_sum, o_rc, o_a, oT_a = sb("o_sum", [P, TT, 8, VW]), sb("o_rc", [P, TT, 8]), tile("o_a"), tile("oT_a")
        y_a, x_b = tile("y_a"), tile("x_b")
        NP_ = 2
        p_f = [sb(f"p_f{i}", [P, 1024]) for i in range(NP_)]
        p_h = [sb(f"p_h{i}", [P, 1024], F16) for i in range(NP_)]
        p_l = [sb(f"p_l{i}", [P, 1024], F16) for i in range(NP_)]
        xn_b, xT_b, res_b = tile("xn_b"), tile("xT_b"), tile("res_b")
        ctx, ctxn, ctxT = sb("ctx", [NC_TOK, 1, D]), sb("ctxn", [NC_TOK, 1, D]), sb("ctxT", [P, CC, NC_TOK])
        qc_hl, kc_hl = sb("qc_hl", [P, 2, CC, NT], F32R), sb("kc_hl", [P, 2, CC, NC_TOK], F32R)
        vc_f = sb("vc_f", [NC_TOK, D])
        vc_cat = sb("vc_cat", [NC_TOK, NH, VC], BF16)
        qc_cat = sb("qc_cat", [P, NPAIR, NT], F32R)
        kc_cat = sb("kc_cat", [P, NPAIR, CPAD], F32R)
        m_b, mT_b = sb("m_b", [P, TT, NH]), sb("mT_b", [NH, 2, NT], F32R)
        o_b, oT_b, x_c = tile("o_b"), tile("oT_b"), tile("x_c")
        xn_c, xT_c, res_c = tile("xn_c"), tile("xT_c"), tile("res_c")
        col_c, row_c = sb("col_c", [P, 4]), sb("row_c", [P, 2, D])
        h_c, y_c = sb("h_c", [P, MC, NT]), tile("y_c")

        score = [Bank(stack.enter_context(nc.psum_tensor(f"score{i}", [P, 2, 512], F32))) for i in range(2)]
        obank = [Bank(stack.enter_context(nc.psum_tensor(f"obank{i}", [P, 8, 64], F32))) for i in range(2)]
        gbank = [Bank(stack.enter_context(nc.psum_tensor(f"gbank{i}", [P, 2, 256], F32))) for i in range(2)]
        turn = [0]
        through = {}
        for ph in "AB":
            for name, width in (("q", NT), ("k", NT if ph == "A" else NC_TOK)):
                through[ph, name] = nc.dram_tensor(f"via_{ph}_{name}", (2, CC, P, width), F32, kind="Internal").ap()
            through[ph, "m"] = nc.dram_tensor(f"via_{ph}_m", (NH, 2, NT), F32, kind="Internal").ap()
        s_one = stack.enter_context(nc.semaphore("b_const"))

        pl = Pipeline(nc, "b", dict(P=0, A=1, B=2, C=3), 3 * NB, stack)
        op, take, empties = pl.op, pl.take, pl.empties

        def run(L):
            pass

        state = {}

        def W(ph):
            return WT[state["L"][ph] % 2]

        def seq_of(ph, s):
            return s - (state["L"][ph] - 1) * NB

        def gemm(ph, bank, out, pairs, after, mark, start_take=True):
            w = (take(bank, ph) if start_take else [])
            n, first = len(pairs), True
            for i, (o, terms) in enumerate(pairs):
                for k, (l, r_) in enumerate(terms):
                    op("pe", ph, lambda e, s, o=o, l=l, r_=r_, k=k, last=len(terms) - 1: e.matmul(
                        o, l, r_, start=(k == 0), stop=(k == last)),
                       after=(list(after) + w) if first else [],
                       mark=mark if i == n - 1 and k == len(terms) - 1 else None)
                    first = False

        def transposes(ph, bank, src, after, mark):
            for i in range(TT * CC):
                tt, c = divmod(i, CC)
                op("pe", ph, lambda e, s, tt=tt, c=c: e.transpose(
                    bank.ap[:, c, tt * P:(tt + 1) * P], src[:, tt, c * P:(c + 1) * P], ident[:, :]),
                   after=(list(after) + take(bank, ph)) if i == 0 else [], mark=mark if i == 3 else None)

        def g_use():
            turn[0] += 1
            return gbank[turn[0] % 2]

        def p_load():
            L = state["L"]["P"]
            after = ["A.res@-1", "P.xn1@-1"]
            if L > 1:
                after.append(f"C.store@-{NB}")
            op("sp", "P", lambda e, s: e.dma_start(x_in[:, :, :], by_tile(xs[L - 1][seq_of("P", s), :, :])),
               after=after, mark="x", dma=1)

        def p_norm():
            e_ = eps5 if state["L"]["P"] == 3 else eps6
            norm_ops(pl, "P", "", x_in, *st_p, e_, half, xn_a, (P, TT), ["P.x"], ["A.xt@-1"])

        def a_load():
            op("sp", "A", lambda e, s: e.dma_start(
                col_a[:, :], cols[state["L"]["A"]].rearrange("p (b m) -> b p m", b=NB)[seq_of("A", s), :, 0:4]),
               after=["A.xT1@-1"], mark="col", dma=1)
            op("sp", "A", lambda e, s: e.dma_start(
                row_a[:, :, :].rearrange("p g f -> p (g f)"),
                rows[state["L"]["A"]][seq_of("A", s), 0:2 * D].unsqueeze(0).to_broadcast([P, 2 * D])),
               after=["A.y@-1", "A.res@-1"], mark="row", dma=1)

        def a_start():
            op("pool", "A", lambda e, s: e.tensor_tensor(
                res_a[:, :, :], x_in[:, :, :], row_a[:, 1, :].unsqueeze(1).to_broadcast([P, TT, D]), ALU.add),
               after=["P.x", "A.row", "A.xb@-1"], mark="res")
            b = g_use()
            transposes("A", b, xn_a, ["P.xn1"], "xt")
            for c in range(CC):
                op("act", "A", lambda e, s, c=c: e.activation(xT_a[:, c, :], b.ap[:, c, :], ACT.Identity,
                                                             bias=col_a[:, c:c + 1], scale=col_a[:, 2 + c:3 + c]),
                   after=["A.xt", "A.col", "A.vp@-1"] if c == 0 else [], mark=f"xT{c}")
            empties(b, "A", "xT1")

        def split(ph, bank, view, dst, bcol, at, name, ready, free):
            w = W(ph)
            for m in range(CC):
                op("act", ph, lambda e, s, m=m: e.activation(dst[:, 0, m, :], view(m), ACT.Identity,
                                                            bias=w["bcol"][:, at + m:at + m + 1]),
                   after=([ready] + free) if m == 0 else [], mark=f"{name}h{m}")
            for m in range(CC):
                op("dve", ph, lambda e, s, m=m: e.scalar_tensor_tensor(
                    dst[:, 1, m, :], view(m), w["bcol"][:, at + m:at + m + 1],
                    dst[:, 0, m, :].bitcast(F32), ALU.add, ALU.subtract),
                   after=([f"{ph}.{name}h1"] + free) if m == 0 else [], mark=f"{name}l{m}")

        def stack_rows(ph, src, dst, width, order, name, free):
            via = through[ph, name]
            op("sp", ph, lambda e, s: e.dma_start(
                via.rearrange("q c p n -> p (q c) n"), src[:, :, :, :].bitcast(F32).rearrange("p q c n -> p (q c) n")),
               after=[f"{ph}.{name}l1", f"{ph}.{name}h1", f"{ph}.{name}cat@-1"], mark=f"{name}out", dma=1)
            for i, part in enumerate(order):
                for c in range(CC):
                    op("sp", ph, lambda e, s, c=c, i=i, part=part: e.dma_start(
                        dst[64 * c + HD * i:64 * c + HD * (i + 1), :, 0:width].bitcast(F32),
                        via[part, c, :, :].rearrange("(j d) n -> d j n", d=HD)),
                       after=([f"{ph}.{name}out"] + free) if i + c == 0 else [],
                       mark=f"{name}cat", dma=6)

        def v_parts(ph, n, view, full, cat, bias, ready, free):
            part = lambda i: cat(i)
            op("dve", ph, lambda e, s: e.tensor_tensor(full(), view(), bias(), ALU.add),
               after=[ready, f"{ph}.v3@-1"], mark="vf")
            op("act", ph, lambda e, s: e.activation(part(0), full(), ACT.Copy), after=[f"{ph}.vf"] + free, mark="v1")
            op("dve", ph, lambda e, s: e.tensor_tensor(full(), full(), part(0), ALU.subtract),
               after=[f"{ph}.v1"], mark="vr")
            op("act", ph, lambda e, s: e.activation(part(1), full(), ACT.Copy), after=[f"{ph}.vr"], mark="v2")
            op("dve", ph, lambda e, s: e.tensor_tensor(part(2), full(), part(1), ALU.subtract),
               after=[f"{ph}.v2"] + free, mark="v3")

        def a_q():
            w, b = W("A"), g_use()
            gemm("A", b, None, [(b.ap[:, m, :], [(w["qkv"][:, k, m * P:(m + 1) * P], xT_a[:, k, :])
                                                 for k in range(CC)]) for m in range(CC)], ["A.xT1"], "qp")
            split("A", b, lambda m: b.ap[:, m, :], q_hl, "bcol", 0, "q", "A.qp", ["A.qout@-1"])
            empties(b, "A", "ql1")
            stack_rows("A", q_hl, q_cat, NT, (0, 1, 0), "q", ["A.stp7@-1"])

        def a_k():
            w, b = W("A"), g_use()
            gemm("A", b, None, [(b.ap[:, m, :], [(w["qkv"][:, k, D + m * P:D + (m + 1) * P], xT_a[:, k, :])
                                                 for k in range(CC)]) for m in range(CC)], ["A.xT1"], "kp")
            split("A", b, lambda m: b.ap[:, m, :], k_hl, "bcol", 2, "k", "A.kp", ["A.kout@-1"])
            empties(b, "A", "kl1")
            stack_rows("A", k_hl, k_cat, NT, (0, 0, 1), "k", ["A.stp7@-1"])

        def a_v():
            w, b = W("A"), g_use()
            gemm("A", b, None, [(b.ap[:, tt, :], [(xT_a[:, k, tt * P:(tt + 1) * P], w["qkv"][:, k, 2 * D:3 * D])
                                                  for k in range(CC)]) for tt in range(TT)], ["A.xT1"], "vp")
            v_parts("A", P, lambda: b.ap[:, :, :], lambda: v_f[:, :, :],
                    lambda i: v_cat[:, :, :, VW * i:VW * i + HD].rearrange("p t h d -> p (t h) d"),
                    lambda: w["bv"][:, :].unsqueeze(1).to_broadcast([P, TT, D]), "A.vp", ["A.pv7@-1"])
            empties(b, "A", "vf")

        heads3 = lambda ap: ap.rearrange("p t (h d) -> p (t h) d", d=HD)

        def a_max(i):
            b = score[i % 2]
            for tt in range(TT):
                for hf in range(2):
                    r0 = 64 * hf
                    op("pe", "A", lambda e, s, tt=tt, hf=hf, r0=r0: e.matmul(
                        b.ap[:, hf, tt * NT:(tt + 1) * NT], q_cat[r0:r0 + QROWS, i, tt * P:(tt + 1) * P],
                        k_cat[r0:r0 + QROWS, i, :], start=True, stop=True),
                       after=(["A.qcat", "A.kcat"] + take(b, "A")) if tt + hf == 0 else [],
                       mark=f"sp{i}" if tt + hf == 2 else None)
            op("dve", "A", lambda e, s: e.tensor_reduce(
                m_a[:, :, i::NPAIR].rearrange("p t h -> p h t"),
                b.ap[:, :, :].rearrange("p h (t k) -> p h t k", t=TT), AX.X, ALU.max),
               after=[f"A.sp{i}", "A.mt@-1"], mark=f"mx{i}")
            empties(b, "A", f"mx{i}")

        def max_rows(ph, m, mT, q_dst, name_last):
            b = g_use()
            for tt in range(TT):
                op("pe", ph, lambda e, s, tt=tt: e.transpose(b.ap[0:NH, 0, tt * P:(tt + 1) * P], m[:, tt, :],
                                                            ident[:, :]),
                   after=([f"{ph}.{name_last}"] + take(b, ph)) if tt == 0 else [], mark="mt" if tt else None)
            op("act", ph, lambda e, s: e.activation(mT[:, 0, :], b.ap[0:NH, 0, :], ACT.Copy),
               after=[f"{ph}.mt", f"{ph}.mout@-1"], mark="mh")
            op("dve", ph, lambda e, s: e.tensor_tensor(mT[:, 1, :], b.ap[0:NH, 0, :], mT[:, 0, :].bitcast(F32),
                                                      ALU.subtract),
               after=[f"{ph}.mh", f"{ph}.mout@-1"], mark="ml")
            empties(b, ph, "ml")
            via = through[ph, "m"]
            op("sp", ph, lambda e, s: e.dma_start(via, mT[:, :, :].bitcast(F32)),
               after=[f"{ph}.ml", f"{ph}.mh", f"{ph}.mrow@-1"], mark="mout", dma=1)
            for c in range(2):
                op("sp", ph, lambda e, s, c=c: e.dma_start(
                    q_dst[64 * c + QROWS:64 * c + QROWS + 2, :, :].bitcast(F32),
                    via[8 * c:8 * c + 8, :, :].rearrange("i q n -> q i n")),
                   after=[f"{ph}.mout"] if c == 0 else [], mark="mrow", dma=2)

        def weights(ph, name, b, rows_, slot):
            pf, phi, plo = p_f[slot], p_h[slot], p_l[slot]
            users = state["p_users"][slot]
            op("act", ph, lambda e, s: e.activation(pf[0:rows_, :], b.ap[0:rows_, :, :].rearrange("p h n -> p (h n)"),
                                                   ACT.Exp, scale=SCALE),
               after=[f"{ph}.stp{name}"] + users(ph, "lo"), mark=f"ex{name}")
            empties(b, ph, f"ex{name}")
            op("act", ph, lambda e, s: e.activation(phi[0:rows_, :], pf[0:rows_, :], ACT.Copy, scale=PSCALE),
               after=[f"{ph}.ex{name}"] + users(ph, "pv"), mark=f"ph{name}")
            op("dve", ph, lambda e, s: e.scalar_tensor_tensor(plo[0:rows_, :], pf[0:rows_, :], PSCALE,
                                                             phi[0:rows_, :], ALU.mult, ALU.subtract),
               after=[f"{ph}.ph{name}"] + users(ph, "pv"), mark=f"pl{name}")

        class Slot:

            def __init__(self):
                self.last, self.when = None, 0

            def __call__(self, ph, what):
                if self.last is None or ph not in pl.active:
                    return []
                other, name = self.last
                off = self.when - pl.iteration - pl.lags[other] + pl.lags[ph]
                return [f"{other}.{'pl' if what == 'lo' else 'pv'}{name}@{off}"]

            def used(self, ph, name):
                if ph in pl.active:
                    self.last, self.when = (ph, name), pl.iteration

        state["p_users"] = [Slot(), Slot()]
        pl.shared = score + obank + gbank + state["p_users"]

        def a_exp(i):
            b, slot = score[i % 2], i % 2
            for kc in range(TT):
                for hf in range(2):
                    r0 = 64 * hf
                    op("pe", "A", lambda e, s, kc=kc, hf=hf, r0=r0: e.matmul(
                        b.ap[:, hf, kc * NT:(kc + 1) * NT], k_cat[r0:r0 + QROWS + 2, i, kc * P:(kc + 1) * P],
                        q_cat[r0:r0 + QROWS + 2, i, :], start=True, stop=True),
                       after=(["A.mrow"] + take(b, "A")) if kc + hf == 0 else [],
                       mark=f"stp{i}" if kc + hf == 2 else None)
            weights("A", str(i), b, P, slot)

        def a_pv(i):
            slot = i % 2
            j = i % 4
            for tt in range(TT):
                ob = obank[tt]
                w = take(ob, "A") if j == 0 else []
                for hf in range(2):
                    terms = [(kc, src) for kc in range(TT) for src in (p_h, p_l)]
                    for n_, (kc, src) in enumerate(terms):
                        at = hf * 512 + kc * NT + tt * P
                        op("pe", "A", lambda e, s, hf=hf, kc=kc, src=src, at=at, n_=n_, ob=ob: e.matmul(
                            ob.ap[:, 4 * hf + j, 0:VC], src[slot][:, at:at + P], v_cat[:, kc, 8 * hf + i, :],
                            start=(n_ == 0), stop=(n_ == 3)),
                           after=([f"A.pl{i}", f"A.ph{i}", "A.v1", "A.v2", "A.v3"] + w) if n_ + hf == 0 else [],
                           mark=f"pv{i}" if tt + hf == 2 and n_ == 3 else None)
            state["p_users"][slot].used("A", str(i))

        def out_heads(ph, u, o, last):
            for tt in range(TT):
                ob = obank[tt]
                op("dve", ph, lambda e, s, tt=tt, ob=ob: e.tensor_reduce(
                    o_sum[:, tt, :, :], ob.ap[:, :, 0:VC].rearrange("p g (q e) -> p g e q", q=VP), AX.X, ALU.add),
                   after=[f"{ph}.{last}"] + state["o_last"][tt], mark=f"os{u}{tt}")
                empties(ob, ph, f"os{u}{tt}")
            for tt in range(TT):
                op("dve", ph, lambda e, s, tt=tt: e.reciprocal(o_rc[:, tt, :], o_sum[:, tt, :, HD]),
                   after=[f"{ph}.os{u}{tt}"], mark=f"rc{u}{tt}")
            for tt in range(TT):
                op("dve", ph, lambda e, s, tt=tt: e.tensor_tensor(
                    o[:, tt, :].rearrange("p (h f) -> p h f", h=2)[:, :, 4 * HD * u:4 * HD * (u + 1)]
                     .rearrange("p h (j d) -> p h j d", d=HD),
                    o_sum[:, tt, :, 0:HD].rearrange("p (h j) d -> p h j d", h=2),
                    o_rc[:, tt, :].rearrange("p (h j) -> p h j", h=2).unsqueeze(3).to_broadcast([P, 2, 4, HD]),
                    ALU.mult),
                   after=[f"{ph}.rc{u}{tt}"] + ([f"{ph}.ot@-1"] if u == 0 else []), mark=f"on{u}{tt}")

        state["o_last"] = [[], []]

        def tail(ph, o, oT, w, evac, norm):
            b = g_use()
            transposes(ph, b, o, [f"{ph}.on11", f"{ph}.on10"], "ot")
            op("act", ph, lambda e, s: e.activation(oT[:, :, :], b.ap[:, :, :], ACT.Copy),
               after=[f"{ph}.ot", f"{ph}.op@-1"], mark="oT")
            empties(b, ph, "oT")
            b2_ = g_use()
            gemm(ph, b2_, None, [(b2_.ap[:, tt, :], [(oT[:, k, tt * P:(tt + 1) * P], w[:, k, :])
                                                     for k in range(CC)]) for tt in range(TT)], [f"{ph}.oT"], "op")
            evac(b2_)
            norm()

        def a_tail():
            def evac(b):
                op("dve", "A", lambda e, s: e.tensor_tensor(
                    y_a[:, :, :], b.ap[:, :, :], row_a[:, 0, :].unsqueeze(1).to_broadcast([P, TT, D]), ALU.mult),
                   after=["A.op", "A.row"], mark="y")
                empties(b, "A", "y")
                op("dve", "A", lambda e, s: e.tensor_tensor(x_b[:, :, :], y_a[:, :, :], res_a[:, :, :], ALU.add),
                   after=["A.y", "A.res", "B.res@-1"] +
                   (["B.xt@-1"] if state["L"]["A"] == 3 else []), mark="xb")

            def norm():
                if state["L"]["A"] < 3:
                    norm_ops(pl, "A", "n", x_b, *st_a, eps6, half, xn_b, (P, TT), ["A.xb"], ["B.xt@-1"],
                             group="An")
            tail("A", o_a, oT_a, W("A")["o"], evac, norm)

        def b_load():
            op("sp", "B", lambda e, s: e.dma_start(ctx[:, 0, :], t["ctx_1024"][seq_of("B", s), :, :]),
               after=["B.ct@-1"] + (["B.cxn0@-1"] if state["L"]["B"] == 1 else []), mark="ctx", dma=1)

        def b_start():
            L, w = state["L"]["B"], W("B")
            src, ready = (xn_b, ["A.nxn1"]) if L < 3 else (x_b, ["A.xb"])
            op("pool", "B", lambda e, s: e.tensor_tensor(
                res_b[:, :, :], x_b[:, :, :], w["boc"][:, :].unsqueeze(1).to_broadcast([P, TT, D]), ALU.add),
               after=["A.xb", "B.xc@-1"], mark="res")
            b = g_use()
            transposes("B", b, src, ready, "xt")
            op("dve", "B", lambda e, s: e.tensor_copy(xT_b[:, :, :], b.ap[:, :, :]),
               after=["B.xt", "B.qp@-1"], mark="xT")
            empties(b, "B", "xT")
            if L == 1:
                norm_ops(pl, "B", "c", ctx, *st_b, eps6, half, ctxn, (NC_TOK, 1), ["B.ctx"], ["B.ct@-1"], group="Bn")
            cs, cr = (ctxn, "B.cxn0") if L == 1 else (ctx, "B.ctx")
            b2_ = g_use()
            for c in range(CC):
                op("pe", "B", lambda e, s, c=c: e.transpose(b2_.ap[:, 0, c * NC_TOK:(c + 1) * NC_TOK],
                                                           cs[:, 0, c * P:(c + 1) * P], ident[0:NC_TOK, 0:NC_TOK]),
                   after=([cr] + take(b2_, "B")) if c == 0 else [], mark="ct" if c else None)
            op("act", "B", lambda e, s: e.activation(
                ctxT[:, :, :], b2_.ap[:, 0, 0:CC * NC_TOK].rearrange("p (c k) -> p c k", c=CC), ACT.Copy),
               after=["B.ct", "B.vp@-1"], mark="cT")
            empties(b2_, "B", "cT")

        def b_q():
            w, b = W("B"), g_use()
            gemm("B", b, None, [(b.ap[:, m, :], [(w["qc"][:, k, m * P:(m + 1) * P], xT_b[:, k, :])
                                                 for k in range(CC)]) for m in range(CC)], ["B.xT"], "qp")
            split("B", b, lambda m: b.ap[:, m, :], qc_hl, "bcol", 4, "q", "B.qp", ["B.qout@-1"])
            empties(b, "B", "ql1")
            stack_rows("B", qc_hl, qc_cat, NT, (0, 1, 0), "q", ["B.stp3@-1"])

        def b_kv():
            w, b = W("B"), g_use()
            kv_ = lambda m: b.ap[:, 0, m * NC_TOK:(m + 1) * NC_TOK]
            gemm("B", b, None, [(kv_(m), [(w["kvc"][:, k, m * P:(m + 1) * P], ctxT[:, k, :])
                                          for k in range(CC)]) for m in range(CC)] +
                 [(b.ap[0:NC_TOK, 1, :], [(ctxT[:, k, :], w["kvc"][:, k, D:2 * D]) for k in range(CC)])],
                 ["B.cT"], "vp")
            split("B", b, kv_, kc_hl, "bcol", 6, "k", "B.vp", ["B.kout@-1"])
            stack_rows("B", kc_hl, kc_cat, NC_TOK, (0, 0, 1), "k", ["B.stp3@-1"])
            v_parts("B", NC_TOK, lambda: b.ap[0:NC_TOK, 1, :], lambda: vc_f[:, :],
                    lambda i: vc_cat[:, :, VW * i:VW * i + HD].rearrange("p h d -> p h d"),
                    lambda: w["bvc"][0:NC_TOK, :], "B.vp", ["B.pv3@-1"])
            empties(b, "B", "vf")

        def b_max(i):
            b = score[i % 2]
            view = b.ap[:, :, :].rearrange("p h (j t k) -> p h j t k", j=2, t=TT)
            for j in range(2):
                for tt in range(TT):
                    for hf in range(2):
                        r0 = 64 * hf
                        op("pe", "B", lambda e, s, j=j, tt=tt, hf=hf, r0=r0: e.matmul(
                            view[:, hf, j, tt, 0:CPAD], qc_cat[r0:r0 + QROWS, 2 * i + j, tt * P:(tt + 1) * P],
                            kc_cat[r0:r0 + QROWS, 2 * i + j, :], start=True, stop=True),
                           after=(["B.qcat", "B.kcat"] + take(b, "B")) if j + tt + hf == 0 else [],
                           mark=f"sp{i}" if j + tt + hf == 3 else None)
            for hf in range(2):
                op("dve", "B", lambda e, s, hf=hf: e.tensor_reduce(
                    m_b[:, :, 8 * hf + 2 * i:8 * hf + 2 * i + 2].rearrange("p t j -> p j t"),
                    view[:, hf, :, :, 0:NC_TOK], AX.X, ALU.max),
                   after=[f"B.sp{i}", "B.mt@-1"], mark=f"mx{i}{hf}")
            empties(b, "B", f"mx{i}1")

        def b_exp(i):
            b, slot = score[i % 2], i % 2
            for j in range(2):
                for hf in range(2):
                    r0 = 64 * hf
                    op("pe", "B", lambda e, s, j=j, hf=hf, r0=r0: e.matmul(
                        b.ap[0:NC_TOK, hf, j * NT:(j + 1) * NT], kc_cat[r0:r0 + QROWS + 2, 2 * i + j, 0:NC_TOK],
                        qc_cat[r0:r0 + QROWS + 2, 2 * i + j, :], start=True, stop=True),
                       after=(["B.mrow"] + take(b, "B")) if j + hf == 0 else [],
                       mark=f"stp{i}" if j + hf == 2 else None)
            weights("B", str(i), b, NC_TOK, slot)

        def b_pv(i):
            slot = i % 2
            for tt in range(TT):
                ob = obank[tt]
                w = take(ob, "B") if i % 2 == 0 else []
                for j in range(2):
                    jj = (2 * i + j) % 4
                    for hf in range(2):
                        for n_, src in enumerate((p_h, p_l)):
                            at = hf * 512 + j * NT + tt * P
                            op("pe", "B", lambda e, s, hf=hf, src=src, at=at, n_=n_, ob=ob, jj=jj, j=j: e.matmul(
                                ob.ap[:, 4 * hf + jj, 0:VC], src[slot][0:NC_TOK, at:at + P],
                                vc_cat[:, 8 * hf + 2 * i + j, :], start=(n_ == 0), stop=(n_ == 1)),
                               after=([f"B.pl{i}", f"B.ph{i}", "B.v1", "B.v2", "B.v3"] + w) if j + n_ + hf == 0 else [],
                               mark=f"pv{i}" if tt + j + hf == 3 and n_ == 1 else None)
            state["p_users"][slot].used("B", str(i))

        def b_tail():
            def evac(b):
                op("dve", "B", lambda e, s: e.tensor_tensor(x_c[:, :, :], b.ap[:, :, :], res_b[:, :, :], ALU.add),
                   after=["B.op", "B.res", "C.res@-1"], mark="xc")
                empties(b, "B", "xc")

            def norm():
                e_ = eps5 if state["L"]["B"] == 3 else eps6
                norm_ops(pl, "B", "n", x_c, *st_c, e_, half, xn_c, (P, TT), ["B.xc"], ["C.xt@-1"])
            tail("B", o_b, oT_b, W("B")["oc"], evac, norm)

        def c_load():
            L = state["L"]["C"]
            op("sp", "C", lambda e, s: e.dma_start(
                col_c[:, :], cols[L].rearrange("p (b m) -> b p m", b=NB)[seq_of("C", s), :, 4:8]),
               after=["C.xT1@-1"], mark="col", dma=1)
            op("sp", "C", lambda e, s: e.dma_start(
                row_c[:, :, :].rearrange("p g f -> p (g f)"),
                rows[L][seq_of("C", s), 2 * D:4 * D].unsqueeze(0).to_broadcast([P, 2 * D])),
               after=["C.y@-1", "C.res@-1"], mark="row", dma=1)

        def c_start():
            op("pool", "C", lambda e, s: e.tensor_tensor(
                res_c[:, :, :], x_c[:, :, :], row_c[:, 1, :].unsqueeze(1).to_broadcast([P, TT, D]), ALU.add),
               after=["B.xc", "C.row", "C.yo@-1"], mark="res")
            b = g_use()
            transposes("C", b, xn_c, ["B.nxn1"], "xt")
            for c in range(CC):
                op("act", "C", lambda e, s, c=c: e.activation(xT_c[:, c, :], b.ap[:, c, :], ACT.Identity,
                                                             bias=col_c[:, c:c + 1], scale=col_c[:, 2 + c:3 + c]),
                   after=["C.xt", "C.col", "C.hp3@-1"] if c == 0 else [], mark=f"xT{c}")
            empties(b, "C", "xT1")

        def c_up(i):
            w, b = W("C"), g_use()
            gelu = ACT.Gelu if state["L"]["C"] == 3 else ACT.Gelu_apprx_tanh
            gemm("C", b, None, [(b.ap[:, j, :], [(w["w1"][:, k, (2 * i + j) * P:(2 * i + j + 1) * P], xT_c[:, k, :])
                                                 for k in range(CC)]) for j in range(2)], ["C.xT1"], f"hp{i}")
            for j in range(2):
                m = 2 * i + j
                op("act", "C", lambda e, s, j=j, m=m: e.activation(h_c[:, m, :], b.ap[:, j, :], gelu,
                                                                  bias=w["bcol"][:, 8 + m:9 + m]),
                   after=[f"C.hp{i}", "C.down@-1"] if j == 0 else [], mark=f"h{m}")
            empties(b, "C", f"h{2 * i + 1}")

        def c_down(tt):
            w = W("C")
            b = state["down"] = g_use() if tt == 0 else state["down"]
            for m in range(MC):
                op("pe", "C", lambda e, s, m=m: e.matmul(b.ap[:, tt, :], h_c[:, m, tt * P:(tt + 1) * P],
                                                        w["w2"][:, m, :], start=(m == 0), stop=(m == MC - 1)),
                   after=([f"C.h{MC - 1}"] + (take(b, "C") if tt == 0 else [])) if m == 0 else [],
                   mark="down" if tt == 1 and m == MC - 1 else None)
            if tt == 0:
                return
            op("dve", "C", lambda e, s: e.tensor_tensor(
                y_c[:, :, :], b.ap[:, :, :], row_c[:, 0, :].unsqueeze(1).to_broadcast([P, TT, D]), ALU.mult),
               after=["C.down", "C.row", "C.store@-1"], mark="y")
            empties(b, "C", "y")
            op("dve", "C", lambda e, s: e.tensor_tensor(y_c[:, :, :], y_c[:, :, :], res_c[:, :, :], ALU.add),
               after=["C.y", "C.res"], mark="yo")
            L = state["L"]["C"]
            op("sp", "C", lambda e, s: e.dma_start(by_tile(xs[L][seq_of("C", s), :, :]), y_c[:, :, :]),
               after=["C.yo"], mark="store", dma=1)

        def iteration(lo, hi):
            pl.iteration = lo
            act = [ph for ph in "PABC" if 0 <= lo - pl.lags[ph] < 3 * NB]
            pl.begin(act)
            state["L"] = {ph: (lo - pl.lags[ph]) // NB + 1 for ph in act}
            fixed = dict(state["L"])
            turn[0] = 0

            def on(*phases):
                return all(p_ in act for p_ in phases)

            if on("A"): a_load()
            if on("C"): c_load()
            if on("B"): b_load()
            if on("A"): a_start(); a_q()
            if on("B"): b_start(); b_q()
            if on("A"): a_k(); a_v()
            if on("B"): b_kv()
            if on("C"): c_start()
            if on("P"): p_load()
            for i in range(NPAIR):
                if on("A"): a_max(i)
                if i % 2 and on("C"): c_up(i // 2)
            if on("A"): max_rows("A", m_a, mT_a, q_cat, "mx7")
            if on("B"):
                for i in range(4): b_max(i)
                max_rows("B", m_b, mT_b, qc_cat, "mx31")
            if on("C"): c_down(0)
            if on("A"):
                for i in range(NPAIR):
                    a_exp(i)
                    if i: a_pv(i - 1)
                    if i == 4:
                        out_heads("A", 0, o_a, "pv3")
            if on("B"):
                b_exp(0)
            if on("A"):
                a_pv(7)
                out_heads("A", 1, o_a, "pv7")
            if on("C"): c_down(1)
            if on("B"):
                for i in range(1, 4):
                    b_exp(i)
                    b_pv(i - 1)
                    if i == 2: out_heads("B", 0, o_b, "pv1")
                b_pv(3)
                out_heads("B", 1, o_b, "pv3")
            if on("P"): p_norm()
            if on("B"): b_tail()
            if on("A"): a_tail()
            ops = pl.ops
            for o in ops:
                o.emit = bind(o.emit, fixed)
            pl.end(lo, hi)

        def bind(emit, layers):
            def f(e, s):
                state["L"] = layers
                return emit(e, s)
            return f

        n = 0
        last = 3 * NB + 3
        while n < last:
            lo, hi = n, n + 1
            if n < 3 * NB and n % NB == 4:
                hi = n // NB * NB + NB
            iteration(lo, hi)
            n = hi

        seams = {L: [NB * (L - 1) + pl.lags[ph] for ph in "ABC"] for L in (2, 3)}
        block = stack.enter_context(nc.Block())

        def emit_with_weights(name, eng, waits):
            segs = pl.segments
            for seg in segs:
                for L in LAYERS:
                    if seg[0] == NB * (L - 1) + 1:
                        waits(eng, L)
                pl.segments = [seg]
                pl.emit(name, eng)
            pl.segments = segs

        def wait_weights(eng, L):
            eng.wait_ge(s_w[L], n_w[L])

        @block.sync
        def _(eng):
            eng.wait_ge(s_one, 3)

            def waits(eng, L):
                pass
            segs = pl.segments
            for seg in segs:
                if seg[0] == NB + 4:
                    for mark in ("C.down", "B.op", "A.op", "B.res", "A.ql1", "A.kl1", "A.vf", "B.ql1", "B.kl1",
                                 "B.vf", f"C.h{MC - 1}"):
                        eng.wait_ge(pl.sem(pl.marks[mark].group), pl.value(mark, NB - 1))
                    load_layer(eng, 3)
                pl.segments = [seg]
                pl.emit("sp", eng)
            pl.segments = segs
            eng.wait_ge(pl.sem("C.store"), 16 * 3 * NB)

        @block.gpsimd
        def _(eng):
            emit_with_weights("pool", eng, wait_weights)

        @block.scalar
        def _(eng):
            emit_with_weights("act", eng, wait_weights)

        @block.vector
        def _(eng):
            eng.memset(k_cat[:, :, :].bitcast(F32), -1.0)
            eng.memset(kc_cat[:, :, :].bitcast(F32), -1.0).then_inc(s_one, 1)
            eng.memset(v_cat[:, :, :, :].rearrange("p t h c -> p (t h c)"), 0.0)
            eng.memset(vc_cat[:, :, :].rearrange("p h c -> p (h c)"), 0.0).then_inc(s_one, 1)
            eng.wait_ge(s_one, 2)
            eng.memset(v_cat[:, :, :, HD:HD + 1], 1.0)
            eng.memset(vc_cat[:, :, HD:HD + 1], 1.0).then_inc(s_one, 1)
            emit_with_weights("dve", eng, wait_weights)

        @block.tensor
        def _(eng):
            eng.wait_ge(s_one, 3)
            emit_with_weights("pe", eng, wait_weights)


def kernel(**inputs):
    import concourse.bacc as bacc
    from concourse import mybir
    from concourse.bass_utils import run_bass_kernel_spmd

    nc = bacc.Bacc("TRN2", target_bir_lowering=False, num_devices=1)
    arrays, t = {}, {}
    for name in inputs:
        a = np.ascontiguousarray(inputs[name])
        arrays[f"in_{name}_dram"] = a
        t[name] = nc.dram_tensor(f"in_{name}_dram", a.shape, mybir.dt.from_np(a.dtype), kind="ExternalInput").ap()
    t["out"] = nc.dram_tensor("out_0_dram", (NB, NT, D), mybir.dt.float32, kind="ExternalOutput").ap()
    build(nc, t)
    r = run_bass_kernel_spmd(nc, [arrays], core_ids=[0])
    return r.results[0]["out_0_dram"]
```

```python
import numpy as np

NB, NT, D, NC_TOK = 16, 256, 256, 77
NH, HD = 16, 16
P = 128
TT, CC = NT // P, D // P
MLP = 1024
MC = MLP // P
NE, RH = 3, 512
EC = NE * RH // P
VP, VW = 3, HD + 1
VC = VP * VW
NPAIR = NH // 2
QROWS = 3 * HD
CPAD = NC_TOK + 1
PSCALE = 2.0 ** 15


class Mark:

    def __init__(self, group, place, count, dma):
        self.group, self.place, self.count, self.dma = group, place, count, dma


class Op:
    def __init__(self, engine, phase, emit, after, mark, alone):
        self.engine, self.phase, self.emit, self.after = engine, phase, emit, after
        self.mark, self.alone = mark, alone


class Bank:

    def __init__(self, ap):
        self.ap, self.emptied, self.when = ap, None, 0


class Slot:

    def __init__(self):
        self.last, self.when = None, 0


class Ring:

    def __init__(self, items):
        self.items = list(items)
        self.rewind()

    def rewind(self):
        self.order, self.held = list(self.items), []

    def get(self):
        item = next(i for i in self.order if i not in self.held)
        self.order.remove(item)
        self.order.append(item)
        self.held.append(item)
        return item

    def free(self, item):
        self.held.remove(item)


class Pipeline:

    def __init__(self, nc, name, lags, n_seq, stack):
        self.nc, self.name, self.lags, self.n_seq, self.stack = nc, name, lags, n_seq, stack
        self.marks, self.per_seq, self.sems = {}, {}, {}
        self.segments, self.shared = [], []

    def begin(self, active):
        self.active, self.ops, self.seen, self.counts = active, [], set(), {}
        self.group_of = {}

    def op(self, engine, phase, emit, after=(), mark=None, dma=0, group=None, alone=False):
        if phase not in self.active:
            return
        if mark:
            name = f"{phase}.{mark}"
            if name not in self.seen:
                self.seen.add(name)
                g = f"{name}" if dma else f"{engine}_{group or phase}"
                place = self.counts.get(g, 0)
                self.counts[g] = place + 1
                m = Mark(g, place, dma or 1, bool(dma))
                old = self.marks.setdefault(name, m)
                assert (old.group, old.place, old.count) == (m.group, m.place, m.count), name
            mark = name
        self.ops.append(Op(engine, phase, emit, list(after), mark, alone))

    def take(self, bank, phase):
        if phase not in self.active or bank.emptied is None:
            return []
        other = bank.emptied.split(".")[0]
        off = bank.when - self.iteration + self.lags[other] * -1 + self.lags[phase]
        return [f"{bank.emptied}@{off}"] if off else [bank.emptied]

    def empties(self, bank, phase, mark):
        if phase in self.active:
            bank.emptied, bank.when = f"{phase}.{mark}", self.iteration

    def end(self, lo, hi):
        for g, n in self.counts.items():
            assert self.per_seq.setdefault(g, n) == n, g
        for b in self.shared:
            if b.when == lo:
                b.when = hi - 1
        self.segments.append((lo, hi, self.ops))

    def sem(self, group):
        if group not in self.sems:
            name = f"{self.name}_{group}".replace(".", "_")
            self.sems[group] = self.stack.enter_context(self.nc.semaphore(name))
        return self.sems[group]

    def value(self, mark, seq):
        m = self.marks[mark]
        if m.dma:
            return seq * (16 * m.count) + 16 * m.count
        return seq * self.per_seq[m.group] + (m.place + 1)

    def emit(self, engine, eng):
        for lo, hi, ops in self.segments:
            mine = [o for o in ops if o.engine == engine]
            if not mine:
                continue
            if hi == lo + 1:
                self._body(eng, mine, lo, False)
            else:
                with eng.Fori(lo, hi) as n:
                    self._body(eng, mine, n, True)

    def _body(self, eng, ops, n, loop):
        waited = {}
        for o in ops:
            seq = n - self.lags[o.phase]
            waits = []
            for w in o.after:
                name, _, off = w.partition("@")
                off = int(off or 0)
                m = self.marks[name]
                lag = self.lags[o.phase]
                reach = (off - lag, m.place)
                if waited.get(m.group, (-99, 0)) >= reach:
                    continue
                waited[m.group] = reach
                if loop:
                    val = self.value(name, seq + off)
                else:
                    at = min(seq + off, self.n_seq - 1)
                    if at < 0:
                        continue
                    val = self.value(name, at)
                waits.append((self.sem(m.group), val))
            for s, v in waits:
                eng.wait_ge(s, v)
                if loop and (o.alone or o.engine == "sp"):
                    eng.sem_inc(self.sem("holder"), 1)
            ins = o.emit(eng, seq)
            if o.mark:
                m = self.marks[o.mark]
                ins.then_inc(self.sem(m.group), 16 if m.dma else 1)


def build(nc, t):
    import concourse.bass as bass
    from concourse import mybir
    from contextlib import ExitStack

    F32, F32R = mybir.dt.float32, mybir.dt.float32r
    BF16, F16 = mybir.dt.bfloat16, mybir.dt.float16
    ALU, ACT, AX = mybir.AluOpType, mybir.ActivationFunctionType, mybir.AxisListType

    root = ExitStack()

    def buffers(stack):
        def sb(name, shape, dt=F32):
            return stack.enter_context(nc.sbuf_tensor(name, shape, dt))
        return sb

    def scratch(name, shape):
        return nc.dram_tensor(name, shape, F32, kind="Internal").ap()

    xs = [scratch(f"x_after_L{i}", (NB, NT, D)) for i in range(3)] + [t["out"]]
    cols = [scratch("cols_L0", (P, NB * 14))] + [scratch(f"cols_L{i}", (P, NB * 8)) for i in (1, 2, 3)]
    rows = [scratch("rows_L0", (NB, NE))] + [scratch(f"rows_L{i}", (NB, 4 * D)) for i in (1, 2, 3)]

    def chunks(w):
        return w.rearrange("(k p) n -> p k n", p=P)

    def column(v):
        return v.rearrange("(k p) -> p k", p=P)

    def spread(v, n=P):
        return v.unsqueeze(0).to_broadcast([n, v.shape[0]])

    def by_tile(x):
        return x.rearrange("(t p) f -> p t f", p=P)

    with root, nc.allow_non_contiguous_dma(reason="bias vectors as columns, a few KB"):
        sbr = buffers(root)
        ident = sbr("ident", [P, P])
        half = sbr("minus_half", [P, 2])
        eps5 = sbr("eps5", [P, 2])
        eps6 = sbr("eps6", [P, 2])
        WT = []
        for s in range(2):
            WT.append(dict(
                qkv=sbr(f"w_qkv{s}", [P, CC, 3 * D]), o=sbr(f"w_o{s}", [P, CC, D]),
                qc=sbr(f"w_qc{s}", [P, CC, D]), kvc=sbr(f"w_kvc{s}", [P, CC, 2 * D]),
                oc=sbr(f"w_oc{s}", [P, CC, D]), w1=sbr(f"w_1{s}", [P, CC, MLP]),
                w2=sbr(f"w_2{s}", [P, MC, D]),
                bcol=sbr(f"b_col{s}", [P, 16]),
                bv=sbr(f"b_v{s}", [P, D]), bvc=sbr(f"b_vc{s}", [P, D]), boc=sbr(f"b_oc{s}", [P, D])))
        s_w = [root.enter_context(nc.semaphore(f"weights_L{L}")) for L in range(4)]
        n_w = [0] * 4

        def layer_parts(L):
            if L == 1:
                g = lambda k: t["L1_xcond_" + k]
                return dict(qkv=[g("W_qkv")], o=g("W_proj"), qc=g("W_qc"), kvc=[g("W_kvc")], oc=g("W_cproj"),
                            w1=g("W_mlp1"), w2=g("W_mlp2"), bqkv=g("b_qkv"), bqc=g("b_qc"), bkvc=g("b_kvc"),
                            boc=g("b_cproj"), b1=g("b_mlp1"))
            if L == 2:
                g = lambda k: t["L2_xcond_" + k]
                return dict(qkv=[g("qkv_w")], o=g("sa_proj_w"), qc=g("q_w"), kvc=[g("kv_w")], oc=g("ca_proj_w"),
                            w1=g("fc1_w"), w2=g("fc2_w"), bqkv=g("qkv_b"), bqc=g("q_b"), bkvc=g("kv_b"),
                            boc=g("ca_proj_b"), b1=g("fc1_b"))
            g = lambda k: t["L3_xcond_" + k]
            return dict(qkv=[g("sa_qw"), g("sa_kw"), g("sa_vw")], o=g("sa_ow"), qc=g("ca_qw"),
                        kvc=[g("ca_kw"), g("ca_vw")], oc=g("ca_ow"), w1=g("ffn_w1"), w2=g("ffn_w2"),
                        bq=g("sa_qb"), bk=g("sa_kb"), bv=g("sa_vb"), bqc=g("ca_qb"), bkc=g("ca_kb"),
                        bvc=g("ca_vb"), boc=g("ca_ob"), b1=g("ffn_b1"))

        def load_layer(eng, L):
            w, p = WT[L % 2], layer_parts(L)

            def go(dst, src):
                eng.dma_start(dst, src).then_inc(s_w[L], 16)
                n_w[L] += 16

            def side_by_side(dst, parts):
                at = 0
                for x in parts:
                    go(dst[:, :, at:at + x.shape[1]], chunks(x))
                    at += x.shape[1]

            side_by_side(w["qkv"], p["qkv"])
            if L < 3:
                bq, bk, bv = (p["bqkv"][i * D:(i + 1) * D] for i in range(3))
                bkc, bvc = (p["bkvc"][i * D:(i + 1) * D] for i in range(2))
            else:
                bq, bk, bv, bkc, bvc = p["bq"], p["bk"], p["bv"], p["bkc"], p["bvc"]
            for i, b in enumerate((bq, bk, p["bqc"], bkc)):
                go(w["bcol"][:, 2 * i:2 * i + 2], column(b))
            go(w["bcol"][:, 8:16], column(p["b1"]))
            go(w["bv"][:, :], spread(bv))
            go(w["bvc"][:, :], spread(bvc))
            go(w["boc"][:, :], spread(p["boc"]))
            side_by_side(w["kvc"], p["kvc"])
            for k in ("o", "qc", "oc", "w1", "w2"):
                go(w[k][:, :, :], chunks(p[k]))

        tables(nc, t, cols, rows, ident, half, eps5, eps6, chunks, column, spread, buffers)
        mixture(nc, t, xs[0], cols[0], rows[0], ident, half, eps5, chunks, column, spread, by_tile, buffers,
                lambda eng: (load_layer(eng, 1), load_layer(eng, 2)))
        blocks(nc, t, xs, cols, rows, ident, half, eps5, eps6, WT, s_w, n_w, load_layer, by_tile, buffers)


def tables(nc, t, cols, rows, ident, half, eps5, eps6, chunks, column, spread, buffers):
    from concourse import mybir
    from contextlib import ExitStack
    F32 = mybir.dt.float32
    ALU, ACT = mybir.AluOpType, mybir.ActivationFunctionType

    with ExitStack() as stack:
        sb = buffers(stack)
        cond = sb("cond", [NB, D])
        cond_silu = sb("cond_silu", [NB, D])
        condT = sb("condT", [P, CC, NB])
        cond_siluT = sb("cond_siluT", [P, CC, NB])
        w_mod = [sb("w_mod1", [P, CC, 6 * D]), sb("w_mod2", [P, CC, 6 * D])]
        w_aff = [sb("w_aff1", [P, CC, 2 * D]), sb("w_aff2", [P, CC, 2 * D])]
        w_anchor = sb("w_anchor", [P, CC, EC + 2, P])
        w_router = sb("w_router", [P, CC, NE])
        b_mod = sb("b_mod", [P, 2, 12])
        b_aff = sb("b_aff", [P, 2, 4])
        ln_gb = sb("ln_gb", [P, 2, 4])
        b_anchor = sb("b_anchor", [P, EC + 2])
        b_router = sb("b_router", [NB, NE])
        g_row = sb("g_row", [NB, 2, 2, D])
        o_row = sb("o_row", [NB, 3, 2, D])
        tab0 = sb("tab0", [P, NB, EC + 2])
        tab = [sb(f"tab{i}", [P, NB, 8]) for i in (1, 2, 3)]
        tr0 = sb("tr0", [NB, NE])
        tr = [sb(f"tr{i}", [NB, 4, D]) for i in (1, 2, 3)]
        ps = [stack.enter_context(nc.psum_tensor(f"t_ps{i}", [P, 512], F32)) for i in range(8)]
        sem = lambda n: stack.enter_context(nc.semaphore(n))
        s_cond, s_in, s_idm, s_id = sem("t_cond"), sem("t_in"), sem("t_idm"), sem("t_id")
        s_silu, s_T, s_cT, s_mm = sem("t_silu"), sem("t_T"), sem("t_cT"), sem("t_mm")
        s_dve, s_out = sem("t_dve"), sem("t_out")
        loads = []

        def load(dst, src):
            loads.append((dst, src))

        W1, W2, G0 = t["L1_xcond_W_mod"], t["L2_xcond_adaln_w"], t["L0_xcond_gate_w1"]
        load(w_mod[0][:, :, :], chunks(W1))
        load(w_mod[1][:, :, :], chunks(W2))
        load(w_aff[0][:, :, :], chunks(t["L3_xcond_aff1_w"]))
        load(w_aff[1][:, :, :], chunks(t["L3_xcond_aff2_w"]))
        for e in range(NE):
            for k in range(CC):
                load(w_anchor[:, k, 4 * e:4 * e + 4, :].rearrange("p m n -> p (m n)"),
                     t["L0_xcond_e_w1"][e, 2 * D + k * P:2 * D + (k + 1) * P, :])
        for k in range(CC):
            load(w_anchor[:, k, EC:EC + 2, :].rearrange("p m n -> p (m n)"), G0[2 * D + k * P:2 * D + (k + 1) * P, :])
        load(w_router[:, :, :], chunks(t["L0_xcond_router_W"][2 * D:3 * D, :]))
        for i, b in enumerate((t["L1_xcond_b_mod"], t["L2_xcond_adaln_b"])):
            load(b_mod[:, i, :], column(b))
            for j, at in enumerate((2 * D, 5 * D)):
                load(g_row[:, i, j, :], spread(b[at:at + D], NB))
        for i in range(2):
            load(b_aff[:, i, :], column(t[f"L3_xcond_aff{i + 1}_b"]))
            load(ln_gb[:, i, 0:2], column(t[f"L3_xcond_ln{i + 1}_g"]))
            load(ln_gb[:, i, 2:4], column(t[f"L3_xcond_ln{i + 1}_b"]))
        load(b_anchor[:, 0:EC], t["L0_xcond_e_b1"].rearrange("e (k p) -> p (e k)", p=P))
        load(b_anchor[:, EC:EC + 2], column(t["L0_xcond_gate_b1"]))
        load(b_router[:, :], spread(t["L0_xcond_router_b"], NB))
        for i, (a, m) in enumerate((("L1_xcond_b_proj", "L1_xcond_b_mlp2"), ("L2_xcond_sa_proj_b", "L2_xcond_fc2_b"),
                                    ("L3_xcond_sa_ob", "L3_xcond_ffn_b2"))):
            load(o_row[:, i, 0, :], spread(t[a], NB))
            load(o_row[:, i, 1, :], spread(t[m], NB))
        ALL = 16 * len(loads)

        block = stack.enter_context(nc.Block())

        @block.sync
        def _(eng):
            eng.dma_start(cond[:, :], t["cond_1024"]).then_inc(s_cond, 16)
            for dst, src in loads:
                eng.dma_start(dst, src).then_inc(s_in, 16)
            eng.wait_ge(s_dve, DVE_DONE)
            outs = [(cols[0], tab0[:, :, :].rearrange("p b m -> p (b m)")), (rows[0], tr0[:, :])]
            for i in range(3):
                outs.append((cols[i + 1], tab[i][:, :, :].rearrange("p b m -> p (b m)")))
                outs.append((rows[i + 1], tr[i][:, :, :].rearrange("b g f -> b (g f)")))
            for dst, src in outs:
                eng.dma_start(dst, src).then_inc(s_out, 16)
            eng.wait_ge(s_out, 16 * len(outs))

        @block.gpsimd
        def _(eng):
            eng.memset(half[:, :], -0.5)
            eng.memset(eps5[:, :], 1e-5)
            eng.memset(eps6[:, :], 1e-6)
            eng.memset(ident[:, :], 0.0).then_inc(s_idm, 1)
            eng.wait_ge(s_idm, 1)
            eng.affine_select(out=ident[:, :], in_=ident[:, :], compare_op=ALU.not_equal, fill=1.0,
                              base=0, pattern=[[-1, P]], channel_multiplier=1).then_inc(s_id, 1)

        @block.scalar
        def _(eng):
            eng.wait_ge(s_cond, 16)
            eng.activation(cond_silu[:, :], cond[:, :], ACT.Silu).then_inc(s_silu, 1)

        @block.tensor
        def _(eng):
            eng.wait_ge(s_id, 1)
            eng.wait_ge(s_cond, 16)
            for c in range(CC):
                eng.transpose(ps[0][:, c * NB:(c + 1) * NB], cond[:, c * P:(c + 1) * P], ident[0:NB, 0:NB])
            eng.wait_ge(s_silu, 1)
            for c in range(CC):
                mm = eng.transpose(ps[0][:, (CC + c) * NB:(CC + c + 1) * NB], cond_silu[:, c * P:(c + 1) * P],
                                   ident[0:NB, 0:NB])
            mm.then_inc(s_T, 1)
            eng.wait_ge(s_cT, 1)
            eng.wait_ge(s_in, ALL)

            def columns(out, lhs, m, rhs):
                for k in range(CC):
                    mm = eng.matmul(out, lhs(k, m), rhs[:, k, :], start=(k == 0), stop=(k == CC - 1))
                return mm

            for m in range(EC + 2):
                columns(ps[1][:, m * NB:(m + 1) * NB], lambda k, m: w_anchor[:, k, m, :], m, condT)
            for i in range(2):
                for j, m in enumerate((0, 1, 2, 3, 6, 7, 8, 9)):
                    columns(ps[2][:, (8 * i + j) * NB:(8 * i + j + 1) * NB],
                            lambda k, m: w_mod[i][:, k, m * P:(m + 1) * P], m, cond_siluT)
                for j in range(4):
                    columns(ps[3][:, (4 * i + j) * NB:(4 * i + j + 1) * NB],
                            lambda k, m: w_aff[i][:, k, m * P:(m + 1) * P], j, condT)
                for j, at in enumerate((2 * D, 5 * D)):
                    for k in range(CC):
                        eng.matmul(ps[4 + i][0:NB, j * D:(j + 1) * D], cond_siluT[:, k, :],
                                   w_mod[i][:, k, at:at + D], start=(k == 0), stop=(k == CC - 1))
            for k in range(CC):
                mm = eng.matmul(ps[6][0:NB, 0:NE], condT[:, k, :], w_router[:, k, :],
                                start=(k == 0), stop=(k == CC - 1))
            mm.then_inc(s_mm, 1)

        dve_marks = [0]

        @block.vector
        def _(eng):
            def done(ins, wait=True):
                ins.then_inc(s_dve, 1)
                dve_marks[0] += 1
                if wait:
                    eng.wait_ge(s_dve, dve_marks[0])

            eng.wait_ge(s_T, 1)
            eng.tensor_copy(condT[:, :, :], ps[0][:, 0:CC * NB].rearrange("p (c b) -> p c b", b=NB))
            eng.tensor_copy(cond_siluT[:, :, :],
                            ps[0][:, CC * NB:2 * CC * NB].rearrange("p (c b) -> p c b", b=NB)).then_inc(s_cT, 1)
            eng.wait_ge(s_in, ALL)
            eng.wait_ge(s_mm, 1)

            def flip(tile, a, b):
                return tile[:, :, a:b].rearrange("p b m -> p m b")

            def over_b(cols_):
                return cols_.unsqueeze(2).to_broadcast([P, cols_.shape[1], NB])

            def ps_cols(i, a, b):
                return ps[i][:, a * NB:b * NB].rearrange("p (m b) -> p m b", b=NB)

            done(eng.tensor_tensor(flip(tab0, 0, EC + 2), ps_cols(1, 0, EC + 2), over_b(b_anchor[:, :]), ALU.add))
            done(eng.tensor_tensor(tr0[:, :], ps[6][0:NB, 0:NE], b_router[:, :], ALU.add))
            for i in range(2):
                done(eng.tensor_tensor(flip(tab[i], 0, 4), ps_cols(2, 8 * i, 8 * i + 4),
                                       over_b(b_mod[:, i, 0:4]), ALU.add))
                done(eng.tensor_tensor(flip(tab[i], 4, 8), ps_cols(2, 8 * i + 4, 8 * i + 8),
                                       over_b(b_mod[:, i, 6:10]), ALU.add))
                for a in (2, 6):
                    done(eng.tensor_scalar(tab[i][:, :, a:a + 2], tab[i][:, :, a:a + 2], 1.0, None, ALU.add))
                for j in range(2):
                    done(eng.tensor_tensor(tr[i][:, 2 * j, :], ps[4 + i][0:NB, j * D:(j + 1) * D],
                                           g_row[:, i, j, :], ALU.add))
                    done(eng.tensor_tensor(tr[i][:, 2 * j + 1, :], tr[i][:, 2 * j, :], o_row[:, i, j, :], ALU.mult))
            for j in range(2):
                at = 4 * j
                done(eng.tensor_tensor(flip(tab[2], at + 2, at + 4), ps_cols(3, at, at + 2),
                                       over_b(b_aff[:, j, 0:2]), ALU.add))
                done(eng.tensor_tensor(flip(tab[2], at, at + 2), flip(tab[2], at + 2, at + 4),
                                       over_b(ln_gb[:, j, 2:4]), ALU.mult))
                done(eng.tensor_tensor(flip(tab[2], at, at + 2), flip(tab[2], at, at + 2),
                                       over_b(b_aff[:, j, 2:4]), ALU.add))
                done(eng.tensor_tensor(flip(tab[2], at, at + 2), ps_cols(3, at + 2, at + 4),
                                       flip(tab[2], at, at + 2), ALU.add))
                done(eng.tensor_tensor(flip(tab[2], at + 2, at + 4), flip(tab[2], at + 2, at + 4),
                                       over_b(ln_gb[:, j, 0:2]), ALU.mult))
                done(eng.memset(tr[2][:, 2 * j, :], 1.0))
                done(eng.tensor_copy(tr[2][:, 2 * j + 1, :], o_row[:, 2, j, :]))
            assert dve_marks[0] == DVE_DONE


DVE_DONE = 2 + 2 * (4 + 4) + 2 * 7


def norm_ops(pl, ph, pre, x, st, mv, rstd, eps, half, out, parts, after, wait_out, group=None, first=()):
    from concourse import mybir
    ALU = mybir.AluOpType
    n, tiles = parts
    G = dict(group=group)
    for i in range(tiles):
        pl.op("dve", ph, lambda e, s, i=i: e.bn_stats(st[0:n, i, :], x[0:n, i, :]),
              after=(list(after) + [f"{ph}.{pre}rstd@-1"] * 0 if i == 0 else []), mark=f"{pre}st{i}", **G)
    for i in range(tiles):
        pl.op("dve", ph, lambda e, s, i=i: e.bn_aggr(mv[0:n, i, :], st[0:n, i, :]),
              after=[f"{ph}.{pre}st{i}"] + ([f"{ph}.{pre}ve@-1"] if i == 0 else []),
              mark=f"{pre}mv{i}", alone=True, **G)
    pl.op("pool", ph, lambda e, s: e.tensor_tensor(rstd[0:n, 0:tiles], mv[0:n, 0:tiles, 1], eps[0:n, 0:tiles], ALU.add),
          after=[f"{ph}.{pre}mv{tiles - 1}", f"{ph}.{pre}xn{tiles - 1}@-1"], mark=f"{pre}ve", **G)
    pl.op("pool", ph, lambda e, s: e.tensor_tensor(rstd[0:n, 0:tiles], rstd[0:n, 0:tiles], half[0:n, 0:tiles], ALU.pow),
          after=[f"{ph}.{pre}ve"], mark=f"{pre}rstd", **G)
    for i in range(tiles):
        pl.op("dve", ph, lambda e, s, i=i: e.tensor_scalar(out[0:n, i, :], x[0:n, i, :], mv[0:n, i, 0:1],
                                                          rstd[0:n, i:i + 1], ALU.subtract, ALU.mult),
              after=([f"{ph}.{pre}rstd"] + list(wait_out)) if i == 0 else [], mark=f"{pre}xn{i}", **G)


def mixture(nc, t, x_out, cols0, rows0, ident, half, eps5, chunks, column, spread, by_tile, buffers, prefetch):
    from concourse import mybir
    from contextlib import ExitStack
    F32 = mybir.dt.float32
    ALU, ACT, AX = mybir.AluOpType, mybir.ActivationFunctionType, mybir.AxisListType
    g = lambda k: t["L0_xcond_" + k]

    with ExitStack() as stack:
        sb = buffers(stack)
        wq, wk, wv = (sb(f"m_{k}", [P, CC, D]) for k in ("wq", "wk", "wv"))
        rw = sb("m_rw", [P, 4, NE])
        w1 = sb("m_w1", [P, 4, EC, P])
        w2 = sb("m_w2", [P, EC, D])
        g1 = sb("m_g1", [P, 4, D])
        g2 = sb("m_g2", [P, CC, D])
        wo = sb("m_wo", [P, CC, D])
        lng = sb("m_lng", [P, 4])
        b2 = sb("m_b2", [P, NE, D])
        bg2 = sb("m_bg2", [P, D])
        bo = sb("m_bo", [P, D])
        x, xn, nx = sb("m_x", [P, TT, D]), sb("m_xn", [P, TT, D]), sb("m_nx", [P, CC, NT])
        st, mv, rstd = sb("m_st", [P, TT, 6]), sb("m_mv", [P, TT, 2]), sb("m_rstd", [P, TT])
        ctx, ctxT = sb("m_ctx", [NC_TOK, D]), sb("m_ctxT", [P, CC, NC_TOK])
        qT, kT, v = sb("m_qT", [P, CC, NT]), sb("m_kT", [P, CC, NC_TOK]), sb("m_v", [NC_TOK, D])
        mx, sm, rs = sb("m_mx", [P, TT]), sb("m_sm", [P, TT]), sb("m_rs", [P, TT])
        wgt, wgtT = sb("m_wgt", [P, TT, NC_TOK]), sb("m_wgtT", [NC_TOK, NT])
        ar, lg = sb("m_ar", [P, NE]), sb("m_lg", [P, TT, NE])
        rmx, rsm, rrs = sb("m_rmx", [P, TT]), sb("m_rsm", [P, TT]), sb("m_rrs", [P, TT])
        rex, prob = sb("m_rex", [P, TT, NE]), sb("m_prob", [P, TT, NE])
        evT = sb("m_evT", [P, CC, NT])
        comb = sb("m_comb", [P, 4, NT])
        xg = sb("m_xg", [P, TT, D])
        acol = sb("m_acol", [P, EC + 2])
        h = sb("m_h", [P, EC, NT])
        gT = sb("m_gT", [P, CC, NT])
        gp, th = sb("m_gp", [P, TT, D]), sb("m_th", [P, TT, D])
        r, rT = sb("m_r", [P, TT, D]), sb("m_rT", [P, CC, NT])
        y = sb("m_y", [P, TT, D])
        ps = [stack.enter_context(nc.psum_tensor(f"m_ps{i}", [P, 2, 256], F32)) for i in range(8)]
        banks = [Bank(p) for p in ps]
        fb, hb, eb, gb = banks[0:2], banks[2:5], banks[5:7], banks[7]
        s_w0 = stack.enter_context(nc.semaphore("m_weights"))
        loads = [(wq, g("Wq")), (wk, g("Wk")), (wv, g("Wv"))]
        loads = [(d[:, :, :], chunks(s_)) for d, s_ in loads]
        loads.append((lng[:, 0:2], column(g("ln_gamma"))))
        loads.append((lng[:, 2:4], column(g("ln_beta"))))
        loads.append((rw[:, :, :], chunks(g("router_W")[0:2 * D, :])))
        for e in range(NE):
            for k in range(4):
                loads.append((w1[:, k, 4 * e:4 * e + 4, :].rearrange("p m n -> p (m n)"),
                              g("e_w1")[e, k * P:(k + 1) * P, :]))
        loads.append((g1[:, :, :], chunks(g("gate_w1")[0:2 * D, :])))
        for e in range(NE):
            loads.append((w2[:, 4 * e:4 * e + 4, :], chunks(g("e_w2")[e, :, :])))
            loads.append((b2[:, e, :], spread(g("e_b2")[e, :])))
        loads.append((g2[:, :, :], chunks(g("gate_w2"))))
        loads.append((wo[:, :, :], chunks(g("out_w"))))
        loads.append((bg2[:, :], spread(g("gate_b2"))))
        loads.append((bo[:, :], spread(g("out_b"))))

        pl = Pipeline(nc, "m", dict(F=0, G=1), NB, stack)
        pl.shared = banks
        op, take, empties = pl.op, pl.take, pl.empties

        def f_load():
            op("sp", "F", lambda e, s: e.dma_start(x[:, :, :], by_tile(t["x"][s, :, :])),
               after=["F.xcopy@-1"], mark="x", dma=1)
            op("sp", "F", lambda e, s: e.dma_start(ctx[:, :], t["ctx_1024"][s, :, :]),
               after=["F.ctxt@-1"], mark="ctx", dma=1)
            op("sp", "F", lambda e, s: e.dma_start(ar[:, :], rows0[s, :].unsqueeze(0).to_broadcast([P, NE])),
               after=["F.lg@-1"], mark="ar", dma=1)

        def f_norm():
            norm_ops(pl, "F", "", x, st, mv, rstd, eps5, half, xn, (P, TT), ["F.x"], ["F.xt@-1"])

        def f_transpose():
            b = fb[0]
            for tt in range(TT):
                for c in range(CC):
                    op("pe", "F", lambda e, s, tt=tt, c=c: e.transpose(
                        b.ap[:, c, tt * P:(tt + 1) * P], xn[:, tt, c * P:(c + 1) * P], ident[:, :]),
                       after=(["F.xn1"] + take(b, "F")) if tt + c == 0 else [],
                       mark="xt" if tt + c == 2 else None)
            for c in range(CC):
                op("dve", "F", lambda e, s, c=c: e.tensor_scalar(nx[:, c, :], b.ap[:, c, :], lng[:, c:c + 1],
                                                                lng[:, 2 + c:3 + c], ALU.mult, ALU.add),
                   after=["F.xt", "F.nxcopy@-1", "F.q@-1", "F.lgp@-1"] if c == 0 else [], mark=f"nx{c}")
            empties(b, "F", "nx1")
            b2_ = fb[1]
            for c in range(CC):
                op("pe", "F", lambda e, s, c=c: e.transpose(b2_.ap[:, 0, c * NC_TOK:(c + 1) * NC_TOK],
                                                           ctx[:, c * P:(c + 1) * P], ident[0:NC_TOK, 0:NC_TOK]),
                   after=(["F.ctx"] + take(b2_, "F")) if c == 0 else [], mark="ctxt" if c else None)
            op("act", "F", lambda e, s: e.activation(
                ctxT[:, :, :], b2_.ap[:, 0, 0:CC * NC_TOK].rearrange("p (c k) -> p c k", c=CC), ACT.Copy),
               after=["F.ctxt", "F.v@-1"], mark="ctxT")
            empties(b2_, "F", "ctxT")

        def f_qkv():
            b = fb[0]
            for m in range(CC):
                for k in range(CC):
                    op("pe", "F", lambda e, s, m=m, k=k: e.matmul(b.ap[:, m, :], wq[:, k, m * P:(m + 1) * P],
                                                                 nx[:, k, :], start=(k == 0), stop=(k == CC - 1)),
                       after=(["F.nx1"] + take(b, "F")) if m + k == 0 else [], mark="q" if m + k == 2 else None)
            op("act", "F", lambda e, s: e.activation(qT[:, :, :], b.ap[:, :, :], ACT.Copy),
               after=["F.q", "F.sc@-1"], mark="qT")
            empties(b, "F", "qT")
            b2_ = fb[1]
            first = take(b2_, "F")
            for m in range(CC):
                for k in range(CC):
                    op("pe", "F", lambda e, s, m=m, k=k: e.matmul(
                        b2_.ap[:, 0, m * NC_TOK:(m + 1) * NC_TOK], wk[:, k, m * P:(m + 1) * P], ctxT[:, k, :],
                        start=(k == 0), stop=(k == CC - 1)),
                       after=(["F.ctxT"] + first) if m + k == 0 else [])
            for k in range(CC):
                op("pe", "F", lambda e, s, k=k: e.matmul(b2_.ap[0:NC_TOK, 1, :], ctxT[:, k, :], wv[:, k, :],
                                                        start=(k == 0), stop=(k == CC - 1)),
                   mark="v" if k else None)
            op("act", "F", lambda e, s: e.activation(
                kT[:, :, :], b2_.ap[:, 0, 0:CC * NC_TOK].rearrange("p (c k) -> p c k", c=CC), ACT.Copy),
               after=["F.v", "F.sc@-1"], mark="kT")
            op("act", "F", lambda e, s: e.activation(v[:, :], b2_.ap[0:NC_TOK, 1, :], ACT.Copy),
               after=["F.ev@-1"], mark="vS")
            empties(b2_, "F", "vS")

        def f_scores():
            b = fb[0]
            for tt in range(TT):
                for k in range(CC):
                    op("pe", "F", lambda e, s, tt=tt, k=k: e.matmul(
                        b.ap[:, 0, tt * P:tt * P + NC_TOK], qT[:, k, tt * P:(tt + 1) * P], kT[:, k, :],
                        start=(k == 0), stop=(k == CC - 1)),
                       after=(["F.qT", "F.kT"] + take(b, "F")) if tt + k == 0 else [],
                       mark="sc" if tt + k == 2 else None)
            view = b.ap[:, 0, :].rearrange("p (t k) -> p t k", t=TT)[:, :, 0:NC_TOK]
            op("dve", "F", lambda e, s: e.tensor_reduce(mx[:, :], view, AX.X, ALU.max, negate=True),
               after=["F.sc"] , mark="mx0")
            op("dve", "F", lambda e, s: e.tensor_scalar(mx[:, :], mx[:, :], D ** -0.5, None, ALU.mult),
               after=["F.mx0", "F.exp1@-1"], mark="mx")
            for tt in range(TT):
                op("act", "F", lambda e, s, tt=tt: e.activation(
                    wgt[:, tt, :], b.ap[:, 0, tt * P:tt * P + NC_TOK], ACT.Exp, bias=mx[:, tt:tt + 1],
                    scale=D ** -0.5, accum_out=sm[:, tt:tt + 1]),
                   after=["F.mx", "F.wn1@-1", "F.rs@-1", "F.wt@-1"] if tt == 0 else [], mark=f"exp{tt}")
            empties(b, "F", "exp1")
            op("dve", "F", lambda e, s: e.reciprocal(rs[:, :], sm[:, :]), after=["F.exp1", "F.wn1@-1"], mark="rs")
            for tt in range(TT):
                op("dve", "F", lambda e, s, tt=tt: e.tensor_scalar(wgt[:, tt, :], wgt[:, tt, :], rs[:, tt:tt + 1],
                                                                  None, ALU.mult),
                   after=["F.rs"] if tt == 0 else [], mark=f"wn{tt}")

        def f_evidence():
            b = fb[1]
            for tt in range(TT):
                op("pe", "F", lambda e, s, tt=tt: e.transpose(b.ap[0:NC_TOK, 0, tt * P:(tt + 1) * P], wgt[:, tt, :],
                                                             ident[:, :]),
                   after=(["F.wn1"] + take(b, "F")) if tt == 0 else [], mark="wt" if tt else None)
            op("act", "F", lambda e, s: e.activation(wgtT[:, :], b.ap[0:NC_TOK, 0, :], ACT.Copy),
               after=["F.wt", "F.ev@-1"], mark="wgtT")
            empties(b, "F", "wgtT")
            b2_ = fb[0]
            for m in range(CC):
                op("pe", "F", lambda e, s, m=m: e.matmul(b2_.ap[:, m, :], v[:, m * P:(m + 1) * P], wgtT[:, :],
                                                        start=True, stop=True),
                   after=(["F.wgtT", "F.vS"] + take(b2_, "F")) if m == 0 else [], mark="ev" if m else None)
            op("act", "F", lambda e, s: e.activation(evT[:, :, :], b2_.ap[:, :, :], ACT.Copy),
               after=["F.ev", "F.evcopy@-1", "F.lgp@-1"], mark="evT")
            empties(b2_, "F", "evT")

        def f_router():
            b = fb[1]
            for tt in range(TT):
                for k in range(4):
                    src = (nx, evT)[k // CC]
                    op("pe", "F", lambda e, s, tt=tt, k=k, src=src: e.matmul(
                        b.ap[:, 0, tt * NE:(tt + 1) * NE], src[:, k % CC, tt * P:(tt + 1) * P], rw[:, k, :],
                        start=(k == 0), stop=(k == 3)),
                       after=(["F.evT", "F.nx1"] + take(b, "F")) if tt + k == 0 else [],
                       mark="lgp" if tt + k == 4 else None)
            op("dve", "F", lambda e, s: e.tensor_tensor(
                lg[:, :, :], b.ap[:, 0, 0:TT * NE].rearrange("p (t e) -> p t e", t=TT),
                ar[:, :].unsqueeze(1).to_broadcast([P, TT, NE]), ALU.add),
               after=["F.lgp", "F.ar", "F.rexp1@-1"], mark="lg")
            empties(b, "F", "lg")
            op("dve", "F", lambda e, s: e.tensor_reduce(rmx[:, :], lg[:, :, :], AX.X, ALU.max, negate=True),
               after=["F.lg"], mark="rmx")
            for tt in range(TT):
                op("act", "F", lambda e, s, tt=tt: e.activation(rex[:, tt, :], lg[:, tt, :], ACT.Exp,
                                                               bias=rmx[:, tt:tt + 1],
                                                               accum_out=rsm[:, tt:tt + 1]),
                   after=["F.rmx", "F.prob1@-1"] if tt == 0 else [], mark=f"rexp{tt}")
            op("dve", "F", lambda e, s: e.reciprocal(rrs[:, :], rsm[:, :]), after=["F.rexp1"], mark="rrs")

        def f_hand_over():
            for tt in range(TT):
                op("dve", "F", lambda e, s, tt=tt: e.tensor_scalar(prob[:, tt, :], rex[:, tt, :], rrs[:, tt:tt + 1],
                                                                  None, ALU.mult),
                   after=["F.rrs", "G.r_last@-1"] if tt == 0 else [], mark=f"prob{tt}")
            op("act", "F", lambda e, s: e.activation(comb[:, 0:2, :], nx[:, :, :], ACT.Copy),
               after=["F.nx1", "G.g1p@-1"], mark="nxcopy")
            op("act", "F", lambda e, s: e.activation(comb[:, 2:4, :], evT[:, :, :], ACT.Copy),
               after=["F.evT"], mark="evcopy")
            op("act", "F", lambda e, s: e.activation(xg[:, :, :], x[:, :, :], ACT.Copy),
               after=["F.x", "G.y3@-1"], mark="xcopy")

        def g_load():
            op("sp", "G", lambda e, s: e.dma_start(
                acol[:, :], cols0.rearrange("p (b m) -> b p m", b=NB)[s, :, :]),
               after=["G.g1s1@-1", f"G.h{EC - 1}@-1"], mark="acol", dma=1)

        def g_h(i):
            b = hb[i % 3]
            for m2 in range(2):
                m = 2 * i + m2
                for k in range(4):
                    op("pe", "G", lambda e, s, m=m, m2=m2, k=k: e.matmul(
                        b.ap[:, m2, :], w1[:, k, m, :], comb[:, k, :], start=(k == 0), stop=(k == 3)),
                       after=(["F.nxcopy", "F.evcopy"] + take(b, "G")) if m2 + k == 0 else [],
                       mark=f"hp{i}" if m2 * 4 + k == 7 else None)
            for m2 in range(2):
                m = 2 * i + m2
                op("act", "G", lambda e, s, m=m, m2=m2: e.activation(h[:, m, :], b.ap[:, m2, :], ACT.Silu,
                                                                    bias=acol[:, m:m + 1]),
                   after=[f"G.hp{i}", "G.acol", f"G.ep{m // 4}@-1"] if m2 == 0 else [], mark=f"h{m}")
            empties(b, "G", f"h{2 * i + 1}")

        def g_e2(ex):
            b = eb[ex % 2]
            for tt in range(TT):
                for k in range(4):
                    op("pe", "G", lambda e, s, tt=tt, k=k: e.matmul(
                        b.ap[:, tt, :], h[:, 4 * ex + k, tt * P:(tt + 1) * P], w2[:, 4 * ex + k, :],
                        start=(k == 0), stop=(k == 3)),
                       after=([f"G.h{4 * ex + 3}"] + take(b, "G")) if tt + k == 0 else [],
                       mark=f"ep{ex}" if tt * 4 + k == 7 else None)
            for tt in range(TT):
                sc = lambda tt=tt: prob[:, tt, ex:ex + 1]
                last = "r_last" if ex == NE - 1 and tt == TT - 1 else f"r{ex}{tt}"
                if ex == 0:
                    op("dve", "G", lambda e, s, tt=tt: e.tensor_scalar(r[:, tt, :], b.ap[:, tt, :],
                                                                      prob[:, tt, 0:1], None, ALU.mult),
                       after=["G.ep0", "F.prob1", "G.rt@-1"], mark=f"r{ex}{tt}")
                else:
                    op("dve", "G", lambda e, s, tt=tt: e.scalar_tensor_tensor(
                        r[:, tt, :], b.ap[:, tt, :], prob[:, tt, ex:ex + 1], r[:, tt, :], ALU.mult, ALU.add),
                       after=[f"G.ep{ex}", f"G.b{ex - 1}{tt}"], mark=f"r{ex}{tt}")
                bl = "r_last" if ex == NE - 1 and tt == TT - 1 else f"b{ex}{tt}"
                op("dve", "G", lambda e, s, tt=tt: e.scalar_tensor_tensor(
                    r[:, tt, :], b2[:, ex, :], prob[:, tt, ex:ex + 1], r[:, tt, :], ALU.mult, ALU.add),
                   after=[f"G.r{ex}{tt}"], mark=bl)
            empties(b, "G", f"r{ex}1")

        def g_gate1():
            b = gb
            for m in range(CC):
                for k in range(4):
                    op("pe", "G", lambda e, s, m=m, k=k: e.matmul(b.ap[:, m, :], g1[:, k, m * P:(m + 1) * P],
                                                                 comb[:, k, :], start=(k == 0), stop=(k == 3)),
                       after=(["F.nxcopy", "F.evcopy"] + take(b, "G")) if m + k == 0 else [],
                       mark="g1p" if m * 4 + k == 7 else None)
            for m in range(CC):
                op("act", "G", lambda e, s, m=m: e.activation(gT[:, m, :], b.ap[:, m, :], ACT.Silu,
                                                             bias=acol[:, EC + m:EC + m + 1]),
                   after=["G.g1p", "G.acol", "G.g2p@-1"] if m == 0 else [], mark=f"g1s{m}")
            empties(b, "G", "g1s1")

        def g_gate2():
            b = gb
            for tt in range(TT):
                for k in range(CC):
                    op("pe", "G", lambda e, s, tt=tt, k=k: e.matmul(b.ap[:, tt, :], gT[:, k, tt * P:(tt + 1) * P],
                                                                   g2[:, k, :], start=(k == 0), stop=(k == 1)),
                       after=(["G.g1s1"] + take(b, "G")) if tt + k == 0 else [],
                       mark="g2p" if tt + k == 2 else None)
            op("dve", "G", lambda e, s: e.tensor_tensor(gp[:, :, :], b.ap[:, :, :],
                                                       bg2[:, :].unsqueeze(1).to_broadcast([P, TT, D]), ALU.add),
               after=["G.g2p", "G.th@-1"], mark="gp")
            empties(b, "G", "gp")
            op("act", "G", lambda e, s: e.activation(th[:, :, :], gp[:, :, :], ACT.Tanh, scale=0.5),
               after=["G.gp", "G.y2@-1"], mark="th")
            op("dve", "G", lambda e, s: e.tensor_scalar(th[:, :, :], th[:, :, :], 0.5, 0.5, ALU.mult, ALU.add),
               after=["G.th"], mark="gate")

        def g_out():
            b = gb
            for tt in range(TT):
                for c in range(CC):
                    op("pe", "G", lambda e, s, tt=tt, c=c: e.transpose(
                        b.ap[:, c, tt * P:(tt + 1) * P], r[:, tt, c * P:(c + 1) * P], ident[:, :]),
                       after=(["G.r_last", f"G.b{NE - 1}0"] + take(b, "G")) if tt + c == 0 else [],
                       mark="rt" if tt + c == 2 else None)
            op("act", "G", lambda e, s: e.activation(rT[:, :, :], b.ap[:, :, :], ACT.Copy),
               after=["G.rt", "G.yp@-1"], mark="rT")
            empties(b, "G", "rT")
            b2_ = eb[1]
            for tt in range(TT):
                for k in range(CC):
                    op("pe", "G", lambda e, s, tt=tt, k=k: e.matmul(b2_.ap[:, tt, :], rT[:, k, tt * P:(tt + 1) * P],
                                                                   wo[:, k, :], start=(k == 0), stop=(k == 1)),
                       after=(["G.rT"] + take(b2_, "G")) if tt + k == 0 else [],
                       mark="yp" if tt + k == 2 else None)
            op("dve", "G", lambda e, s: e.tensor_tensor(y[:, :, :], b2_.ap[:, :, :],
                                                       bo[:, :].unsqueeze(1).to_broadcast([P, TT, D]), ALU.add),
               after=["G.yp", "G.store@-1"], mark="y1")
            empties(b2_, "G", "y1")
            op("dve", "G", lambda e, s: e.tensor_tensor(y[:, :, :], y[:, :, :], th[:, :, :], ALU.mult),
               after=["G.y1", "G.gate"], mark="y2")
            op("dve", "G", lambda e, s: e.tensor_tensor(y[:, :, :], y[:, :, :], xg[:, :, :], ALU.add),
               after=["G.y2", "F.xcopy"], mark="y3")
            op("sp", "G", lambda e, s: e.dma_start(by_tile(x_out[s, :, :]), y[:, :, :]),
               after=["G.y3"], mark="store", dma=1)

        def iteration(n, hi, active):
            pl.iteration = n
            pl.begin(active)
            f_load()
            g_load()
            g_h(0)
            f_norm()
            g_h(1)
            f_transpose()
            g_e2(0)
            f_qkv()
            g_h(2)
            f_scores()
            g_h(3)
            g_e2(1)
            f_evidence()
            g_gate1()
            f_router()
            g_h(4)
            g_h(5)
            g_gate2()
            g_e2(2)
            g_out()
            f_hand_over()
            pl.end(n, hi)

        iteration(0, 1, "F")
        iteration(1, 2, "FG")
        iteration(2, NB, "FG")
        iteration(NB, NB + 1, "G")

        block = stack.enter_context(nc.Block())

        @block.sync
        def _(eng):
            for dst, src in loads:
                eng.dma_start(dst, src).then_inc(s_w0, 16)
            prefetch(eng)
            pl.emit("sp", eng)
            eng.wait_ge(pl.sem("G.store"), 16 * NB)

        @block.gpsimd
        def _(eng):
            pl.emit("pool", eng)

        @block.scalar
        def _(eng):
            pl.emit("act", eng)

        @block.vector
        def _(eng):
            eng.wait_ge(s_w0, 16 * len(loads))
            pl.emit("dve", eng)

        @block.tensor
        def _(eng):
            eng.wait_ge(s_w0, 16 * len(loads))
            pl.emit("pe", eng)


def blocks(nc, t, xs, cols, rows, ident, half, eps5, eps6, WT, s_w, n_w, load_layer, by_tile, buffers):
    from concourse import mybir
    from contextlib import ExitStack
    from itertools import islice
    F32, F32R = mybir.dt.float32, mybir.dt.float32r
    BF16, F16 = mybir.dt.bfloat16, mybir.dt.float16
    ALU, ACT, AX = mybir.AluOpType, mybir.ActivationFunctionType, mybir.AxisListType
    LAYERS, SCALE = (1, 2, 3), HD ** -0.5

    with ExitStack() as stack:
        sb = buffers(stack)
        tile = lambda n: sb(n, [P, 2, 256])

        def stats(n):
            return sb(n + "_st", [P, TT, 6]), sb(n + "_mv", [P, TT, 2]), sb(n + "_rstd", [P, TT])

        x_in, xn_a, xT_a, x_res, res_a = (tile(n) for n in ("x_in", "xn_a", "xT_a", "x_res", "res_a"))
        st_p, st_t, st_k, st_b = stats("p"), stats("t"), stats("k"), stats("b")
        col_a, bias_a, gate_a = sb("col_a", [P, 4]), sb("bias_a", [P, D]), sb("gate_a", [P, D])
        q_hl, k_hl = sb("q_hl", [P, 2, CC, NT], F32R), sb("k_hl", [P, 2, CC, NT], F32R)
        v_f = tile("v_f")
        v_cat = sb("v_cat", [P, TT, NH, VC], BF16)
        q_cat = sb("q_cat", [P, NPAIR, NT], F32R)
        k_cat = sb("k_cat", [P, NPAIR, NT], F32R)
        m_a, mT_a = sb("m_a", [P, TT, NH]), sb("mT_a", [NH, 2, NT], F32R)
        o_sum, o_rc, o_a, oT_a = sb("o_sum", [P, TT, 8, VW]), sb("o_rc", [P, TT, 8]), tile("o_a"), tile("oT_a")
        y_a, x_b = tile("y_a"), tile("x_b")
        p_f = [sb(f"p_f{i}", [P, 1024]) for i in range(2)]
        p_h = [sb(f"p_h{i}", [P, 1024], F16) for i in range(2)]
        p_l = [sb(f"p_l{i}", [P, 1024], F16) for i in range(2)]
        xn_b, xT_b, res_b = tile("xn_b"), tile("xT_b"), tile("res_b")
        ctx, ctxn, ctxT = sb("ctx", [NC_TOK, 1, D]), sb("ctxn", [NC_TOK, 1, D]), sb("ctxT", [P, CC, NC_TOK])
        qc_hl, kc_hl = sb("qc_hl", [P, 2, CC, NT], F32R), sb("kc_hl", [P, 2, CC, NC_TOK], F32R)
        vc_f = sb("vc_f", [NC_TOK, D])
        vc_cat = sb("vc_cat", [NC_TOK, NH, VC], BF16)
        qc_cat = sb("qc_cat", [P, NPAIR, NT], F32R)
        kc_cat = sb("kc_cat", [P, NPAIR, CPAD], F32R)
        m_b, mT_b = sb("m_b", [P, TT, NH]), sb("mT_b", [NH, 2, NT], F32R)
        o_b, oT_b, x_c = tile("o_b"), tile("oT_b"), tile("x_c")
        xn_c, xT_c, res_c = tile("xn_c"), tile("xT_c"), tile("res_c")
        col_c, bias_c, gate_c = sb("col_c", [P, 4]), sb("bias_c", [P, D]), sb("gate_c", [P, D])
        h_c, y_c = sb("h_c", [P, MC, NT]), tile("y_c")

        score = Ring(Bank(stack.enter_context(nc.psum_tensor(f"score{i}", [P, 2, 512], F32))) for i in range(2))
        obank = [Bank(stack.enter_context(nc.psum_tensor(f"obank{i}", [P, 8, 64], F32))) for i in range(2)]
        gbank = Ring(Bank(stack.enter_context(nc.psum_tensor(f"gbank{i}", [P, 2, 256], F32))) for i in range(2))
        p_slots = Ring([Slot(), Slot()])
        through = {}
        for ph, mph in ("QA", "KK"):
            for name, width in (("q", NT), ("k", NT if ph == "Q" else NC_TOK)):
                through[ph, name] = nc.dram_tensor(f"via_{ph}_{name}", (2, CC, P, width), F32, kind="Internal").ap()
            through[mph, "m"] = nc.dram_tensor(f"via_{mph}_m", (NH, 2, NT), F32, kind="Internal").ap()
        s_one = stack.enter_context(nc.semaphore("b_const"))

        pl = Pipeline(nc, "b", dict(P=0, Q=0, A=1, V=1, T=2, K=2, B=3, C=4), 3 * NB, stack)
        op, take = pl.op, pl.take
        pl.shared = score.items + obank + gbank.items + p_slots.items
        state = {}

        def W(ph):
            return WT[state["L"][ph] % 2]

        def seq_of(ph, s):
            return s - (state["L"][ph] - 1) * NB

        def empties(bank, ph, mark):
            pl.empties(bank, ph, mark)
            for ring in (score, gbank):
                if bank in ring.held:
                    ring.free(bank)

        def gemm(ph, bank, outs, after, mark):
            after = list(after) + take(bank, ph)
            for i, (o, terms) in enumerate(outs):
                for k, (l, r_) in enumerate(terms):
                    op("pe", ph, lambda e, s, o=o, l=l, r_=r_, k=k, last=len(terms) - 1: e.matmul(
                        o, l, r_, start=(k == 0), stop=(k == last)), after=after,
                       mark=mark if i == len(outs) - 1 and k == len(terms) - 1 else None)
                    after = []
                    yield

        def transposes(ph, bank, src, after, mark):
            for i in range(TT * CC):
                tt, c = divmod(i, CC)
                op("pe", ph, lambda e, s, tt=tt, c=c: e.transpose(
                    bank.ap[:, c, tt * P:(tt + 1) * P], src[:, tt, c * P:(c + 1) * P], ident[:, :]),
                   after=(list(after) + take(bank, ph)) if i == 0 else [], mark=mark if i == 3 else None)

        def load(ph, mark, after, dst, src):
            op("sp", ph, lambda e, s: e.dma_start(dst, src(s)), after=after, mark=mark, dma=1)

        def load_cols(ph, mark, after, dst, at):
            load(ph, mark, after, dst[:, :], lambda s: cols[state["L"][ph]].rearrange(
                "p (b m) -> b p m", b=NB)[seq_of(ph, s), :, at:at + 4])

        def load_row(ph, mark, after, dst, i):
            load(ph, mark, after, dst[:, :], lambda s: rows[state["L"][ph]][
                seq_of(ph, s), i * D:(i + 1) * D].unsqueeze(0).to_broadcast([P, D]))

        def residual(ph, out, x, bias, after):
            op("pool", ph, lambda e, s: e.tensor_tensor(
                out[:, :, :], x[:, :, :], bias(s).unsqueeze(1).to_broadcast([P, TT, D]), ALU.add),
               after=after, mark="res")

        def x_of_layer(ph, after, dst):
            if state["L"][ph] > 1:
                after = after + [f"C.store@-{NB}"]
            load(ph, "x", after, dst[:, :, :], lambda s: by_tile(xs[state["L"][ph] - 1][seq_of(ph, s), :, :]))

        def p_load():
            x_of_layer("P", ["P.xn1@-1"], x_in)
            load_cols("P", "col", ["Q.xT1@-1"], col_a, 0)

        def p_norm():
            e_ = eps5 if state["L"]["P"] == 3 else eps6
            norm_ops(pl, "P", "", x_in, *st_p, e_, half, xn_a, (P, TT), ["P.x"], ["Q.xt@-1"])

        def q_start():
            b = gbank.get()
            transposes("Q", b, xn_a, ["P.xn1"], "xt")
            for c in range(CC):
                op("act", "Q", lambda e, s, c=c: e.activation(xT_a[:, c, :], b.ap[:, c, :], ACT.Identity,
                                                             bias=col_a[:, c:c + 1], scale=col_a[:, 2 + c:3 + c]),
                   after=["Q.xt", "P.col", "V.vp@-1"] if c == 0 else [], mark=f"xT{c}")
            empties(b, "Q", "xT1")

        def split(ph, view, dst, at, name, ready):
            w, free = W(ph), [f"{ph}.{name}out@-1"]
            for m in range(CC):
                op("act", ph, lambda e, s, m=m: e.activation(dst[:, 0, m, :], view(m), ACT.Identity,
                                                            bias=w["bcol"][:, at + m:at + m + 1]),
                   after=([ready] + free) if m == 0 else [], mark=f"{name}h{m}")
            for m in range(CC):
                op("dve", ph, lambda e, s, m=m: e.scalar_tensor_tensor(
                    dst[:, 1, m, :], view(m), w["bcol"][:, at + m:at + m + 1],
                    dst[:, 0, m, :].bitcast(F32), ALU.add, ALU.subtract),
                   after=[f"{ph}.{name}h1"] + (free if m == 0 else []), mark=f"{name}l{m}")

        def parts_out(ph, src, name):
            via = through[ph, name]
            op("sp", ph, lambda e, s: e.dma_start(
                via.rearrange("q c p n -> p (q c) n"), src[:, :, :, :].bitcast(F32).rearrange("p q c n -> p (q c) n")),
               after=[f"{ph}.{name}l1", f"{ph}.{name}h1", f"{ph}.{name}cat@-1"], mark=f"{name}out", dma=1)

        def parts_in(ph, dst, width, order, name, free):
            via = through[ph, name]
            for i, part in enumerate(order):
                for c in range(CC):
                    op("sp", ph, lambda e, s, c=c, i=i, part=part: e.dma_start(
                        dst[64 * c + HD * i:64 * c + HD * (i + 1), :, 0:width].bitcast(F32),
                        via[part, c, :, :].rearrange("(j d) n -> d j n", d=HD)),
                       after=([f"{ph}.{name}out", free]) if i + c == 0 else [],
                       mark=f"{name}cat", dma=6)

        def q_project(name, hl, at):
            w, b = W("Q"), gbank.get()
            yield from gemm("Q", b, [(b.ap[:, m, :], [(w["qkv"][:, k, at * D + m * P:at * D + (m + 1) * P],
                                                       xT_a[:, k, :]) for k in range(CC)]) for m in range(CC)],
                            ["Q.xT1"], name + "p")
            split("Q", lambda m: b.ap[:, m, :], hl, 2 * at, name, f"Q.{name}p")
            empties(b, "Q", name + "l1")
            parts_out("Q", hl, name)

        def q_stack():
            parts_in("Q", q_cat, NT, (0, 1, 0), "q", "A.stp7@-1")
            parts_in("Q", k_cat, NT, (0, 0, 1), "k", "A.stp7@-1")

        def v_parts(ph, full, cat, free):
            op("act", ph, lambda e, s: e.activation(cat(0), full, ACT.Copy), after=[f"{ph}.vf"] + free, mark="v1")
            op("dve", ph, lambda e, s: e.tensor_tensor(full, full, cat(0), ALU.subtract),
               after=[f"{ph}.v1"], mark="vr")
            op("act", ph, lambda e, s: e.activation(cat(1), full, ACT.Copy), after=[f"{ph}.vr"], mark="v2")
            op("dve", ph, lambda e, s: e.tensor_tensor(cat(2), full, cat(1), ALU.subtract),
               after=[f"{ph}.v2"] + free, mark="v3")

        def v_project():
            w, b = W("V"), gbank.get()
            yield from gemm("V", b, [(b.ap[:, tt, :], [(xT_a[:, k, tt * P:(tt + 1) * P], w["qkv"][:, k, 2 * D:3 * D])
                                                       for k in range(CC)]) for tt in range(TT)], ["Q.xT1"], "vp")
            op("dve", "V", lambda e, s: e.tensor_tensor(
                v_f[:, :, :], b.ap[:, :, :], w["bv"][:, :].unsqueeze(1).to_broadcast([P, TT, D]), ALU.add),
               after=["V.vp", "V.v3@-1"], mark="vf")
            empties(b, "V", "vf")

        def v_split():
            v_parts("V", v_f[:, :, :], lambda i: v_cat[:, :, :, VW * i:VW * i + HD].rearrange("p t h d -> p (t h) d"),
                    ["T.pv7@-1"])

        def a_load():
            x_of_layer("A", ["A.res@-1"], x_res)
            load_row("A", "bias", ["A.res@-1"], bias_a, 1)
            load_row("A", "gate", ["T.y@-1"], gate_a, 0)
            residual("A", res_a, x_res, lambda s: bias_a[:, :], ["A.x", "A.bias", "T.xb@-1"])

        def a_max(i):
            b = score.get()
            for tt in range(TT):
                for hf in range(2):
                    r0 = 64 * hf
                    op("pe", "A", lambda e, s, tt=tt, hf=hf, r0=r0: e.matmul(
                        b.ap[:, hf, tt * NT:(tt + 1) * NT], q_cat[r0:r0 + QROWS, i, tt * P:(tt + 1) * P],
                        k_cat[r0:r0 + QROWS, i, :], start=True, stop=True),
                       after=(["Q.qcat", "Q.kcat"] + take(b, "A")) if tt + hf == 0 else [],
                       mark=f"sp{i}" if tt + hf == 2 else None)
            op("dve", "A", lambda e, s: e.tensor_reduce(
                m_a[:, :, i::NPAIR].rearrange("p t h -> p h t"),
                b.ap[:, :, :].rearrange("p h (t k) -> p h t k", t=TT), AX.X, ALU.max),
               after=[f"A.sp{i}", "A.mt@-1"], mark=f"mx{i}")
            empties(b, "A", f"mx{i}")

        def max_rows(ph, m, mT, q_dst, last):
            b = gbank.get()
            for tt in range(TT):
                op("pe", ph, lambda e, s, tt=tt: e.transpose(b.ap[0:NH, 0, tt * P:(tt + 1) * P], m[:, tt, :],
                                                            ident[:, :]),
                   after=([f"{ph}.{last}"] + take(b, ph)) if tt == 0 else [], mark="mt" if tt else None)
            op("act", ph, lambda e, s: e.activation(mT[:, 0, :], b.ap[0:NH, 0, :], ACT.Copy),
               after=[f"{ph}.mt", f"{ph}.mout@-1"], mark="mh")
            op("dve", ph, lambda e, s: e.tensor_tensor(mT[:, 1, :], b.ap[0:NH, 0, :], mT[:, 0, :].bitcast(F32),
                                                      ALU.subtract),
               after=[f"{ph}.mh", f"{ph}.mout@-1"], mark="ml")
            empties(b, ph, "ml")
            via = through[ph, "m"]
            op("sp", ph, lambda e, s: e.dma_start(via, mT[:, :, :].bitcast(F32)),
               after=[f"{ph}.ml", f"{ph}.mh", f"{ph}.mrow@-1"], mark="mout", dma=1)
            for c in range(2):
                op("sp", ph, lambda e, s, c=c: e.dma_start(
                    q_dst[64 * c + QROWS:64 * c + QROWS + 2, :, :].bitcast(F32),
                    via[8 * c:8 * c + 8, :, :].rearrange("i q n -> q i n")),
                   after=[f"{ph}.mout"] if c == 0 else [], mark="mrow", dma=2)

        def slot_wait(slot, ph, what):
            if slot.last is None or ph not in pl.active:
                return []
            p1, p2, name = slot.last
            other = p1 if what == "pl" else p2
            return [f"{other}.{what}{name}@{slot.when - pl.iteration - pl.lags[other] + pl.lags[ph]}"]

        def weights(ph, pv_ph, i, b, rows_):
            slot = p_slots.get()
            p_slots.free(slot)
            n = p_slots.items.index(slot)
            pf, phi, plo = p_f[n], p_h[n], p_l[n]
            made, used = slot_wait(slot, ph, "pl"), slot_wait(slot, ph, "pv")
            op("act", ph, lambda e, s: e.activation(pf[0:rows_, :], b.ap[0:rows_, :, :].rearrange("p h n -> p (h n)"),
                                                   ACT.Exp, scale=SCALE),
               after=[f"{ph}.stp{i}"] + made, mark=f"ex{i}")
            empties(b, ph, f"ex{i}")
            op("act", ph, lambda e, s: e.activation(phi[0:rows_, :], pf[0:rows_, :], ACT.Copy, scale=PSCALE),
               after=[f"{ph}.ex{i}"] + used, mark=f"ph{i}")
            op("dve", ph, lambda e, s: e.scalar_tensor_tensor(plo[0:rows_, :], pf[0:rows_, :], PSCALE,
                                                             phi[0:rows_, :], ALU.mult, ALU.subtract),
               after=[f"{ph}.ph{i}"] + used, mark=f"pl{i}")
            if ph in pl.active:
                slot.last, slot.when = (ph, pv_ph, i), pl.iteration
            slot_of[ph, i] = n

        slot_of = {}

        def a_exp(i):
            b = score.get()
            for kc in range(TT):
                for hf in range(2):
                    r0 = 64 * hf
                    op("pe", "A", lambda e, s, kc=kc, hf=hf, r0=r0: e.matmul(
                        b.ap[:, hf, kc * NT:(kc + 1) * NT], k_cat[r0:r0 + QROWS + 2, i, kc * P:(kc + 1) * P],
                        q_cat[r0:r0 + QROWS + 2, i, :], start=True, stop=True),
                       after=(["A.mrow"] + take(b, "A")) if kc + hf == 0 else [],
                       mark=f"stp{i}" if kc + hf == 2 else None)
            weights("A", "T" if i == NPAIR - 1 else "A", i, b, P)

        def a_pv(ph, i):
            slot, j = slot_of["A", i], i % 4
            for tt in range(TT):
                ob = obank[tt]
                w = take(ob, ph) if j == 0 else []
                for hf in range(2):
                    terms = [(kc, src) for kc in range(TT) for src in (p_h, p_l)]
                    for n_, (kc, src) in enumerate(terms):
                        at = hf * 512 + kc * NT + tt * P
                        op("pe", ph, lambda e, s, hf=hf, kc=kc, src=src, at=at, n_=n_, ob=ob: e.matmul(
                            ob.ap[:, 4 * hf + j, 0:VC], src[slot][:, at:at + P], v_cat[:, kc, 8 * hf + i, :],
                            start=(n_ == 0), stop=(n_ == 3)),
                           after=([f"A.pl{i}", f"A.ph{i}", "V.v1", "V.v2", "V.v3"] + w) if n_ + hf == 0 else [],
                           mark=f"pv{i}" if tt + hf == 2 and n_ == 3 else None)

        def out_heads(ph, u, o, last, free):
            for tt in range(TT):
                ob = obank[tt]
                op("dve", ph, lambda e, s, tt=tt, ob=ob: e.tensor_reduce(
                    o_sum[:, tt, :, :], ob.ap[:, :, 0:VC].rearrange("p g (q e) -> p g e q", q=VP), AX.X, ALU.add),
                   after=[f"{ph}.{last}"], mark=f"os{u}{tt}")
                empties(ob, ph, f"os{u}{tt}")
            for tt in range(TT):
                op("dve", ph, lambda e, s, tt=tt: e.reciprocal(o_rc[:, tt, :], o_sum[:, tt, :, HD]),
                   after=[f"{ph}.os{u}{tt}"], mark=f"rc{u}{tt}")
            for tt in range(TT):
                op("dve", ph, lambda e, s, tt=tt: e.tensor_tensor(
                    o[:, tt, :].rearrange("p (h f) -> p h f", h=2)[:, :, 4 * HD * u:4 * HD * (u + 1)]
                     .rearrange("p h (j d) -> p h j d", d=HD),
                    o_sum[:, tt, :, 0:HD].rearrange("p (h j) d -> p h j d", h=2),
                    o_rc[:, tt, :].rearrange("p (h j) -> p h j", h=2).unsqueeze(3).to_broadcast([P, 2, 4, HD]),
                    ALU.mult),
                   after=[f"{ph}.rc{u}{tt}"] + (free if tt == 0 else []), mark=f"on{u}{tt}")

        def turn_heads(ph, o, oT, ready):
            b = gbank.get()
            transposes(ph, b, o, ready, "ot")
            op("act", ph, lambda e, s: e.activation(oT[:, :, :], b.ap[:, :, :], ACT.Copy),
               after=[f"{ph}.ot", f"{ph}.op@-1"], mark="oT")
            empties(b, ph, "oT")

        def project(ph, oT, w):
            b = gbank.get()
            yield from gemm(ph, b, [(b.ap[:, tt, :], [(oT[:, k, tt * P:(tt + 1) * P], w[:, k, :])
                                                      for k in range(CC)]) for tt in range(TT)], [f"{ph}.oT"], "op")
            return b

        def t_project():
            b = yield from project("T", oT_a, W("T")["o"])
            op("dve", "T", lambda e, s: e.tensor_tensor(
                y_a[:, :, :], b.ap[:, :, :], gate_a[:, :].unsqueeze(1).to_broadcast([P, TT, D]), ALU.mult),
               after=["T.op", "A.gate"], mark="y")
            empties(b, "T", "y")
            op("dve", "T", lambda e, s: e.tensor_tensor(x_b[:, :, :], y_a[:, :, :], res_a[:, :, :], ALU.add),
               after=["T.y", "A.res", "K.res@-1"] + (["K.xt@-1"] if state["L"]["T"] == 3 else []), mark="xb")
            if state["L"]["T"] < 3:
                norm_ops(pl, "T", "n", x_b, *st_t, eps6, half, xn_b, (P, TT), ["T.xb"], ["K.xt@-1"], group="Tn")

        def k_load():
            load("K", "ctx", ["K.ct@-1"] + (["K.cxn0@-1"] if state["L"]["K"] == 1 else []), ctx[:, 0, :],
                 lambda s: t["ctx_1024"][seq_of("K", s), :, :])

        def k_norm():
            if state["L"]["K"] == 1:
                norm_ops(pl, "K", "c", ctx, *st_k, eps6, half, ctxn, (NC_TOK, 1), ["K.ctx"], ["K.ct@-1"], group="Kn")

        def k_context():
            cs, cr = (ctxn, "K.cxn0") if state["L"]["K"] == 1 else (ctx, "K.ctx")
            b = gbank.get()
            for c in range(CC):
                op("pe", "K", lambda e, s, c=c: e.transpose(b.ap[:, 0, c * NC_TOK:(c + 1) * NC_TOK],
                                                           cs[:, 0, c * P:(c + 1) * P], ident[0:NC_TOK, 0:NC_TOK]),
                   after=([cr] + take(b, "K")) if c == 0 else [], mark="ct" if c else None)
            op("act", "K", lambda e, s: e.activation(
                ctxT[:, :, :], b.ap[:, 0, 0:CC * NC_TOK].rearrange("p (c k) -> p c k", c=CC), ACT.Copy),
               after=["K.ct", "K.vp@-1"], mark="cT")
            empties(b, "K", "cT")

        def k_kv():
            w, b = W("K"), gbank.get()
            kv_ = lambda m: b.ap[:, 0, m * NC_TOK:(m + 1) * NC_TOK]
            yield from gemm("K", b, [(kv_(m), [(w["kvc"][:, k, m * P:(m + 1) * P], ctxT[:, k, :])
                                               for k in range(CC)]) for m in range(CC)] +
                            [(b.ap[0:NC_TOK, 1, :], [(ctxT[:, k, :], w["kvc"][:, k, D:2 * D]) for k in range(CC)])],
                            ["K.cT"], "vp")
            split("K", kv_, kc_hl, 6, "k", "K.vp")
            op("dve", "K", lambda e, s: e.tensor_tensor(vc_f[:, :], b.ap[0:NC_TOK, 1, :], w["bvc"][0:NC_TOK, :],
                                                       ALU.add), after=["K.v3@-1"], mark="vf")
            empties(b, "K", "vf")
            parts_out("K", kc_hl, "k")
            v_parts("K", vc_f[:, :], lambda i: vc_cat[:, :, VW * i:VW * i + HD], ["B.pv3@-1"])
            parts_in("K", kc_cat, NC_TOK, (0, 0, 1), "k", "B.stp3@-1")

        def k_start():
            w = W("K")
            src, ready = (xn_b, ["T.nxn1"]) if state["L"]["K"] < 3 else (x_b, ["T.xb"])
            residual("K", res_b, x_b, lambda s: w["boc"][:, :], ["T.xb", "B.xc@-1"])
            b = gbank.get()
            transposes("K", b, src, ready, "xt")
            op("act", "K", lambda e, s: e.activation(xT_b[:, :, :], b.ap[:, :, :], ACT.Copy),
               after=["K.xt", "K.qp@-1"], mark="xT")
            empties(b, "K", "xT")

        def k_q():
            w, b = W("K"), gbank.get()
            yield from gemm("K", b, [(b.ap[:, m, :], [(w["qc"][:, k, m * P:(m + 1) * P], xT_b[:, k, :])
                                                      for k in range(CC)]) for m in range(CC)], ["K.xT"], "qp")
            split("K", lambda m: b.ap[:, m, :], qc_hl, 4, "q", "K.qp")
            empties(b, "K", "ql1")
            parts_out("K", qc_hl, "q")
            parts_in("K", qc_cat, NT, (0, 1, 0), "q", "B.stp3@-1")

        def k_max(i):
            b = score.get()
            view = b.ap[:, :, :].rearrange("p h (j t k) -> p h j t k", j=2, t=TT)
            for j in range(2):
                for tt in range(TT):
                    for hf in range(2):
                        r0 = 64 * hf
                        op("pe", "K", lambda e, s, j=j, tt=tt, hf=hf, r0=r0: e.matmul(
                            view[:, hf, j, tt, 0:CPAD], qc_cat[r0:r0 + QROWS, 2 * i + j, tt * P:(tt + 1) * P],
                            kc_cat[r0:r0 + QROWS, 2 * i + j, :], start=True, stop=True),
                           after=(["K.qcat", "K.kcat"] + take(b, "K")) if j + tt + hf == 0 else [],
                           mark=f"sp{i}" if j + tt + hf == 3 else None)
            for hf in range(2):
                op("dve", "K", lambda e, s, hf=hf: e.tensor_reduce(
                    m_b[:, :, 8 * hf + 2 * i:8 * hf + 2 * i + 2].rearrange("p t j -> p j t"),
                    view[:, hf, :, :, 0:NC_TOK], AX.X, ALU.max),
                   after=[f"K.sp{i}", "K.mt@-1"], mark=f"mx{i}{hf}")
            empties(b, "K", f"mx{i}1")

        def b_exp(i):
            b = score.get()
            for j in range(2):
                for hf in range(2):
                    r0 = 64 * hf
                    op("pe", "B", lambda e, s, j=j, hf=hf, r0=r0: e.matmul(
                        b.ap[0:NC_TOK, hf, j * NT:(j + 1) * NT], kc_cat[r0:r0 + QROWS + 2, 2 * i + j, 0:NC_TOK],
                        qc_cat[r0:r0 + QROWS + 2, 2 * i + j, :], start=True, stop=True),
                       after=(["K.mrow"] + take(b, "B")) if j + hf == 0 else [],
                       mark=f"stp{i}" if j + hf == 2 else None)
            weights("B", "B", i, b, NC_TOK)

        def b_pv(i):
            slot = slot_of["B", i]
            for tt in range(TT):
                ob = obank[tt]
                w = take(ob, "B") if i % 2 == 0 else []
                for j in range(2):
                    jj = (2 * i + j) % 4
                    for hf in range(2):
                        for n_, src in enumerate((p_h, p_l)):
                            at = hf * 512 + j * NT + tt * P
                            op("pe", "B", lambda e, s, hf=hf, src=src, at=at, n_=n_, ob=ob, jj=jj, j=j: e.matmul(
                                ob.ap[:, 4 * hf + jj, 0:VC], src[slot][0:NC_TOK, at:at + P],
                                vc_cat[:, 8 * hf + 2 * i + j, :], start=(n_ == 0), stop=(n_ == 1)),
                               after=([f"B.pl{i}", f"B.ph{i}", "K.v1", "K.v2", "K.v3"] + w) if j + n_ + hf == 0 else [],
                               mark=f"pv{i}" if tt + j + hf == 3 and n_ == 1 else None)

        def b_project():
            b = yield from project("B", oT_b, W("B")["oc"])
            op("dve", "B", lambda e, s: e.tensor_tensor(x_c[:, :, :], b.ap[:, :, :], res_b[:, :, :], ALU.add),
               after=["B.op", "K.res", "C.res@-1"], mark="xc")
            empties(b, "B", "xc")
            e_ = eps5 if state["L"]["B"] == 3 else eps6
            norm_ops(pl, "B", "n", x_c, *st_b, e_, half, xn_c, (P, TT), ["B.xc"], ["C.xt@-1"])

        def b_load():
            load_cols("B", "col", ["C.xT1@-1"], col_c, 4)
            load_row("B", "bias", ["C.res@-1"], bias_c, 3)

        def c_start():
            residual("C", res_c, x_c, lambda s: bias_c[:, :], ["B.xc", "B.bias", "C.yo@-1"])
            b = gbank.get()
            transposes("C", b, xn_c, ["B.nxn1"], "xt")
            for c in range(CC):
                op("act", "C", lambda e, s, c=c: e.activation(xT_c[:, c, :], b.ap[:, c, :], ACT.Identity,
                                                             bias=col_c[:, c:c + 1], scale=col_c[:, 2 + c:3 + c]),
                   after=["C.xt", "B.col", f"C.hp{MC // 2 - 1}@-1"] if c == 0 else [], mark=f"xT{c}")
            empties(b, "C", "xT1")

        def c_up():
            w = W("C")
            gelu = ACT.Gelu if state["L"]["C"] == 3 else ACT.Gelu_apprx_tanh
            for i in range(MC // 2):
                b = gbank.get()
                yield from gemm("C", b, [(b.ap[:, j, :], [(w["w1"][:, k, (2 * i + j) * P:(2 * i + j + 1) * P],
                                                           xT_c[:, k, :]) for k in range(CC)]) for j in range(2)],
                                ["C.xT1"], f"hp{i}")
                for j in range(2):
                    m = 2 * i + j
                    op("act", "C", lambda e, s, j=j, m=m, b=b: e.activation(
                        h_c[:, m, :], b.ap[:, j, :], gelu, bias=w["bcol"][:, 8 + m:9 + m]),
                       after=[f"C.hp{i}", "C.down@-1"] if j == 0 else [], mark=f"h{m}")
                empties(b, "C", f"h{2 * i + 1}")

        def c_down():
            w, b = W("C"), gbank.get()
            yield from gemm("C", b, [(b.ap[:, tt, :], [(h_c[:, m, tt * P:(tt + 1) * P], w["w2"][:, m, :])
                                                       for m in range(MC)]) for tt in range(TT)],
                            [f"C.h{MC - 1}"], "down")
            op("dve", "C", lambda e, s: e.tensor_tensor(
                y_c[:, :, :], b.ap[:, :, :], gate_c[:, :].unsqueeze(1).to_broadcast([P, TT, D]), ALU.mult),
               after=["C.down", "C.gate", "C.store@-1"], mark="y")
            empties(b, "C", "y")
            op("dve", "C", lambda e, s: e.tensor_tensor(y_c[:, :, :], y_c[:, :, :], res_c[:, :, :], ALU.add),
               after=["C.y", "C.res"], mark="yo")
            L = state["L"]["C"]
            op("sp", "C", lambda e, s: e.dma_start(by_tile(xs[L][seq_of("C", s), :, :]), y_c[:, :, :]),
               after=["C.yo"], mark="store", dma=1)

        def iteration(lo, hi):
            pl.iteration = lo
            act = [ph for ph in "PQVATKBC" if 0 <= lo - pl.lags[ph] < 3 * NB]
            pl.begin(act)
            state["L"] = {ph: (lo - pl.lags[ph]) // NB + 1 for ph in act}
            fixed = dict(state["L"])
            for ring in (score, gbank, p_slots):
                ring.rewind()

            def on(ph, step, *args):
                if ph in act:
                    for _ in step(*args) or ():
                        pass

            def some(ph, steps, n):
                if ph in act:
                    for _ in (steps if n is None else islice(steps, n)):
                        pass

            up, down = c_up(), c_down()

            on("P", p_load)
            on("K", k_load)
            on("C", load_row, "C", "gate", ["C.y@-1"], gate_c, 2)
            on("B", b_exp, 0)
            on("T", a_pv, "T", 7)
            on("T", out_heads, "T", 1, o_a, "pv7", [])
            on("B", b_exp, 1)
            vv = v_project()
            some("V", vv, 2)
            on("B", b_pv, 0)
            on("T", turn_heads, "T", o_a, oT_a, ["A.on01", "T.on11"])
            on("B", b_exp, 2)
            some("V", vv, None)
            on("B", b_pv, 1)
            on("B", out_heads, "B", 0, o_b, "pv1", ["B.ot@-1"])
            on("T", t_project)
            on("B", b_exp, 3)
            on("C", c_start)
            on("B", b_pv, 2)
            on("K", k_norm)
            some("C", up, 2)
            on("B", b_pv, 3)
            on("B", out_heads, "B", 1, o_b, "pv3", [])
            on("A", a_max, 0)
            some("C", up, 2)
            on("K", k_context)
            on("A", a_max, 1)
            on("B", turn_heads, "B", o_b, oT_b, ["B.on01", "B.on11"])
            on("K", k_kv)
            on("A", a_max, 2)
            on("K", k_start)
            on("B", b_project)
            on("A", a_max, 3)
            on("V", v_split)
            on("K", k_q)
            on("A", a_max, 4)
            some("C", up, 3)
            on("P", p_norm)
            on("A", a_max, 5)
            some("C", up, 3)
            on("A", a_max, 6)
            some("C", up, 3)
            on("A", a_max, 7)
            some("C", up, 3)
            on("A", max_rows, "A", m_a, mT_a, q_cat, "mx7")
            some("C", up, None)
            on("Q", q_start)
            on("Q", q_project, "q", q_hl, 0)
            on("Q", q_project, "k", k_hl, 1)
            on("A", a_load)
            for i in range(NPAIR):
                on("A", a_exp, i)
                if 1 <= i <= 4:
                    on("K", k_max, i - 1)
                some("C", down, 2)
                if i == 5:
                    on("K", max_rows, "K", m_b, mT_b, qc_cat, "mx31")
                if i:
                    on("A", a_pv, "A", i - 1)
                if i == 4:
                    on("A", out_heads, "A", 0, o_a, "pv3", ["T.ot@-1"])
            some("C", down, None)
            on("B", b_load)
            on("Q", q_stack)
            for o in pl.ops:
                o.emit = bind(o.emit, fixed)
            pl.end(lo, hi)

        def bind(emit, layers):
            def f(e, s):
                state["L"] = layers
                return emit(e, s)
            return f

        n, last = 0, 3 * NB + max(pl.lags.values())
        while n < last:
            lo, hi = n, n + 1
            if n < 3 * NB and n % NB == 5:
                hi = n // NB * NB + NB
            iteration(lo, hi)
            n = hi

        block = stack.enter_context(nc.Block())

        def emit_with_weights(name, eng, waits):
            segs = pl.segments
            for seg in segs:
                for L in LAYERS:
                    if seg[0] == NB * (L - 1):
                        waits(eng, L)
                pl.segments = [seg]
                pl.emit(name, eng)
            pl.segments = segs

        def wait_weights(eng, L):
            eng.wait_ge(s_w[L], n_w[L])

        @block.sync
        def _(eng):
            eng.wait_ge(s_one, 3)

            segs = pl.segments
            for seg in segs:
                if seg[0] == NB + 5:
                    for mark in ("C.down", "B.op", "T.op", "V.vf", "K.res", "Q.kl1", "Q.kp", "K.kl1",
                                 "K.vf", f"C.h{MC - 1}"):
                        eng.wait_ge(pl.sem(pl.marks[mark].group), pl.value(mark, NB - 1))
                    load_layer(eng, 3)
                pl.segments = [seg]
                pl.emit("sp", eng)
            pl.segments = segs
            eng.wait_ge(pl.sem("C.store"), 16 * 3 * NB)

        @block.gpsimd
        def _(eng):
            emit_with_weights("pool", eng, wait_weights)

        @block.scalar
        def _(eng):
            emit_with_weights("act", eng, wait_weights)

        @block.vector
        def _(eng):
            eng.memset(k_cat[:, :, :].bitcast(F32), -1.0)
            eng.memset(kc_cat[:, :, :].bitcast(F32), -1.0).then_inc(s_one, 1)
            eng.memset(v_cat[:, :, :, :].rearrange("p t h c -> p (t h c)"), 0.0)
            eng.memset(vc_cat[:, :, :].rearrange("p h c -> p (h c)"), 0.0).then_inc(s_one, 1)
            eng.wait_ge(s_one, 2)
            eng.memset(v_cat[:, :, :, HD:HD + 1], 1.0)
            eng.memset(vc_cat[:, :, HD:HD + 1], 1.0).then_inc(s_one, 1)
            emit_with_weights("dve", eng, wait_weights)

        @block.tensor
        def _(eng):
            eng.wait_ge(s_one, 3)
            emit_with_weights("pe", eng, wait_weights)


def kernel(**inputs):
    import concourse.bacc as bacc
    from concourse import mybir
    from concourse.bass_utils import run_bass_kernel_spmd

    nc = bacc.Bacc("TRN2", target_bir_lowering=False, num_devices=1)
    arrays, t = {}, {}
    for name in inputs:
        a = np.ascontiguousarray(inputs[name])
        arrays[f"in_{name}_dram"] = a
        t[name] = nc.dram_tensor(f"in_{name}_dram", a.shape, mybir.dt.from_np(a.dtype), kind="ExternalInput").ap()
    t["out"] = nc.dram_tensor("out_0_dram", (NB, NT, D), mybir.dt.float32, kind="ExternalOutput").ap()
    build(nc, t)
    r = run_bass_kernel_spmd(nc, [arrays], core_ids=[0])
    return r.results[0]["out_0_dram"]
```

```python
import numpy as np

NB, NT, D, NC_TOK = 16, 256, 256, 77
NH, HD = 16, 16
P = 128
TT, CC = NT // P, D // P
MLP = 1024
MC = MLP // P
NE, RH = 3, 512
EC = NE * RH // P
VP, VW = 3, HD + 1
VC = VP * VW
NPAIR = NH // 2
QROWS = 3 * HD
CPAD = NC_TOK + 1
PSCALE = 2.0 ** 15


def start(eng, loads):
    for dst, src, sem in loads:
        eng.dma_start(dst, src).then_inc(sem, 16)


class Mark:

    def __init__(self, group, place, count, dma):
        self.group, self.place, self.count, self.dma = group, place, count, dma


class Op:
    def __init__(self, engine, phase, emit, after, mark, alone):
        self.engine, self.phase, self.emit, self.after = engine, phase, emit, after
        self.mark, self.alone = mark, alone


class Bank:

    def __init__(self, ap):
        self.ap, self.emptied, self.when = ap, None, 0


class Slot:

    def __init__(self):
        self.last, self.when = None, 0


class Ring:

    def __init__(self, items):
        self.items = list(items)
        self.rewind()

    def rewind(self):
        self.order, self.held = list(self.items), []

    def get(self):
        item = next(i for i in self.order if i not in self.held)
        self.order.remove(item)
        self.order.append(item)
        self.held.append(item)
        return item

    def free(self, item):
        self.held.remove(item)

    def lend(self, items):
        self.order = list(items) + self.order

    def give_back(self, items):
        self.order = [i for i in self.order if i not in items]


class Pipeline:

    def __init__(self, nc, name, lags, n_seq, stack):
        self.nc, self.name, self.lags, self.n_seq, self.stack = nc, name, lags, n_seq, stack
        self.marks, self.per_seq, self.sems = {}, {}, {}
        self.segments, self.shared = [], []

    def begin(self, active):
        self.active, self.ops, self.seen, self.counts = active, [], set(), {}
        self.group_of = {}

    def op(self, engine, phase, emit, after=(), mark=None, dma=0, group=None, alone=False):
        if phase not in self.active:
            return
        if mark:
            name = f"{phase}.{mark}"
            if name not in self.seen:
                self.seen.add(name)
                g = f"{name}" if dma else f"{engine}_{group or phase}"
                place = self.counts.get(g, 0)
                self.counts[g] = place + 1
                m = Mark(g, place, dma or 1, bool(dma))
                old = self.marks.setdefault(name, m)
                assert (old.group, old.place, old.count) == (m.group, m.place, m.count), name
            mark = name
        self.ops.append(Op(engine, phase, emit, list(after), mark, alone))

    def take(self, bank, phase):
        if phase not in self.active or bank.emptied is None:
            return []
        other = bank.emptied.split(".")[0]
        off = bank.when - self.iteration + self.lags[other] * -1 + self.lags[phase]
        return [f"{bank.emptied}@{off}"] if off else [bank.emptied]

    def empties(self, bank, phase, mark):
        if phase in self.active:
            bank.emptied, bank.when = f"{phase}.{mark}", self.iteration

    def end(self, lo, hi):
        for g, n in self.counts.items():
            assert self.per_seq.setdefault(g, n) == n, g
        for b in self.shared:
            if b.when == lo:
                b.when = hi - 1
        self.segments.append((lo, hi, self.ops))

    def sem(self, group):
        if group not in self.sems:
            name = f"{self.name}_{group}".replace(".", "_")
            self.sems[group] = self.stack.enter_context(self.nc.semaphore(name))
        return self.sems[group]

    def value(self, mark, seq):
        m = self.marks[mark]
        if m.dma:
            return seq * (16 * m.count) + 16 * m.count
        return seq * self.per_seq[m.group] + (m.place + 1)

    def emit(self, engine, eng):
        for lo, hi, ops in self.segments:
            mine = [o for o in ops if o.engine == engine]
            if not mine:
                continue
            if hi == lo + 1:
                self._body(eng, mine, lo, False)
            else:
                with eng.Fori(lo, hi) as n:
                    self._body(eng, mine, n, True)

    def _body(self, eng, ops, n, loop):
        waited = {}
        for o in ops:
            seq = n - self.lags[o.phase]
            waits = []
            for w in o.after:
                name, _, off = w.partition("@")
                off = int(off or 0)
                m = self.marks[name]
                lag = self.lags[o.phase]
                reach = (off - lag, m.place)
                if waited.get(m.group, (-99, 0)) >= reach:
                    continue
                waited[m.group] = reach
                if loop:
                    val = self.value(name, seq + off)
                else:
                    at = min(seq + off, self.n_seq - 1)
                    if at < 0:
                        continue
                    val = self.value(name, at)
                waits.append((self.sem(m.group), val))
            for s, v in waits:
                eng.wait_ge(s, v)
                if loop and (o.alone or o.engine == "sp"):
                    eng.sem_inc(self.sem("holder"), 1)
            ins = o.emit(eng, seq)
            if o.mark:
                m = self.marks[o.mark]
                ins.then_inc(self.sem(m.group), 16 if m.dma else 1)


def build(nc, t):
    import concourse.bass as bass
    from concourse import mybir
    from contextlib import ExitStack

    F32, F32R = mybir.dt.float32, mybir.dt.float32r
    BF16, F16 = mybir.dt.bfloat16, mybir.dt.float16
    ALU, ACT, AX = mybir.AluOpType, mybir.ActivationFunctionType, mybir.AxisListType

    root = ExitStack()

    def buffers(stack):
        def sb(name, shape, dt=F32):
            return stack.enter_context(nc.sbuf_tensor(name, shape, dt))
        return sb

    def scratch(name, shape):
        return nc.dram_tensor(name, shape, F32, kind="Internal").ap()

    xs = [scratch(f"x_after_L{i}", (NB, NT, D)) for i in range(3)] + [t["out"]]
    cols = [scratch("cols_L0", (P, NB * 14))] + [scratch(f"cols_L{i}", (P, NB * 8)) for i in (1, 2, 3)]
    rows = [scratch("rows_L0", (NB, NE))] + [scratch(f"rows_L{i}", (NB, 4 * D)) for i in (1, 2, 3)]

    def chunks(w):
        return w.rearrange("(k p) n -> p k n", p=P)

    def column(v):
        return v.rearrange("(k p) -> p k", p=P)

    def spread(v, n=P):
        return v.unsqueeze(0).to_broadcast([n, v.shape[0]])

    def by_tile(x):
        return x.rearrange("(t p) f -> p t f", p=P)

    with root, nc.allow_non_contiguous_dma(reason="bias vectors as columns, a few KB"):
        sbr = buffers(root)
        ident = sbr("ident", [P, P])
        half = sbr("minus_half", [P, 2])
        eps5 = sbr("eps5", [P, 2])
        eps6 = sbr("eps6", [P, 2])
        condT = sbr("condT", [P, CC, NB])
        cond_siluT = sbr("cond_siluT", [P, CC, NB])

        def layer_buffers(stack, i):
            sb = buffers(stack)
            return dict(
                qkv=sb(f"w_qkv{i}", [P, CC, 3 * D]), o=sb(f"w_o{i}", [P, CC, D]),
                qc=sb(f"w_qc{i}", [P, CC, D]), kvc=sb(f"w_kvc{i}", [P, CC, 2 * D]),
                oc=sb(f"w_oc{i}", [P, CC, D]), w1=sb(f"w_1{i}", [P, CC, MLP]),
                w2=sb(f"w_2{i}", [P, MC, D]),
                bcol=sb(f"b_col{i}", [P, 16]),
                bv=sb(f"b_v{i}", [P, D]), bvc=sb(f"b_vc{i}", [P, D]), boc=sb(f"b_oc{i}", [P, D]))

        WT = [None, layer_buffers(root, 1)]
        s_w = [root.enter_context(nc.semaphore(f"weights_L{L}")) for L in range(4)]
        n_w = [0] * 4

        def layer_parts(L):
            if L == 1:
                g = lambda k: t["L1_xcond_" + k]
                return dict(qkv=[g("W_qkv")], o=g("W_proj"), qc=g("W_qc"), kvc=[g("W_kvc")], oc=g("W_cproj"),
                            w1=g("W_mlp1"), w2=g("W_mlp2"), bqkv=g("b_qkv"), bqc=g("b_qc"), bkvc=g("b_kvc"),
                            boc=g("b_cproj"), b1=g("b_mlp1"))
            if L == 2:
                g = lambda k: t["L2_xcond_" + k]
                return dict(qkv=[g("qkv_w")], o=g("sa_proj_w"), qc=g("q_w"), kvc=[g("kv_w")], oc=g("ca_proj_w"),
                            w1=g("fc1_w"), w2=g("fc2_w"), bqkv=g("qkv_b"), bqc=g("q_b"), bkvc=g("kv_b"),
                            boc=g("ca_proj_b"), b1=g("fc1_b"))
            g = lambda k: t["L3_xcond_" + k]
            return dict(qkv=[g("sa_qw"), g("sa_kw"), g("sa_vw")], o=g("sa_ow"), qc=g("ca_qw"),
                        kvc=[g("ca_kw"), g("ca_vw")], oc=g("ca_ow"), w1=g("ffn_w1"), w2=g("ffn_w2"),
                        bq=g("sa_qb"), bk=g("sa_kb"), bv=g("sa_vb"), bqc=g("ca_qb"), bkc=g("ca_kb"),
                        bvc=g("ca_vb"), boc=g("ca_ob"), b1=g("ffn_b1"))

        def layer_loads(L):
            w, p, loads = WT[L % 2], layer_parts(L), []

            def go(dst, src):
                loads.append((dst, src, s_w[L]))
                n_w[L] += 16

            def side_by_side(dst, parts):
                at = 0
                for x in parts:
                    go(dst[:, :, at:at + x.shape[1]], chunks(x))
                    at += x.shape[1]

            side_by_side(w["qkv"], p["qkv"])
            if L < 3:
                bq, bk, bv = (p["bqkv"][i * D:(i + 1) * D] for i in range(3))
                bkc, bvc = (p["bkvc"][i * D:(i + 1) * D] for i in range(2))
            else:
                bq, bk, bv, bkc, bvc = p["bq"], p["bk"], p["bv"], p["bkc"], p["bvc"]
            for i, b in enumerate((bq, bk, p["bqc"], bkc)):
                go(w["bcol"][:, 2 * i:2 * i + 2], column(b))
            go(w["bcol"][:, 8:16], column(p["b1"]))
            go(w["bv"][:, :], spread(bv))
            go(w["bvc"][:, :], spread(bvc))
            go(w["boc"][:, :], spread(p["boc"]))
            side_by_side(w["kvc"], p["kvc"])
            for k in ("o", "qc", "oc", "w1", "w2"):
                go(w[k][:, :, :], chunks(p[k]))
            return loads

        with ExitStack() as for_tables:
            mods = mod_buffers(nc, t, chunks, column, spread, buffers, for_tables)
            with ExitStack() as for_mixture:
                mix = mixture_buffers(nc, t, chunks, column, spread, buffers, for_mixture)

                anchor_table(nc, t, cols[0], rows[0], ident, half, eps5, eps6, condT, cond_siluT, column, spread,
                             chunks, buffers, mix["loads_f"], mix["loads_g"])
                mixture(nc, t, mix, mods["loads"] + layer_loads(1), xs[0], cols[0], rows[0], ident, half, eps5, by_tile, buffers)
            layer_tables(nc, mods, cols, rows, condT, cond_siluT, buffers)
        WT[0] = layer_buffers(root, 0)
        blocks(nc, t, xs, cols, rows, ident, half, eps5, eps6, WT, s_w, n_w, layer_loads, by_tile, buffers)


def anchor_table(nc, t, cols0, rows0, ident, half, eps5, eps6, condT, cond_siluT, column, spread, chunks, buffers,
                 loads_f, loads_g):
    from concourse import mybir
    from contextlib import ExitStack
    F32 = mybir.dt.float32
    ALU, ACT = mybir.AluOpType, mybir.ActivationFunctionType

    with ExitStack() as stack:
        sb = buffers(stack)
        cond = sb("cond", [NB, D])
        cond_silu = sb("cond_silu", [NB, D])
        w_anchor = sb("w_anchor", [P, CC, EC + 2, P])
        w_router = sb("w_router", [P, CC, NE])
        b_anchor = sb("b_anchor", [P, EC + 2])
        b_router = sb("b_router", [NB, NE])
        tab0 = sb("tab0", [P, NB, EC + 2])
        tr0 = sb("tr0", [NB, NE])
        ps = [stack.enter_context(nc.psum_tensor(f"t_ps{i}", [P, 512], F32)) for i in range(3)]
        sem = lambda n: stack.enter_context(nc.semaphore(n))
        s_cond, s_in, s_idm, s_id = sem("t_cond"), sem("t_in"), sem("t_idm"), sem("t_id")
        s_silu, s_T, s_cT, s_mm = sem("t_silu"), sem("t_T"), sem("t_cT"), sem("t_mm")
        s_dve, s_out = sem("t_dve"), sem("t_out")
        loads = []
        G0 = t["L0_xcond_gate_w1"]
        for e in range(NE):
            for k in range(CC):
                loads.append((w_anchor[:, k, 4 * e:4 * e + 4, :].rearrange("p m n -> p (m n)"),
                              t["L0_xcond_e_w1"][e, 2 * D + k * P:2 * D + (k + 1) * P, :]))
        for k in range(CC):
            loads.append((w_anchor[:, k, EC:EC + 2, :].rearrange("p m n -> p (m n)"),
                          G0[2 * D + k * P:2 * D + (k + 1) * P, :]))
        loads.append((w_router[:, :, :], chunks(t["L0_xcond_router_W"][2 * D:3 * D, :])))
        loads.append((b_anchor[:, 0:EC], t["L0_xcond_e_b1"].rearrange("e (k p) -> p (e k)", p=P)))
        loads.append((b_anchor[:, EC:EC + 2], column(t["L0_xcond_gate_b1"])))
        loads.append((b_router[:, :], spread(t["L0_xcond_router_b"], NB)))
        ALL = 16 * len(loads)

        block = stack.enter_context(nc.Block())

        @block.sync
        def _(eng):
            eng.dma_start(cond[:, :], t["cond_1024"]).then_inc(s_cond, 16)
            for dst, src in loads:
                eng.dma_start(dst, src).then_inc(s_in, 16)
            start(eng, loads_f)
            eng.wait_ge(s_dve, 2)
            eng.dma_start(cols0, tab0[:, :, :].rearrange("p b m -> p (b m)")).then_inc(s_out, 16)
            eng.dma_start(rows0, tr0[:, :]).then_inc(s_out, 16)
            eng.wait_ge(s_out, 32)

        @block.gpsimd
        def _(eng):
            eng.memset(half[:, :], -0.5)
            eng.memset(eps5[:, :], 1e-5)
            eng.memset(eps6[:, :], 1e-6)
            eng.memset(ident[:, :], 0.0).then_inc(s_idm, 1)
            eng.wait_ge(s_idm, 1)
            eng.affine_select(out=ident[:, :], in_=ident[:, :], compare_op=ALU.not_equal, fill=1.0,
                              base=0, pattern=[[-1, P]], channel_multiplier=1).then_inc(s_id, 1)

        @block.scalar
        def _(eng):
            eng.wait_ge(s_cond, 16)
            eng.activation(cond_silu[:, :], cond[:, :], ACT.Silu).then_inc(s_silu, 1)
            eng.wait_ge(s_in, ALL)
            start(eng, loads_g)

        @block.tensor
        def _(eng):
            eng.wait_ge(s_id, 1)
            eng.wait_ge(s_cond, 16)
            for c in range(CC):
                eng.transpose(ps[0][:, c * NB:(c + 1) * NB], cond[:, c * P:(c + 1) * P], ident[0:NB, 0:NB])
            eng.wait_ge(s_silu, 1)
            for c in range(CC):
                mm = eng.transpose(ps[0][:, (CC + c) * NB:(CC + c + 1) * NB], cond_silu[:, c * P:(c + 1) * P],
                                   ident[0:NB, 0:NB])
            mm.then_inc(s_T, 1)
            eng.wait_ge(s_cT, 1)
            eng.wait_ge(s_in, ALL)
            for m in range(EC + 2):
                for k in range(CC):
                    eng.matmul(ps[1][:, m * NB:(m + 1) * NB], w_anchor[:, k, m, :], condT[:, k, :],
                               start=(k == 0), stop=(k == CC - 1))
            for k in range(CC):
                mm = eng.matmul(ps[2][0:NB, 0:NE], condT[:, k, :], w_router[:, k, :],
                                start=(k == 0), stop=(k == CC - 1))
            mm.then_inc(s_mm, 1)

        @block.vector
        def _(eng):
            eng.wait_ge(s_T, 1)
            eng.tensor_copy(condT[:, :, :], ps[0][:, 0:CC * NB].rearrange("p (c b) -> p c b", b=NB))
            eng.tensor_copy(cond_siluT[:, :, :],
                            ps[0][:, CC * NB:2 * CC * NB].rearrange("p (c b) -> p c b", b=NB)).then_inc(s_cT, 1)
            eng.wait_ge(s_in, ALL)
            eng.wait_ge(s_mm, 1)
            eng.tensor_tensor(tab0[:, :, :].rearrange("p b m -> p m b"),
                              ps[1][:, 0:(EC + 2) * NB].rearrange("p (m b) -> p m b", b=NB),
                              b_anchor[:, :].unsqueeze(2).to_broadcast([P, EC + 2, NB]), ALU.add).then_inc(s_dve, 1)
            eng.tensor_tensor(tr0[:, :], ps[2][0:NB, 0:NE], b_router[:, :], ALU.add).then_inc(s_dve, 1)


def mod_buffers(nc, t, chunks, column, spread, buffers, stack):
    sb = buffers(stack)
    w_mod = [sb("w_mod1", [P, CC, 6 * D]), sb("w_mod2", [P, CC, 6 * D])]
    w_aff = [sb("w_aff1", [P, CC, 2 * D]), sb("w_aff2", [P, CC, 2 * D])]
    b_mod = sb("b_mod", [P, 2, 12])
    b_aff = sb("b_aff", [P, 2, 4])
    ln_gb = sb("ln_gb", [P, 2, 4])
    g_row = sb("g_row", [NB, 2, 2, D])
    o_row = sb("o_row", [NB, 3, 2, D])
    s_mod = stack.enter_context(nc.semaphore("mod_weights"))
    loads = []

    def load(dst, src):
        loads.append((dst, src, s_mod))

    load(w_mod[0][:, :, :], chunks(t["L1_xcond_W_mod"]))
    load(w_mod[1][:, :, :], chunks(t["L2_xcond_adaln_w"]))
    load(w_aff[0][:, :, :], chunks(t["L3_xcond_aff1_w"]))
    load(w_aff[1][:, :, :], chunks(t["L3_xcond_aff2_w"]))
    for i, b in enumerate((t["L1_xcond_b_mod"], t["L2_xcond_adaln_b"])):
        load(b_mod[:, i, :], column(b))
        for j, at in enumerate((2 * D, 5 * D)):
            load(g_row[:, i, j, :], spread(b[at:at + D], NB))
    for i in range(2):
        load(b_aff[:, i, :], column(t[f"L3_xcond_aff{i + 1}_b"]))
        load(ln_gb[:, i, 0:2], column(t[f"L3_xcond_ln{i + 1}_g"]))
        load(ln_gb[:, i, 2:4], column(t[f"L3_xcond_ln{i + 1}_b"]))
    for i, (a, m) in enumerate((("L1_xcond_b_proj", "L1_xcond_b_mlp2"), ("L2_xcond_sa_proj_b", "L2_xcond_fc2_b"),
                                ("L3_xcond_sa_ob", "L3_xcond_ffn_b2"))):
        load(o_row[:, i, 0, :], spread(t[a], NB))
        load(o_row[:, i, 1, :], spread(t[m], NB))
    return dict(w_mod=w_mod, w_aff=w_aff, b_mod=b_mod, b_aff=b_aff, ln_gb=ln_gb, g_row=g_row, o_row=o_row,
                sem=s_mod, loads=loads)


def layer_tables(nc, mods, cols, rows, condT, cond_siluT, buffers):
    from concourse import mybir
    from contextlib import ExitStack
    F32 = mybir.dt.float32
    ALU = mybir.AluOpType
    w_mod, w_aff, b_mod, b_aff, ln_gb, g_row, o_row = (mods[k] for k in (
        "w_mod", "w_aff", "b_mod", "b_aff", "ln_gb", "g_row", "o_row"))

    with ExitStack() as stack:
        sb = buffers(stack)
        tab = [sb(f"tab{i}", [P, NB, 8]) for i in (1, 2, 3)]
        tr = [sb(f"tr{i}", [NB, 4, D]) for i in (1, 2, 3)]
        ps = [stack.enter_context(nc.psum_tensor(f"l_ps{i}", [P, 512], F32)) for i in range(5)]
        sem = lambda n: stack.enter_context(nc.semaphore(n))
        s_mm, s_dve, s_out = sem("l_mm"), sem("l_dve"), sem("l_out")
        ALL = 16 * len(mods["loads"])

        block = stack.enter_context(nc.Block())

        @block.sync
        def _(eng):
            eng.wait_ge(s_dve, DVE_DONE)
            for i in range(3):
                eng.dma_start(cols[i + 1], tab[i][:, :, :].rearrange("p b m -> p (b m)")).then_inc(s_out, 16)
                eng.dma_start(rows[i + 1], tr[i][:, :, :].rearrange("b g f -> b (g f)")).then_inc(s_out, 16)
            eng.wait_ge(s_out, 16 * 6)

        @block.tensor
        def _(eng):
            eng.wait_ge(mods["sem"], ALL)
            for i in range(2):
                for j, m in enumerate((0, 1, 2, 3, 6, 7, 8, 9)):
                    for k in range(CC):
                        eng.matmul(ps[i][:, j * NB:(j + 1) * NB],
                                   w_mod[i][:, k, m * P:(m + 1) * P], cond_siluT[:, k, :],
                                   start=(k == 0), stop=(k == CC - 1))
                for j in range(4):
                    for k in range(CC):
                        eng.matmul(ps[4][:, (4 * i + j) * NB:(4 * i + j + 1) * NB],
                                   w_aff[i][:, k, j * P:(j + 1) * P], condT[:, k, :],
                                   start=(k == 0), stop=(k == CC - 1))
                for j, at in enumerate((2 * D, 5 * D)):
                    for k in range(CC):
                        mm = eng.matmul(ps[2 + i][0:NB, j * D:(j + 1) * D], cond_siluT[:, k, :],
                                        w_mod[i][:, k, at:at + D], start=(k == 0), stop=(k == CC - 1))
                mm.then_inc(s_mm, 1)

        dve_marks = [0]

        @block.vector
        def _(eng):
            def done(ins, wait=True):
                ins.then_inc(s_dve, 1)
                dve_marks[0] += 1
                if wait:
                    eng.wait_ge(s_dve, dve_marks[0])

            eng.wait_ge(mods["sem"], ALL)

            def flip(tile, a, b):
                return tile[:, :, a:b].rearrange("p b m -> p m b")

            def over_b(cols_):
                return cols_.unsqueeze(2).to_broadcast([P, cols_.shape[1], NB])

            def ps_cols(i, a, b):
                return ps[i][:, a * NB:b * NB].rearrange("p (m b) -> p m b", b=NB)

            for i in range(2):
                eng.wait_ge(s_mm, i + 1)
                done(eng.tensor_tensor(flip(tab[i], 0, 4), ps_cols(i, 0, 4),
                                       over_b(b_mod[:, i, 0:4]), ALU.add))
                done(eng.tensor_tensor(flip(tab[i], 4, 8), ps_cols(i, 4, 8),
                                       over_b(b_mod[:, i, 6:10]), ALU.add))
                for a in (2, 6):
                    done(eng.tensor_scalar(tab[i][:, :, a:a + 2], tab[i][:, :, a:a + 2], 1.0, None, ALU.add))
                for j in range(2):
                    done(eng.tensor_tensor(tr[i][:, 2 * j, :], ps[2 + i][0:NB, j * D:(j + 1) * D],
                                           g_row[:, i, j, :], ALU.add))
                    done(eng.tensor_tensor(tr[i][:, 2 * j + 1, :], tr[i][:, 2 * j, :], o_row[:, i, j, :], ALU.mult))
            for j in range(2):
                at = 4 * j
                done(eng.tensor_tensor(flip(tab[2], at + 2, at + 4), ps_cols(4, at, at + 2),
                                       over_b(b_aff[:, j, 0:2]), ALU.add))
                done(eng.tensor_tensor(flip(tab[2], at, at + 2), flip(tab[2], at + 2, at + 4),
                                       over_b(ln_gb[:, j, 2:4]), ALU.mult))
                done(eng.tensor_tensor(flip(tab[2], at, at + 2), flip(tab[2], at, at + 2),
                                       over_b(b_aff[:, j, 2:4]), ALU.add))
                done(eng.tensor_tensor(flip(tab[2], at, at + 2), ps_cols(4, at + 2, at + 4),
                                       flip(tab[2], at, at + 2), ALU.add))
                done(eng.tensor_tensor(flip(tab[2], at + 2, at + 4), flip(tab[2], at + 2, at + 4),
                                       over_b(ln_gb[:, j, 0:2]), ALU.mult))
                done(eng.memset(tr[2][:, 2 * j, :], 1.0))
                done(eng.tensor_copy(tr[2][:, 2 * j + 1, :], o_row[:, 2, j, :]))
            assert dve_marks[0] == DVE_DONE


DVE_DONE = 2 * (4 + 4) + 2 * 7


def norm_stats(pl, ph, pre, x, st, mv, rstd, eps, half, parts, after, group=None):
    from concourse import mybir
    ALU = mybir.AluOpType
    n, tiles = parts
    G = dict(group=group)
    for i in range(tiles):
        pl.op("dve", ph, lambda e, s, i=i: e.bn_stats(st[0:n, i, :], x[0:n, i, :]),
              after=list(after) if i == 0 else [], mark=f"{pre}st{i}", **G)
    for i in range(tiles):
        pl.op("dve", ph, lambda e, s, i=i: e.bn_aggr(mv[0:n, i, :], st[0:n, i, :]),
              after=[f"{ph}.{pre}st{i}"] + ([f"{ph}.{pre}ve@-1"] if i == 0 else []),
              mark=f"{pre}mv{i}", alone=True, **G)
    pl.op("pool", ph, lambda e, s: e.tensor_tensor(rstd[0:n, 0:tiles], mv[0:n, 0:tiles, 1], eps[0:n, 0:tiles], ALU.add),
          after=[f"{ph}.{pre}mv{tiles - 1}", f"{ph}.{pre}xn{tiles - 1}@-1"], mark=f"{pre}ve", **G)
    pl.op("pool", ph, lambda e, s: e.tensor_tensor(rstd[0:n, 0:tiles], rstd[0:n, 0:tiles], half[0:n, 0:tiles], ALU.pow),
          after=[f"{ph}.{pre}ve"], mark=f"{pre}rstd", **G)


def norm_apply(pl, ph, pre, x, mv, rstd, out, parts, wait_out, group=None):
    from concourse import mybir
    ALU = mybir.AluOpType
    n, tiles = parts
    for i in range(tiles):
        pl.op("dve", ph, lambda e, s, i=i: e.tensor_scalar(out[0:n, i, :], x[0:n, i, :], mv[0:n, i, 0:1],
                                                          rstd[0:n, i:i + 1], ALU.subtract, ALU.mult),
              after=([f"{ph}.{pre}rstd"] + list(wait_out)) if i == 0 else [], mark=f"{pre}xn{i}", group=group)


def mixture_buffers(nc, t, chunks, column, spread, buffers, stack):
    g = lambda k: t["L0_xcond_" + k]
    sb = buffers(stack)
    wq, wk, wv = (sb(f"m_{k}", [P, CC, D]) for k in ("wq", "wk", "wv"))
    rw = sb("m_rw", [P, 4, NE])
    w1 = sb("m_w1", [P, 4, EC, P])
    w2 = sb("m_w2", [P, EC, D])
    g1 = sb("m_g1", [P, 4, D])
    g2 = sb("m_g2", [P, CC, D])
    wo = sb("m_wo", [P, CC, D])
    lng = sb("m_lng", [P, 4])
    b2 = sb("m_b2", [P, NE, D])
    bg2 = sb("m_bg2", [P, D])
    bo = sb("m_bo", [P, D])
    s_f, s_g = (stack.enter_context(nc.semaphore(n)) for n in ("weights_L0_F", "weights_L0_G"))
    loads = [(d[:, :, :], chunks(s_), s_f) for d, s_ in ((wq, g("Wq")), (wk, g("Wk")), (wv, g("Wv")))]
    loads.append((lng[:, 0:2], column(g("ln_gamma")), s_f))
    loads.append((lng[:, 2:4], column(g("ln_beta")), s_f))
    loads.append((rw[:, :, :], chunks(g("router_W")[0:2 * D, :]), s_f))
    n_f = len(loads)
    for e in range(NE):
        for k in range(4):
            loads.append((w1[:, k, 4 * e:4 * e + 4, :].rearrange("p m n -> p (m n)"),
                          g("e_w1")[e, k * P:(k + 1) * P, :], s_g))
    loads.append((g1[:, :, :], chunks(g("gate_w1")[0:2 * D, :]), s_g))
    for e in range(NE):
        loads.append((w2[:, 4 * e:4 * e + 4, :], chunks(g("e_w2")[e, :, :]), s_g))
        loads.append((b2[:, e, :], spread(g("e_b2")[e, :]), s_g))
    loads.append((g2[:, :, :], chunks(g("gate_w2")), s_g))
    loads.append((wo[:, :, :], chunks(g("out_w")), s_g))
    loads.append((bg2[:, :], spread(g("gate_b2")), s_g))
    loads.append((bo[:, :], spread(g("out_b")), s_g))
    return dict(w=(wq, wk, wv, rw, w1, w2, g1, g2, wo, lng, b2, bg2, bo), loads_f=loads[:n_f], loads_g=loads[n_f:], s_f=s_f,
                n_f=16 * n_f, s_g=s_g, n_g=16 * (len(loads) - n_f))


def mixture(nc, t, mix, later, x_out, cols0, rows0, ident, half, eps5, by_tile, buffers):
    from concourse import mybir
    from contextlib import ExitStack
    F32 = mybir.dt.float32
    ALU, ACT, AX = mybir.AluOpType, mybir.ActivationFunctionType, mybir.AxisListType
    wq, wk, wv, rw, w1, w2, g1, g2, wo, lng, b2, bg2, bo = mix["w"]

    with ExitStack() as stack:
        sb = buffers(stack)
        x, xn, nx = sb("m_x", [P, TT, D]), sb("m_xn", [P, TT, D]), sb("m_nx", [P, CC, NT])
        st, mv, rstd = sb("m_st", [P, TT, 6]), sb("m_mv", [P, TT, 2]), sb("m_rstd", [P, TT])
        ctx, ctxT = sb("m_ctx", [NC_TOK, D]), sb("m_ctxT", [P, CC, NC_TOK])
        qT, kT, v = sb("m_qT", [P, CC, NT]), sb("m_kT", [P, CC, NC_TOK]), sb("m_v", [NC_TOK, D])
        mx, sm, rs = sb("m_mx", [P, TT]), sb("m_sm", [P, TT]), sb("m_rs", [P, TT])
        wgt, wgtT = sb("m_wgt", [P, TT, NC_TOK]), sb("m_wgtT", [NC_TOK, NT])
        ar, lg = sb("m_ar", [P, NE]), sb("m_lg", [P, TT, NE])
        rmx, rsm, rrs = sb("m_rmx", [P, TT]), sb("m_rsm", [P, TT]), sb("m_rrs", [P, TT])
        rex, prob = sb("m_rex", [P, TT, NE]), sb("m_prob", [P, TT, NE])
        evT = sb("m_evT", [P, CC, NT])
        comb = sb("m_comb", [P, 4, NT])
        xg = sb("m_xg", [P, TT, D])
        acol = sb("m_acol", [P, EC + 2])
        h = sb("m_h", [P, EC, NT])
        gT = sb("m_gT", [P, CC, NT])
        gp, th = sb("m_gp", [P, TT, D]), sb("m_th", [P, TT, D])
        r, rT = sb("m_r", [P, TT, D]), sb("m_rT", [P, CC, NT])
        y = sb("m_y", [P, TT, D])
        ps = [stack.enter_context(nc.psum_tensor(f"m_ps{i}", [P, 2, 256], F32)) for i in range(8)]
        banks = [Bank(p) for p in ps]
        fb, hb, eb, gb = banks[0:2], banks[2:5], banks[5:7], banks[7]
        pl = Pipeline(nc, "m", dict(F=0, G=1), NB, stack)
        pl.shared = banks
        op, take, empties = pl.op, pl.take, pl.empties

        def f_load():
            op("sp", "F", lambda e, s: e.dma_start(x[:, :, :], by_tile(t["x"][s, :, :])),
               after=["F.xcopy@-1"], mark="x", dma=1)
            op("sp", "F", lambda e, s: e.dma_start(ctx[:, :], t["ctx_1024"][s, :, :]),
               after=["F.ctxt@-1"], mark="ctx", dma=1)
            op("sp", "F", lambda e, s: e.dma_start(ar[:, :], rows0[s, :].unsqueeze(0).to_broadcast([P, NE])),
               after=["F.lg@-1"], mark="ar", dma=1)

        def f_norm():
            norm_stats(pl, "F", "", x, st, mv, rstd, eps5, half, (P, TT), ["F.x"])
            norm_apply(pl, "F", "", x, mv, rstd, xn, (P, TT), ["F.xt@-1"])

        def f_transpose():
            b = fb[0]
            for tt in range(TT):
                for c in range(CC):
                    op("pe", "F", lambda e, s, tt=tt, c=c: e.transpose(
                        b.ap[:, c, tt * P:(tt + 1) * P], xn[:, tt, c * P:(c + 1) * P], ident[:, :]),
                       after=(["F.xn1"] + take(b, "F")) if tt + c == 0 else [],
                       mark="xt" if tt + c == 2 else None)
            for c in range(CC):
                op("dve", "F", lambda e, s, c=c: e.tensor_scalar(nx[:, c, :], b.ap[:, c, :], lng[:, c:c + 1],
                                                                lng[:, 2 + c:3 + c], ALU.mult, ALU.add),
                   after=["F.xt", "F.nxcopy@-1", "F.q@-1", "F.lgp@-1"] if c == 0 else [], mark=f"nx{c}")
            empties(b, "F", "nx1")
            b2_ = fb[1]
            for c in range(CC):
                op("pe", "F", lambda e, s, c=c: e.transpose(b2_.ap[:, 0, c * NC_TOK:(c + 1) * NC_TOK],
                                                           ctx[:, c * P:(c + 1) * P], ident[0:NC_TOK, 0:NC_TOK]),
                   after=(["F.ctx"] + take(b2_, "F")) if c == 0 else [], mark="ctxt" if c else None)
            op("act", "F", lambda e, s: e.activation(
                ctxT[:, :, :], b2_.ap[:, 0, 0:CC * NC_TOK].rearrange("p (c k) -> p c k", c=CC), ACT.Copy),
               after=["F.ctxt", "F.v@-1"], mark="ctxT")
            empties(b2_, "F", "ctxT")

        def f_qkv():
            b = fb[0]
            for m in range(CC):
                for k in range(CC):
                    op("pe", "F", lambda e, s, m=m, k=k: e.matmul(b.ap[:, m, :], wq[:, k, m * P:(m + 1) * P],
                                                                 nx[:, k, :], start=(k == 0), stop=(k == CC - 1)),
                       after=(["F.nx1"] + take(b, "F")) if m + k == 0 else [], mark="q" if m + k == 2 else None)
            op("act", "F", lambda e, s: e.activation(qT[:, :, :], b.ap[:, :, :], ACT.Copy),
               after=["F.q", "F.sc@-1"], mark="qT")
            empties(b, "F", "qT")
            b2_ = fb[1]
            first = take(b2_, "F")
            for m in range(CC):
                for k in range(CC):
                    op("pe", "F", lambda e, s, m=m, k=k: e.matmul(
                        b2_.ap[:, 0, m * NC_TOK:(m + 1) * NC_TOK], wk[:, k, m * P:(m + 1) * P], ctxT[:, k, :],
                        start=(k == 0), stop=(k == CC - 1)),
                       after=(["F.ctxT"] + first) if m + k == 0 else [])
            for k in range(CC):
                op("pe", "F", lambda e, s, k=k: e.matmul(b2_.ap[0:NC_TOK, 1, :], ctxT[:, k, :], wv[:, k, :],
                                                        start=(k == 0), stop=(k == CC - 1)),
                   mark="v" if k else None)
            op("act", "F", lambda e, s: e.activation(
                kT[:, :, :], b2_.ap[:, 0, 0:CC * NC_TOK].rearrange("p (c k) -> p c k", c=CC), ACT.Copy),
               after=["F.v", "F.sc@-1"], mark="kT")
            op("act", "F", lambda e, s: e.activation(v[:, :], b2_.ap[0:NC_TOK, 1, :], ACT.Copy),
               after=["F.ev@-1"], mark="vS")
            empties(b2_, "F", "vS")

        def f_scores():
            b = fb[0]
            for tt in range(TT):
                for k in range(CC):
                    op("pe", "F", lambda e, s, tt=tt, k=k: e.matmul(
                        b.ap[:, 0, tt * P:tt * P + NC_TOK], qT[:, k, tt * P:(tt + 1) * P], kT[:, k, :],
                        start=(k == 0), stop=(k == CC - 1)),
                       after=(["F.qT", "F.kT"] + take(b, "F")) if tt + k == 0 else [],
                       mark="sc" if tt + k == 2 else None)
            view = b.ap[:, 0, :].rearrange("p (t k) -> p t k", t=TT)[:, :, 0:NC_TOK]
            op("dve", "F", lambda e, s: e.tensor_reduce(mx[:, :], view, AX.X, ALU.max, negate=True),
               after=["F.sc"] , mark="mx0")
            op("dve", "F", lambda e, s: e.tensor_scalar(mx[:, :], mx[:, :], D ** -0.5, None, ALU.mult),
               after=["F.mx0", "F.exp1@-1"], mark="mx")
            for tt in range(TT):
                op("act", "F", lambda e, s, tt=tt: e.activation(
                    wgt[:, tt, :], b.ap[:, 0, tt * P:tt * P + NC_TOK], ACT.Exp, bias=mx[:, tt:tt + 1],
                    scale=D ** -0.5, accum_out=sm[:, tt:tt + 1]),
                   after=["F.mx", "F.wn1@-1", "F.rs@-1", "F.wt@-1"] if tt == 0 else [], mark=f"exp{tt}")
            empties(b, "F", "exp1")
            op("dve", "F", lambda e, s: e.reciprocal(rs[:, :], sm[:, :]), after=["F.exp1", "F.wn1@-1"], mark="rs")
            for tt in range(TT):
                op("dve", "F", lambda e, s, tt=tt: e.tensor_scalar(wgt[:, tt, :], wgt[:, tt, :], rs[:, tt:tt + 1],
                                                                  None, ALU.mult),
                   after=["F.rs"] if tt == 0 else [], mark=f"wn{tt}")

        def f_evidence():
            b = fb[1]
            for tt in range(TT):
                op("pe", "F", lambda e, s, tt=tt: e.transpose(b.ap[0:NC_TOK, 0, tt * P:(tt + 1) * P], wgt[:, tt, :],
                                                             ident[:, :]),
                   after=(["F.wn1"] + take(b, "F")) if tt == 0 else [], mark="wt" if tt else None)
            op("act", "F", lambda e, s: e.activation(wgtT[:, :], b.ap[0:NC_TOK, 0, :], ACT.Copy),
               after=["F.wt", "F.ev@-1"], mark="wgtT")
            empties(b, "F", "wgtT")
            b2_ = fb[0]
            for m in range(CC):
                op("pe", "F", lambda e, s, m=m: e.matmul(b2_.ap[:, m, :], v[:, m * P:(m + 1) * P], wgtT[:, :],
                                                        start=True, stop=True),
                   after=(["F.wgtT", "F.vS"] + take(b2_, "F")) if m == 0 else [], mark="ev" if m else None)
            op("act", "F", lambda e, s: e.activation(evT[:, :, :], b2_.ap[:, :, :], ACT.Copy),
               after=["F.ev", "F.evcopy@-1", "F.lgp@-1"], mark="evT")
            empties(b2_, "F", "evT")

        def f_router():
            b = fb[1]
            for tt in range(TT):
                for k in range(4):
                    src = (nx, evT)[k // CC]
                    op("pe", "F", lambda e, s, tt=tt, k=k, src=src: e.matmul(
                        b.ap[:, 0, tt * NE:(tt + 1) * NE], src[:, k % CC, tt * P:(tt + 1) * P], rw[:, k, :],
                        start=(k == 0), stop=(k == 3)),
                       after=(["F.evT", "F.nx1"] + take(b, "F")) if tt + k == 0 else [],
                       mark="lgp" if tt + k == 4 else None)
            op("dve", "F", lambda e, s: e.tensor_tensor(
                lg[:, :, :], b.ap[:, 0, 0:TT * NE].rearrange("p (t e) -> p t e", t=TT),
                ar[:, :].unsqueeze(1).to_broadcast([P, TT, NE]), ALU.add),
               after=["F.lgp", "F.ar", "F.rexp1@-1"], mark="lg")
            empties(b, "F", "lg")
            op("dve", "F", lambda e, s: e.tensor_reduce(rmx[:, :], lg[:, :, :], AX.X, ALU.max, negate=True),
               after=["F.lg"], mark="rmx")
            for tt in range(TT):
                op("act", "F", lambda e, s, tt=tt: e.activation(rex[:, tt, :], lg[:, tt, :], ACT.Exp,
                                                               bias=rmx[:, tt:tt + 1],
                                                               accum_out=rsm[:, tt:tt + 1]),
                   after=["F.rmx", "F.prob1@-1"] if tt == 0 else [], mark=f"rexp{tt}")
            op("dve", "F", lambda e, s: e.reciprocal(rrs[:, :], rsm[:, :]), after=["F.rexp1"], mark="rrs")

        def f_hand_over():
            for tt in range(TT):
                op("dve", "F", lambda e, s, tt=tt: e.tensor_scalar(prob[:, tt, :], rex[:, tt, :], rrs[:, tt:tt + 1],
                                                                  None, ALU.mult),
                   after=["F.rrs", "G.r_last@-1"] if tt == 0 else [], mark=f"prob{tt}")
            op("act", "F", lambda e, s: e.activation(comb[:, 0:2, :], nx[:, :, :], ACT.Copy),
               after=["F.nx1", "G.g1p@-1"], mark="nxcopy")
            op("act", "F", lambda e, s: e.activation(comb[:, 2:4, :], evT[:, :, :], ACT.Copy),
               after=["F.evT"], mark="evcopy")
            op("act", "F", lambda e, s: e.activation(xg[:, :, :], x[:, :, :], ACT.Copy),
               after=["F.x", "G.y3@-1"], mark="xcopy")

        def g_load():
            op("sp", "G", lambda e, s: e.dma_start(
                acol[:, :], cols0.rearrange("p (b m) -> b p m", b=NB)[s, :, :]),
               after=["G.g1s1@-1", f"G.h{EC - 1}@-1"], mark="acol", dma=1)

        def g_h(i):
            b = hb[i % 3]
            for m2 in range(2):
                m = 2 * i + m2
                for k in range(4):
                    op("pe", "G", lambda e, s, m=m, m2=m2, k=k: e.matmul(
                        b.ap[:, m2, :], w1[:, k, m, :], comb[:, k, :], start=(k == 0), stop=(k == 3)),
                       after=(["F.nxcopy", "F.evcopy"] + take(b, "G")) if m2 + k == 0 else [],
                       mark=f"hp{i}" if m2 * 4 + k == 7 else None)
            for m2 in range(2):
                m = 2 * i + m2
                op("act", "G", lambda e, s, m=m, m2=m2: e.activation(h[:, m, :], b.ap[:, m2, :], ACT.Silu,
                                                                    bias=acol[:, m:m + 1]),
                   after=[f"G.hp{i}", "G.acol", f"G.ep{m // 4}@-1"] if m2 == 0 else [], mark=f"h{m}")
            empties(b, "G", f"h{2 * i + 1}")

        def g_e2(ex):
            b = eb[ex % 2]
            for tt in range(TT):
                for k in range(4):
                    op("pe", "G", lambda e, s, tt=tt, k=k: e.matmul(
                        b.ap[:, tt, :], h[:, 4 * ex + k, tt * P:(tt + 1) * P], w2[:, 4 * ex + k, :],
                        start=(k == 0), stop=(k == 3)),
                       after=([f"G.h{4 * ex + 3}"] + take(b, "G")) if tt + k == 0 else [],
                       mark=f"ep{ex}" if tt * 4 + k == 7 else None)
            for tt in range(TT):
                if ex == 0:
                    op("dve", "G", lambda e, s, tt=tt: e.tensor_scalar(r[:, tt, :], b.ap[:, tt, :],
                                                                      prob[:, tt, 0:1], None, ALU.mult),
                       after=["G.ep0", "F.prob1", "G.rt@-1"], mark=f"r{ex}{tt}")
                else:
                    op("dve", "G", lambda e, s, tt=tt: e.scalar_tensor_tensor(
                        r[:, tt, :], b.ap[:, tt, :], prob[:, tt, ex:ex + 1], r[:, tt, :], ALU.mult, ALU.add),
                       after=[f"G.ep{ex}", f"G.b{ex - 1}{tt}"], mark=f"r{ex}{tt}")
                bl = "r_last" if ex == NE - 1 and tt == TT - 1 else f"b{ex}{tt}"
                op("dve", "G", lambda e, s, tt=tt: e.scalar_tensor_tensor(
                    r[:, tt, :], b2[:, ex, :], prob[:, tt, ex:ex + 1], r[:, tt, :], ALU.mult, ALU.add),
                   after=[f"G.r{ex}{tt}"], mark=bl)
            empties(b, "G", f"r{ex}1")

        def g_gate1():
            b = gb
            for m in range(CC):
                for k in range(4):
                    op("pe", "G", lambda e, s, m=m, k=k: e.matmul(b.ap[:, m, :], g1[:, k, m * P:(m + 1) * P],
                                                                 comb[:, k, :], start=(k == 0), stop=(k == 3)),
                       after=(["F.nxcopy", "F.evcopy"] + take(b, "G")) if m + k == 0 else [],
                       mark="g1p" if m * 4 + k == 7 else None)
            for m in range(CC):
                op("act", "G", lambda e, s, m=m: e.activation(gT[:, m, :], b.ap[:, m, :], ACT.Silu,
                                                             bias=acol[:, EC + m:EC + m + 1]),
                   after=["G.g1p", "G.acol", "G.g2p@-1"] if m == 0 else [], mark=f"g1s{m}")
            empties(b, "G", "g1s1")

        def g_gate2():
            b = gb
            for tt in range(TT):
                for k in range(CC):
                    op("pe", "G", lambda e, s, tt=tt, k=k: e.matmul(b.ap[:, tt, :], gT[:, k, tt * P:(tt + 1) * P],
                                                                   g2[:, k, :], start=(k == 0), stop=(k == 1)),
                       after=(["G.g1s1"] + take(b, "G")) if tt + k == 0 else [],
                       mark="g2p" if tt + k == 2 else None)
            op("dve", "G", lambda e, s: e.tensor_tensor(gp[:, :, :], b.ap[:, :, :],
                                                       bg2[:, :].unsqueeze(1).to_broadcast([P, TT, D]), ALU.add),
               after=["G.g2p", "G.th@-1"], mark="gp")
            empties(b, "G", "gp")
            op("act", "G", lambda e, s: e.activation(th[:, :, :], gp[:, :, :], ACT.Tanh, scale=0.5),
               after=["G.gp", "G.y2@-1"], mark="th")
            op("dve", "G", lambda e, s: e.tensor_scalar(th[:, :, :], th[:, :, :], 0.5, 0.5, ALU.mult, ALU.add),
               after=["G.th"], mark="gate")

        def g_out():
            b = gb
            for tt in range(TT):
                for c in range(CC):
                    op("pe", "G", lambda e, s, tt=tt, c=c: e.transpose(
                        b.ap[:, c, tt * P:(tt + 1) * P], r[:, tt, c * P:(c + 1) * P], ident[:, :]),
                       after=(["G.r_last", f"G.b{NE - 1}0"] + take(b, "G")) if tt + c == 0 else [],
                       mark="rt" if tt + c == 2 else None)
            op("act", "G", lambda e, s: e.activation(rT[:, :, :], b.ap[:, :, :], ACT.Copy),
               after=["G.rt", "G.yp@-1"], mark="rT")
            empties(b, "G", "rT")
            b2_ = eb[1]
            for tt in range(TT):
                for k in range(CC):
                    op("pe", "G", lambda e, s, tt=tt, k=k: e.matmul(b2_.ap[:, tt, :], rT[:, k, tt * P:(tt + 1) * P],
                                                                   wo[:, k, :], start=(k == 0), stop=(k == 1)),
                       after=(["G.rT"] + take(b2_, "G")) if tt + k == 0 else [],
                       mark="yp" if tt + k == 2 else None)
            op("dve", "G", lambda e, s: e.tensor_tensor(y[:, :, :], b2_.ap[:, :, :],
                                                       bo[:, :].unsqueeze(1).to_broadcast([P, TT, D]), ALU.add),
               after=["G.yp", "G.store@-1"], mark="y1")
            empties(b2_, "G", "y1")
            op("dve", "G", lambda e, s: e.tensor_tensor(y[:, :, :], y[:, :, :], th[:, :, :], ALU.mult),
               after=["G.y1", "G.gate"], mark="y2")
            op("dve", "G", lambda e, s: e.tensor_tensor(y[:, :, :], y[:, :, :], xg[:, :, :], ALU.add),
               after=["G.y2", "F.xcopy"], mark="y3")
            op("sp", "G", lambda e, s: e.dma_start(by_tile(x_out[s, :, :]), y[:, :, :]),
               after=["G.y3"], mark="store", dma=1)

        def iteration(n, hi, active):
            pl.iteration = n
            pl.begin(active)
            f_load()
            g_load()
            if 1 <= n <= n_late:
                op("sp", "F", lambda e, s: start(e, later[n - 1::n_late]))
            g_h(0)
            f_norm()
            g_h(1)
            f_transpose()
            g_e2(0)
            f_qkv()
            g_h(2)
            f_scores()
            g_h(3)
            g_e2(1)
            f_evidence()
            g_gate1()
            f_router()
            g_h(4)
            g_h(5)
            g_gate2()
            g_e2(2)
            g_out()
            f_hand_over()
            pl.end(n, hi)

        n_late = 5
        iteration(0, 1, "F")
        iteration(1, 2, "FG")
        for n in range(2, 1 + n_late):
            iteration(n, n + 1, "FG")
        iteration(1 + n_late, NB, "FG")
        iteration(NB, NB + 1, "G")

        def emit_with_weights(name, eng):
            segs = pl.segments
            for n, seg in enumerate(segs):
                if n == 0:
                    eng.wait_ge(mix["s_f"], mix["n_f"])
                if n == 1:
                    eng.wait_ge(mix["s_g"], mix["n_g"])
                pl.segments = [seg]
                pl.emit(name, eng)
            pl.segments = segs

        block = stack.enter_context(nc.Block())

        @block.sync
        def _(eng):
            pl.emit("sp", eng)
            eng.wait_ge(pl.sem("G.store"), 16 * NB)

        @block.gpsimd
        def _(eng):
            pl.emit("pool", eng)

        @block.scalar
        def _(eng):
            pl.emit("act", eng)

        @block.vector
        def _(eng):
            emit_with_weights("dve", eng)

        @block.tensor
        def _(eng):
            emit_with_weights("pe", eng)


def blocks(nc, t, xs, cols, rows, ident, half, eps5, eps6, WT, s_w, n_w, layer_loads, by_tile, buffers):
    from concourse import mybir
    from contextlib import ExitStack
    from itertools import islice
    F32, F32R = mybir.dt.float32, mybir.dt.float32r
    BF16, F16 = mybir.dt.bfloat16, mybir.dt.float16
    ALU, ACT, AX = mybir.AluOpType, mybir.ActivationFunctionType, mybir.AxisListType
    LAYERS, SCALE = (1, 2, 3), HD ** -0.5

    with ExitStack() as stack:
        sb = buffers(stack)
        tile = lambda n: sb(n, [P, 2, 256])

        def stats(n):
            return sb(n + "_st", [P, TT, 6]), sb(n + "_mv", [P, TT, 2]), sb(n + "_rstd", [P, TT])

        x_in, xn_a, xT_a, x_res, res_a = (tile(n) for n in ("x_in", "xn_a", "xT_a", "x_res", "res_a"))
        st_p, st_t, st_k, st_b = stats("p"), stats("t"), stats("k"), stats("b")
        col_a, bias_a, gate_a = sb("col_a", [P, 4]), sb("bias_a", [P, D]), sb("gate_a", [P, D])
        q_hl, k_hl = sb("q_hl", [P, 2, CC, NT], F32R), sb("k_hl", [P, 2, CC, NT], F32R)
        v_f = tile("v_f")
        v_cat = sb("v_cat", [P, TT, NH, VC], BF16)
        q_cat = sb("q_cat", [P, NPAIR, NT], F32R)
        k_cat = sb("k_cat", [P, NPAIR, NT], F32R)
        m_a, mT_a = sb("m_a", [P, TT, NH]), sb("mT_a", [NH, 2, NT], F32R)
        o_sum, o_rc, o_a, oT_a = sb("o_sum", [P, TT, 8, VW]), sb("o_rc", [P, TT, 8]), tile("o_a"), tile("oT_a")
        y_a, x_b = tile("y_a"), tile("x_b")
        p_f = [sb(f"p_f{i}", [P, 1024]) for i in range(2)]
        p_h = [sb(f"p_h{i}", [P, 1024], F16) for i in range(2)]
        p_l = [sb(f"p_l{i}", [P, 1024], F16) for i in range(2)]
        warm = sb("warm", [P, 2])
        xn_b, xT_b, res_b = tile("xn_b"), tile("xT_b"), tile("res_b")
        ctx, ctxn, ctxT = sb("ctx", [NC_TOK, 1, D]), sb("ctxn", [NC_TOK, 1, D]), sb("ctxT", [P, CC, NC_TOK])
        qc_hl, kc_hl = sb("qc_hl", [P, 2, CC, NT], F32R), sb("kc_hl", [P, 2, CC, NC_TOK], F32R)
        vc_f = sb("vc_f", [NC_TOK, D])
        vc_cat = sb("vc_cat", [NC_TOK, NH, VC], BF16)
        qc_cat = sb("qc_cat", [P, NPAIR, NT], F32R)
        kc_cat = sb("kc_cat", [P, NPAIR, CPAD], F32R)
        m_b, mT_b = sb("m_b", [P, TT, NH]), sb("mT_b", [NH, 2, NT], F32R)
        o_b, oT_b, x_c = tile("o_b"), tile("oT_b"), tile("x_c")
        xn_c, xT_c, res_c = tile("xn_c"), tile("xT_c"), tile("res_c")
        col_c, bias_c, gate_c = sb("col_c", [P, 4]), sb("bias_c", [P, D]), sb("gate_c", [P, D])
        h_c, y_c = sb("h_c", [P, MC, NT]), tile("y_c")

        score = Ring(Bank(stack.enter_context(nc.psum_tensor(f"score{i}", [P, 2, 512], F32))) for i in range(2))
        obank = [Bank(stack.enter_context(nc.psum_tensor(f"obank{i}", [P, 2, 256], F32))) for i in range(2)]
        gbank = Ring(Bank(stack.enter_context(nc.psum_tensor(f"gbank{i}", [P, 2, 256], F32))) for i in range(2))
        p_slots = Ring([Slot(), Slot()])
        through = {}
        for ph, mph in ("QA", "KK"):
            for name, width in (("q", NT), ("k", NT if ph == "Q" else NC_TOK)):
                through[ph, name] = nc.dram_tensor(f"via_{ph}_{name}", (2, CC, P, width), F32, kind="Internal").ap()
            through[mph, "m"] = nc.dram_tensor(f"via_{mph}_m", (NH, 2, NT), F32, kind="Internal").ap()
        s_one = stack.enter_context(nc.semaphore("b_const"))

        pl = Pipeline(nc, "b", dict(P=0, Q=1, A=2, V=2, T=3, K=3, B=4, C=5), 3 * NB, stack)
        op, take = pl.op, pl.take
        pl.shared = score.items + obank + gbank.items + p_slots.items
        state = {}

        def W(ph):
            return WT[state["L"][ph] % 2]

        def heads(bank):
            return bank.ap[:, :, :].rearrange("p a (b c) -> p (a b) c", c=64)

        def seq_of(ph, s):
            return s - (state["L"][ph] - 1) * NB

        def empties(bank, ph, mark):
            pl.empties(bank, ph, mark)
            for ring in (score, gbank):
                if bank in ring.held:
                    ring.free(bank)

        def gemm(ph, bank, outs, after, mark):
            after = list(after) + take(bank, ph)
            for i, (o, terms) in enumerate(outs):
                for k, (l, r_) in enumerate(terms):
                    op("pe", ph, lambda e, s, o=o, l=l, r_=r_, k=k, last=len(terms) - 1: e.matmul(
                        o, l, r_, start=(k == 0), stop=(k == last)), after=after,
                       mark=mark if i == len(outs) - 1 and k == len(terms) - 1 else None)
                    after = []
                    yield

        def transposes(ph, bank, src, after, mark):
            for i in range(TT * CC):
                tt, c = divmod(i, CC)
                op("pe", ph, lambda e, s, tt=tt, c=c: e.transpose(
                    bank.ap[:, c, tt * P:(tt + 1) * P], src[:, tt, c * P:(c + 1) * P], ident[:, :]),
                   after=(list(after) + take(bank, ph)) if i == 0 else [], mark=mark if i == 3 else None)

        def load(ph, mark, after, dst, src):
            op("sp", ph, lambda e, s: e.dma_start(dst, src(s)), after=after, mark=mark, dma=1)

        def load_cols(ph, mark, after, dst, at):
            load(ph, mark, after, dst[:, :], lambda s: cols[state["L"][ph]].rearrange(
                "p (b m) -> b p m", b=NB)[seq_of(ph, s), :, at:at + 4])

        def load_row(ph, mark, after, dst, i):
            load(ph, mark, after, dst[:, :], lambda s: rows[state["L"][ph]][
                seq_of(ph, s), i * D:(i + 1) * D].unsqueeze(0).to_broadcast([P, D]))

        def residual(ph, out, x, bias, after):
            op("pool", ph, lambda e, s: e.tensor_tensor(
                out[:, :, :], x[:, :, :], bias(s).unsqueeze(1).to_broadcast([P, TT, D]), ALU.add),
               after=after, mark="res")

        def x_of_layer(ph, after, dst):
            if state["L"][ph] > 1:
                after = after + [f"C.store@-{NB}"]
            load(ph, "x", after, dst[:, :, :], lambda s: by_tile(xs[state["L"][ph] - 1][seq_of(ph, s), :, :]))

        def p_load():
            x_of_layer("P", ["P.xn1@-1"], x_in)
            load_cols("P", "col", ["Q.xT1@-1"], col_a, 0)

        def p_norm():
            e_ = eps5 if state["L"]["P"] == 3 else eps6
            norm_stats(pl, "P", "", x_in, *st_p, e_, half, (P, TT), ["P.x"])
            yield
            norm_apply(pl, "P", "", x_in, *st_p[1:], xn_a, (P, TT), ["Q.xt@-1"])

        def q_start():
            b = gbank.get()
            transposes("Q", b, xn_a, ["P.xn1"], "xt")
            for c in range(CC):
                op("act", "Q", lambda e, s, c=c: e.activation(xT_a[:, c, :], b.ap[:, c, :], ACT.Identity,
                                                             bias=col_a[:, c:c + 1], scale=col_a[:, 2 + c:3 + c]),
                   after=["Q.xt", "P.col", "V.vp@-1"] if c == 0 else [], mark=f"xT{c}")
            empties(b, "Q", "xT1")

        def split(ph, view, dst, at, name, ready):
            w, free = W(ph), [f"{ph}.{name}out@-1"]
            for m in range(CC):
                op("act", ph, lambda e, s, m=m: e.activation(dst[:, 0, m, :], view(m), ACT.Identity,
                                                            bias=w["bcol"][:, at + m:at + m + 1]),
                   after=([ready] + free) if m == 0 else [], mark=f"{name}h{m}")
            for m in range(CC):
                op("dve", ph, lambda e, s, m=m: e.scalar_tensor_tensor(
                    dst[:, 1, m, :], view(m), w["bcol"][:, at + m:at + m + 1],
                    dst[:, 0, m, :].bitcast(F32), ALU.add, ALU.subtract),
                   after=[f"{ph}.{name}h1"] + (free if m == 0 else []), mark=f"{name}l{m}")

        def parts_out(ph, src, name):
            via = through[ph, name]
            op("sp", ph, lambda e, s: e.dma_start(
                via.rearrange("q c p n -> p (q c) n"), src[:, :, :, :].bitcast(F32).rearrange("p q c n -> p (q c) n")),
               after=[f"{ph}.{name}l1", f"{ph}.{name}h1", f"{ph}.{name}cat@-1"], mark=f"{name}out", dma=1)

        def parts_in(ph, dst, width, order, name, free):
            via = through[ph, name]
            for i, part in enumerate(order):
                for c in range(CC):
                    op("sp", ph, lambda e, s, c=c, i=i, part=part: e.dma_start(
                        dst[64 * c + HD * i:64 * c + HD * (i + 1), :, 0:width].bitcast(F32),
                        via[part, c, :, :].rearrange("(j d) n -> d j n", d=HD)),
                       after=([f"{ph}.{name}out", free]) if i + c == 0 else [],
                       mark=f"{name}cat", dma=6)

        def q_project(name, hl, at):
            w, b = W("Q"), gbank.get()
            yield from gemm("Q", b, [(b.ap[:, m, :], [(w["qkv"][:, k, at * D + m * P:at * D + (m + 1) * P],
                                                       xT_a[:, k, :]) for k in range(CC)]) for m in range(CC)],
                            ["Q.xT1"], name + "p")
            split("Q", lambda m: b.ap[:, m, :], hl, 2 * at, name, f"Q.{name}p")
            empties(b, "Q", name + "l1")
            parts_out("Q", hl, name)

        def q_stack():
            parts_in("Q", q_cat, NT, (0, 1, 0), "q", "A.stp7@-1")
            parts_in("Q", k_cat, NT, (0, 0, 1), "k", "A.stp7@-1")

        def v_parts(ph, full, cat, free):
            op("act", ph, lambda e, s: e.activation(cat(0), full, ACT.Copy), after=[f"{ph}.vf"] + free, mark="v1")
            op("pool", ph, lambda e, s: e.tensor_tensor(full, full, cat(0), ALU.subtract),
               after=[f"{ph}.v1"], mark="vr")
            yield
            op("act", ph, lambda e, s: e.activation(cat(1), full, ACT.Copy), after=[f"{ph}.vr"], mark="v2")
            op("pool", ph, lambda e, s: e.tensor_tensor(cat(2), full, cat(1), ALU.subtract),
               after=[f"{ph}.v2"] + free, mark="v3")

        def v_project():
            w, b = W("V"), gbank.get()
            yield from gemm("V", b, [(b.ap[:, tt, :], [(xT_a[:, k, tt * P:(tt + 1) * P], w["qkv"][:, k, 2 * D:3 * D])
                                                       for k in range(CC)]) for tt in range(TT)], ["Q.xT1"], "vp")
            op("dve", "V", lambda e, s: e.tensor_tensor(
                v_f[:, :, :], b.ap[:, :, :], w["bv"][:, :].unsqueeze(1).to_broadcast([P, TT, D]), ALU.add),
               after=["V.vp", "V.v3@-1"], mark="vf")
            empties(b, "V", "vf")

        def v_split():
            yield from v_parts("V", v_f[:, :, :], lambda i: v_cat[:, :, :, VW * i:VW * i + HD].rearrange("p t h d -> p (t h) d"),
                    ["T.pv7@-1"])

        def a_load():
            x_of_layer("A", ["A.res@-1"], x_res)
            load_row("A", "bias", ["A.res@-1"], bias_a, 1)
            load_row("A", "gate", ["T.y@-1"], gate_a, 0)
            residual("A", res_a, x_res, lambda s: bias_a[:, :], ["A.x", "A.bias", "T.xb@-1"])

        def a_plain(i):
            b = scored["A", i] = score.get()
            for tt in range(TT):
                for hf in range(2):
                    r0 = 64 * hf
                    op("pe", "A", lambda e, s, tt=tt, hf=hf, r0=r0: e.matmul(
                        b.ap[:, hf, tt * NT:(tt + 1) * NT], q_cat[r0:r0 + QROWS, i, tt * P:(tt + 1) * P],
                        k_cat[r0:r0 + QROWS, i, :], start=True, stop=True),
                       after=(["Q.qcat", "Q.kcat"] + take(b, "A")) if tt + hf == 0 else [],
                       mark=f"sp{i}" if tt + hf == 2 else None)

        def a_max(i):
            b = scored["A", i]
            op("dve", "A", lambda e, s: e.tensor_reduce(
                m_a[:, :, i::NPAIR].rearrange("p t h -> p h t"),
                b.ap[:, :, :].rearrange("p h (t k) -> p h t k", t=TT), AX.X, ALU.max),
               after=[f"A.sp{i}", "A.mt@-1"], mark=f"mx{i}")
            empties(b, "A", f"mx{i}")

        def max_rows(ph, m, mT, q_dst, last):
            b = gbank.get()
            for tt in range(TT):
                op("pe", ph, lambda e, s, tt=tt: e.transpose(b.ap[0:NH, 0, tt * P:(tt + 1) * P], m[:, tt, :],
                                                            ident[:, :]),
                   after=([f"{ph}.{last}"] + take(b, ph)) if tt == 0 else [], mark="mt" if tt else None)
            op("act", ph, lambda e, s: e.activation(mT[:, 0, :], b.ap[0:NH, 0, :], ACT.Copy),
               after=[f"{ph}.mt", f"{ph}.mout@-1"], mark="mh")
            op("dve", ph, lambda e, s: e.tensor_tensor(mT[:, 1, :], b.ap[0:NH, 0, :], mT[:, 0, :].bitcast(F32),
                                                      ALU.subtract),
               after=[f"{ph}.mh", f"{ph}.mout@-1"], mark="ml")
            empties(b, ph, "ml")
            via = through[ph, "m"]
            op("sp", ph, lambda e, s: e.dma_start(via, mT[:, :, :].bitcast(F32)),
               after=[f"{ph}.ml", f"{ph}.mh", f"{ph}.mrow@-1"], mark="mout", dma=1)
            for c in range(2):
                op("sp", ph, lambda e, s, c=c: e.dma_start(
                    q_dst[64 * c + QROWS:64 * c + QROWS + 2, :, :].bitcast(F32),
                    via[8 * c:8 * c + 8, :, :].rearrange("i q n -> q i n")),
                   after=[f"{ph}.mout"] if c == 0 else [], mark="mrow", dma=2)

        def exp_table():
            op("act", "A", lambda e, s: e.activation(warm[:, 1:2], half[:, 0:1], ACT.Exp))

        def slot_wait(slot, ph, what):
            if slot.last is None or ph not in pl.active:
                return []
            p1, p2, name = slot.last
            other = p1 if what == "pl" else p2
            return [f"{other}.{what}{name}@{slot.when - pl.iteration - pl.lags[p1] + pl.lags[ph]}"]

        def weights(ph, i):
            b, rows_ = scored[ph, i], (P if ph == "A" else NC_TOK)
            pv_ph = "T" if (ph, i) == ("A", NPAIR - 1) else ph
            slot = p_slots.get()
            p_slots.free(slot)
            n = p_slots.items.index(slot)
            pf, phi, plo = p_f[n], p_h[n], p_l[n]
            made, used = slot_wait(slot, ph, "pl"), slot_wait(slot, ph, "pv")
            op("act", ph, lambda e, s: e.activation(pf[0:rows_, :], b.ap[0:rows_, :, :].rearrange("p h n -> p (h n)"),
                                                   ACT.Exp, scale=SCALE),
               after=[f"{ph}.stp{i}"] + made, mark=f"ex{i}")
            empties(b, ph, f"ex{i}")
            op("act", ph, lambda e, s: e.activation(phi[0:rows_, :], pf[0:rows_, :], ACT.Copy, scale=PSCALE),
               after=[f"{ph}.ex{i}"] + used, mark=f"ph{i}")
            op("dve", ph, lambda e, s: e.scalar_tensor_tensor(plo[0:rows_, :], pf[0:rows_, :], PSCALE,
                                                             phi[0:rows_, :], ALU.mult, ALU.subtract),
               after=[f"{ph}.ph{i}"] + used, mark=f"pl{i}")
            if ph in pl.active:
                slot.last, slot.when = (ph, pv_ph, i), pl.iteration
            slot_of[ph, i] = n

        slot_of, scored = {}, {}

        def a_scores(i):
            b = scored["A", i] = score.get()
            for kc in range(TT):
                for hf in range(2):
                    r0 = 64 * hf
                    op("pe", "A", lambda e, s, kc=kc, hf=hf, r0=r0: e.matmul(
                        b.ap[:, hf, kc * NT:(kc + 1) * NT], k_cat[r0:r0 + QROWS + 2, i, kc * P:(kc + 1) * P],
                        q_cat[r0:r0 + QROWS + 2, i, :], start=True, stop=True),
                       after=(["A.mrow"] + take(b, "A")) if kc + hf == 0 else [],
                       mark=f"stp{i}" if kc + hf == 2 else None)

        def a_pv(ph, i):
            slot, j = slot_of["A", i], i % 4
            for tt in range(TT):
                ob = obank[tt]
                w = take(ob, ph) if j == 0 else []
                for hf in range(2):
                    terms = [(kc, src) for kc in range(TT) for src in (p_h, p_l)]
                    for n_, (kc, src) in enumerate(terms):
                        at = hf * 512 + kc * NT + tt * P
                        op("pe", ph, lambda e, s, hf=hf, kc=kc, src=src, at=at, n_=n_, ob=ob: e.matmul(
                            heads(ob)[:, 4 * hf + j, 0:VC], src[slot][:, at:at + P], v_cat[:, kc, 8 * hf + i, :],
                            start=(n_ == 0), stop=(n_ == 3)),
                           after=([f"A.pl{i}", f"A.ph{i}", "V.v1", "V.v2", "V.v3"] + w) if n_ + hf == 0 else [],
                           mark=f"pv{i}" if tt + hf == 2 and n_ == 3 else None)

        def out_heads(ph, u, o, last, free):
            for tt in range(TT):
                ob = obank[tt]
                op("dve", ph, lambda e, s, tt=tt, ob=ob: e.tensor_reduce(
                    o_sum[:, tt, :, :], heads(ob)[:, :, 0:VC].rearrange("p g (q e) -> p g e q", q=VP), AX.X, ALU.add),
                   after=[f"{ph}.{last}"], mark=f"os{u}{tt}")
                empties(ob, ph, f"os{u}{tt}")
            yield
            for tt in range(TT):
                op("dve", ph, lambda e, s, tt=tt: e.reciprocal(o_rc[:, tt, :], o_sum[:, tt, :, HD]),
                   after=[f"{ph}.os{u}{tt}"], mark=f"rc{u}{tt}")
            for tt in range(TT):
                op("dve", ph, lambda e, s, tt=tt: e.tensor_tensor(
                    o[:, tt, :].rearrange("p (h f) -> p h f", h=2)[:, :, 4 * HD * u:4 * HD * (u + 1)]
                     .rearrange("p h (j d) -> p h j d", d=HD),
                    o_sum[:, tt, :, 0:HD].rearrange("p (h j) d -> p h j d", h=2),
                    o_rc[:, tt, :].rearrange("p (h j) -> p h j", h=2).unsqueeze(3).to_broadcast([P, 2, 4, HD]),
                    ALU.mult),
                   after=[f"{ph}.rc{u}{tt}"] + (free if tt == 0 else []), mark=f"on{u}{tt}")

        def turn_heads(ph, o, oT, ready):
            b = gbank.get()
            transposes(ph, b, o, ready, "ot")
            op("act", ph, lambda e, s: e.activation(oT[:, :, :], b.ap[:, :, :], ACT.Copy),
               after=[f"{ph}.ot", f"{ph}.op@-1"], mark="oT")
            empties(b, ph, "oT")

        def project(ph, oT, w):
            b = gbank.get()
            yield from gemm(ph, b, [(b.ap[:, tt, :], [(oT[:, k, tt * P:(tt + 1) * P], w[:, k, :])
                                                      for k in range(CC)]) for tt in range(TT)], [f"{ph}.oT"], "op")
            return b

        def t_project():
            b = yield from project("T", oT_a, W("T")["o"])
            op("dve", "T", lambda e, s: e.tensor_tensor(
                y_a[:, :, :], b.ap[:, :, :], gate_a[:, :].unsqueeze(1).to_broadcast([P, TT, D]), ALU.mult),
               after=["T.op", "A.gate"], mark="y")
            empties(b, "T", "y")
            op("pool", "T", lambda e, s: e.tensor_tensor(x_b[:, :, :], y_a[:, :, :], res_a[:, :, :], ALU.add),
               after=["T.y", "A.res", "K.res@-1"] + (["K.xt@-1"] if state["L"]["T"] == 3 else []), mark="xb")

        def t_norm():
            if state["L"]["T"] < 3:
                norm_stats(pl, "T", "n", x_b, *st_t, eps6, half, (P, TT), ["T.xb"], group="Tn")
                yield
                norm_apply(pl, "T", "n", x_b, *st_t[1:], xn_b, (P, TT), ["K.xt@-1"], group="Tn")

        def k_load():
            load("K", "ctx", ["K.ct@-1"] + (["K.cxn0@-1"] if state["L"]["K"] == 1 else []), ctx[:, 0, :],
                 lambda s: t["ctx_1024"][seq_of("K", s), :, :])

        def k_norm():
            if state["L"]["K"] == 1:
                norm_stats(pl, "K", "c", ctx, *st_k, eps6, half, (NC_TOK, 1), ["K.ctx"], group="Kn")
                yield
                norm_apply(pl, "K", "c", ctx, *st_k[1:], ctxn, (NC_TOK, 1), ["K.ct@-1"], group="Kn")

        def k_context():
            cs, cr = (ctxn, "K.cxn0") if state["L"]["K"] == 1 else (ctx, "K.ctx")
            b = gbank.get()
            for c in range(CC):
                op("pe", "K", lambda e, s, c=c: e.transpose(b.ap[:, 0, c * NC_TOK:(c + 1) * NC_TOK],
                                                           cs[:, 0, c * P:(c + 1) * P], ident[0:NC_TOK, 0:NC_TOK]),
                   after=([cr] + take(b, "K")) if c == 0 else [], mark="ct" if c else None)
            op("act", "K", lambda e, s: e.activation(
                ctxT[:, :, :], b.ap[:, 0, 0:CC * NC_TOK].rearrange("p (c k) -> p c k", c=CC), ACT.Copy),
               after=["K.ct", "K.vp@-1"], mark="cT")
            empties(b, "K", "cT")

        def k_kv():
            w, b = W("K"), gbank.get()
            kv_ = lambda m: b.ap[:, 0, m * NC_TOK:(m + 1) * NC_TOK]
            yield from gemm("K", b, [(kv_(m), [(w["kvc"][:, k, m * P:(m + 1) * P], ctxT[:, k, :])
                                               for k in range(CC)]) for m in range(CC)] +
                            [(b.ap[0:NC_TOK, 1, :], [(ctxT[:, k, :], w["kvc"][:, k, D:2 * D]) for k in range(CC)])],
                            ["K.cT"], "vp")
            split("K", kv_, kc_hl, 6, "k", "K.vp")
            op("dve", "K", lambda e, s: e.tensor_tensor(vc_f[:, :], b.ap[0:NC_TOK, 1, :], w["bvc"][0:NC_TOK, :],
                                                       ALU.add), after=["K.v3@-1"], mark="vf")
            empties(b, "K", "vf")
            parts_out("K", kc_hl, "k")
            parts_in("K", kc_cat, NC_TOK, (0, 0, 1), "k", "B.stp3@-1")

        def k_v_split():
            yield from v_parts("K", vc_f[:, :], lambda i: vc_cat[:, :, VW * i:VW * i + HD], ["B.pv3@-1"])

        def k_start():
            w = W("K")
            src, ready = (xn_b, ["T.nxn1"]) if state["L"]["K"] < 3 else (x_b, ["T.xb"])
            residual("K", res_b, x_b, lambda s: w["boc"][:, :], ["T.xb", "B.xc@-1"])
            b = gbank.get()
            transposes("K", b, src, ready, "xt")
            op("act", "K", lambda e, s: e.activation(xT_b[:, :, :], b.ap[:, :, :], ACT.Copy),
               after=["K.xt", "K.qp@-1"], mark="xT")
            empties(b, "K", "xT")

        def k_q():
            w, b = W("K"), gbank.get()
            yield from gemm("K", b, [(b.ap[:, m, :], [(w["qc"][:, k, m * P:(m + 1) * P], xT_b[:, k, :])
                                                      for k in range(CC)]) for m in range(CC)], ["K.xT"], "qp")
            split("K", lambda m: b.ap[:, m, :], qc_hl, 4, "q", "K.qp")
            empties(b, "K", "ql1")
            parts_out("K", qc_hl, "q")
            parts_in("K", qc_cat, NT, (0, 1, 0), "q", "B.stp3@-1")

        def k_max(i):
            for hf, b in enumerate((gbank.get(), gbank.get())):
                view = b.ap[:, :, :].rearrange("p t (j k) -> p j t k", j=2)
                for j in range(2):
                    for tt in range(TT):
                        r0 = 64 * hf
                        op("pe", "K", lambda e, s, j=j, tt=tt, hf=hf, r0=r0, view=view: e.matmul(
                            view[:, j, tt, 0:CPAD], qc_cat[r0:r0 + QROWS, 2 * i + j, tt * P:(tt + 1) * P],
                            kc_cat[r0:r0 + QROWS, 2 * i + j, :], start=True, stop=True),
                           after=(["K.qcat", "K.kcat"] + take(b, "K")) if j + tt == 0 else [],
                           mark=f"sp{i}{hf}" if j + tt == 2 else None)
                op("dve", "K", lambda e, s, hf=hf, view=view: e.tensor_reduce(
                    m_b[:, :, 8 * hf + 2 * i:8 * hf + 2 * i + 2].rearrange("p t j -> p j t"),
                    view[:, :, :, 0:NC_TOK], AX.X, ALU.max),
                   after=[f"K.sp{i}{hf}", "K.mt@-1"], mark=f"mx{i}{hf}")
                empties(b, "K", f"mx{i}{hf}")

        def b_scores(i):
            b = scored["B", i] = score.get()
            for j in range(2):
                for hf in range(2):
                    r0 = 64 * hf
                    op("pe", "B", lambda e, s, j=j, hf=hf, r0=r0: e.matmul(
                        b.ap[0:NC_TOK, hf, j * NT:(j + 1) * NT], kc_cat[r0:r0 + QROWS + 2, 2 * i + j, 0:NC_TOK],
                        qc_cat[r0:r0 + QROWS + 2, 2 * i + j, :], start=True, stop=True),
                       after=(["K.mrow"] + take(b, "B")) if j + hf == 0 else [],
                       mark=f"stp{i}" if j + hf == 2 else None)

        def b_pv(i):
            slot = slot_of["B", i]
            for tt in range(TT):
                ob = obank[tt]
                w = take(ob, "B") if i % 2 == 0 else []
                for j in range(2):
                    jj = (2 * i + j) % 4
                    for hf in range(2):
                        for n_, src in enumerate((p_h, p_l)):
                            at = hf * 512 + j * NT + tt * P
                            op("pe", "B", lambda e, s, hf=hf, src=src, at=at, n_=n_, ob=ob, jj=jj, j=j: e.matmul(
                                heads(ob)[:, 4 * hf + jj, 0:VC], src[slot][0:NC_TOK, at:at + P],
                                vc_cat[:, 8 * hf + 2 * i + j, :], start=(n_ == 0), stop=(n_ == 1)),
                               after=([f"B.pl{i}", f"B.ph{i}", "K.v1", "K.v2", "K.v3"] + w) if j + n_ + hf == 0 else [],
                               mark=f"pv{i}" if tt + j + hf == 3 and n_ == 1 else None)

        def b_project():
            b = yield from project("B", oT_b, W("B")["oc"])
            op("dve", "B", lambda e, s: e.tensor_tensor(x_c[:, :, :], b.ap[:, :, :], res_b[:, :, :], ALU.add),
               after=["B.op", "K.res", "C.res@-1"], mark="xc")
            empties(b, "B", "xc")

        def b_norm():
            e_ = eps5 if state["L"]["B"] == 3 else eps6
            norm_stats(pl, "B", "n", x_c, *st_b, e_, half, (P, TT), ["B.xc"])
            yield
            norm_apply(pl, "B", "n", x_c, *st_b[1:], xn_c, (P, TT), ["C.xt@-1"])

        def b_load():
            load_cols("B", "col", ["C.xT1@-1"], col_c, 4)
            load_row("B", "bias", ["C.res@-1"], bias_c, 3)

        def c_start():
            residual("C", res_c, x_c, lambda s: bias_c[:, :], ["B.xc", "B.bias", "C.yo@-1"])
            b = gbank.get()
            transposes("C", b, xn_c, ["B.nxn1"], "xt")
            for c in range(CC):
                op("act", "C", lambda e, s, c=c: e.activation(xT_c[:, c, :], b.ap[:, c, :], ACT.Identity,
                                                             bias=col_c[:, c:c + 1], scale=col_c[:, 2 + c:3 + c]),
                   after=["C.xt", "B.col", f"C.hp{MC // 2 - 1}@-1"] if c == 0 else [], mark=f"xT{c}")
            empties(b, "C", "xT1")

        def c_up():
            w = W("C")
            gelu = ACT.Gelu if state["L"]["C"] == 3 else ACT.Gelu_apprx_tanh
            for i in range(MC // 2):
                b = gbank.get()
                yield from gemm("C", b, [(b.ap[:, j, :], [(w["w1"][:, k, (2 * i + j) * P:(2 * i + j + 1) * P],
                                                           xT_c[:, k, :]) for k in range(CC)]) for j in range(2)],
                                ["C.xT1"], f"hp{i}")
                for j in range(2):
                    m = 2 * i + j
                    op("act", "C", lambda e, s, j=j, m=m, b=b: e.activation(
                        h_c[:, m, :], b.ap[:, j, :], gelu, bias=w["bcol"][:, 8 + m:9 + m]),
                       after=[f"C.hp{i}", "C.down@-1"] if j == 0 else [], mark=f"h{m}")
                empties(b, "C", f"h{2 * i + 1}")

        def c_down():
            w, b = W("C"), gbank.get()
            yield from gemm("C", b, [(b.ap[:, tt, :], [(h_c[:, m, tt * P:(tt + 1) * P], w["w2"][:, m, :])
                                                       for m in range(MC)]) for tt in range(TT)],
                            [f"C.h{MC - 1}"], "down")
            op("dve", "C", lambda e, s: e.tensor_tensor(
                y_c[:, :, :], b.ap[:, :, :], gate_c[:, :].unsqueeze(1).to_broadcast([P, TT, D]), ALU.mult),
               after=["C.down", "C.gate", "C.store@-1"], mark="y")
            empties(b, "C", "y")
            op("pool", "C", lambda e, s: e.tensor_tensor(y_c[:, :, :], y_c[:, :, :], res_c[:, :, :], ALU.add),
               after=["C.y", "C.res"], mark="yo")
            L = state["L"]["C"]
            op("sp", "C", lambda e, s: e.dma_start(by_tile(xs[L][seq_of("C", s), :, :]), y_c[:, :, :]),
               after=["C.yo"], mark="store", dma=1)

        def iteration(lo, hi):
            pl.iteration = lo
            act = [ph for ph in "PQVATKBC" if 0 <= lo - pl.lags[ph] < 3 * NB]
            pl.begin(act)
            state["L"] = {ph: (lo - pl.lags[ph]) // NB + 1 for ph in act}
            fixed = dict(state["L"])
            for ring in (score, gbank, p_slots):
                ring.rewind()

            def on(ph, step, *args):
                if ph in act:
                    for _ in step(*args) or ():
                        pass

            def some(ph, steps, n):
                if ph in act:
                    for _ in (steps if n is None else islice(steps, n)):
                        pass

            mlp_up, mlp_down = c_up(), c_down()
            q_pieces, k_pieces = q_project("q", q_hl, 0), q_project("k", k_hl, 1)
            v_pieces, v_split_pieces = v_project(), v_split()
            a_proj, a_norm_pieces = t_project(), t_norm()
            ctx_norm, ctx_kv, ctx_v_split, cross_q = k_norm(), k_kv(), k_v_split(), k_q()
            b_proj, b_norm_pieces, p_norm_pieces = b_project(), b_norm(), p_norm()

            on("K", k_load)
            on("C", load_row, "C", "gate", ["C.y@-1"], gate_c, 2)
            on("B", b_scores, 0)
            on("B", b_scores, 1)
            on("T", a_pv, "T", 7)
            on("T", out_heads, "T", 1, o_a, "pv7", [])
            on("B", weights, "B", 0)
            some("V", v_pieces, 2)

            on("B", b_scores, 2)
            some("V", v_pieces, 2)
            on("B", weights, "B", 1)
            some("V", v_pieces, None)
            on("T", turn_heads, "T", o_a, oT_a, ["A.on01", "T.on11"])
            on("B", b_pv, 0)

            on("B", b_scores, 3)
            some("T", a_proj, 2)
            on("B", b_pv, 1)
            some("T", a_proj, 2)
            on("B", weights, "B", 2)
            on("B", out_heads, "B", 0, o_b, "pv1", ["B.ot@-1"])

            on("A", a_plain, 0)
            some("T", a_proj, None)
            on("B", b_pv, 2)
            on("B", weights, "B", 3)
            on("C", c_start)
            some("K", ctx_norm, 1)
            on("A", a_plain, 1)
            some("T", a_norm_pieces, 1)
            some("C", mlp_up, 2)
            on("A", a_max, 0)
            on("B", b_pv, 3)
            some("C", mlp_up, 2)
            some("K", ctx_norm, None)
            on("B", out_heads, "B", 1, o_b, "pv3", [])
            gbank.lend(obank)

            on("A", a_plain, 2)
            on("A", a_max, 1)
            on("K", k_context)
            some("T", a_norm_pieces, None)
            some("C", mlp_up, 2)
            some("V", v_split_pieces, 1)
            on("B", turn_heads, "B", o_b, oT_b, ["B.on01", "B.on11"])
            some("C", mlp_up, 2)

            on("A", a_plain, 3)
            on("K", k_start)
            on("A", a_max, 2)
            some("K", ctx_kv, 6)

            on("A", a_plain, 4)
            on("A", a_max, 3)
            some("K", ctx_kv, None)
            some("K", cross_q, 4)
            some("V", v_split_pieces, None)

            on("A", a_plain, 5)
            on("A", a_max, 4)
            some("K", cross_q, None)
            some("C", mlp_up, 4)

            on("A", a_plain, 6)
            on("A", a_max, 5)
            some("K", ctx_v_split, 1)
            some("B", b_proj, 4)

            on("A", a_plain, 7)
            on("A", a_max, 6)

            on("A", a_max, 7)
            some("C", mlp_up, 2)
            on("Q", q_start)
            on("A", max_rows, "A", m_a, mT_a, q_cat, "mx7")
            some("C", mlp_up, None)
            some("B", b_proj, None)
            some("Q", q_pieces, 4)
            some("Q", q_pieces, None)
            some("Q", k_pieces, 4)
            on("K", k_max, 0)
            some("Q", k_pieces, None)
            some("K", ctx_v_split, None)
            on("A", exp_table)
            on("K", k_max, 1)
            on("P", p_load)
            on("K", k_max, 2)
            on("A", a_load)
            on("A", a_scores, 0)
            on("K", k_max, 3)
            gbank.give_back(obank)
            for i in range(NPAIR):
                if i < NPAIR - 1:
                    on("A", a_scores, i + 1)
                on("A", weights, "A", i)
                some("C", mlp_down, 2 if i else 0)
                if i == 3:
                    on("K", max_rows, "K", m_b, mT_b, qc_cat, "mx31")
                if i in (1, 2):
                    some("B", b_norm_pieces, 1)
                if i in (3, 6):
                    some("P", p_norm_pieces, 1)
                if i:
                    on("A", a_pv, "A", i - 1)
                if i == 4:
                    first_heads = out_heads("A", 0, o_a, "pv3", ["T.ot@-1"])
                    some("A", first_heads, 1)
                if i == 5:
                    some("A", first_heads, None)
                    on("B", b_load)
            on("Q", q_stack)
            some("C", mlp_down, None)
            for o in pl.ops:
                o.emit = bind(o.emit, fixed)
            pl.end(lo, hi)

        def bind(emit, layers):
            def f(e, s):
                state["L"] = layers
                return emit(e, s)
            return f

        n, last = 0, 3 * NB + max(pl.lags.values())
        while n < last:
            lo, hi = n, n + 1
            if n < 3 * NB and n % NB == 6:
                hi = n // NB * NB + NB
            iteration(lo, hi)
            n = hi

        block = stack.enter_context(nc.Block())

        def emit_with_weights(name, eng, waits):
            segs = pl.segments
            for seg in segs:
                for L in LAYERS:
                    if seg[0] == NB * (L - 1):
                        waits(eng, L)
                pl.segments = [seg]
                pl.emit(name, eng)
            pl.segments = segs

        def wait_weights(eng, L):
            eng.wait_ge(s_w[L], n_w[L])

        @block.sync
        def _(eng):
            eng.wait_ge(s_one, 3)
            segs = pl.segments
            for seg in segs:
                if seg[0] == 3:
                    start(eng, layer_loads(2))
                if seg[0] == NB + 6:
                    for mark in ("C.down", "B.op", "T.op", "V.vf", "K.res", "Q.ql1", "Q.kl1", "K.ql1", "K.kl1",
                                 "K.vf", f"C.h{MC - 1}"):
                        eng.wait_ge(pl.sem(pl.marks[mark].group), pl.value(mark, NB - 1))
                    start(eng, layer_loads(3))
                pl.segments = [seg]
                pl.emit("sp", eng)
            pl.segments = segs
            eng.wait_ge(pl.sem("C.store"), 16 * 3 * NB)

        @block.gpsimd
        def _(eng):
            emit_with_weights("pool", eng, wait_weights)

        @block.scalar
        def _(eng):
            emit_with_weights("act", eng, wait_weights)

        @block.vector
        def _(eng):
            eng.memset(k_cat[:, :, :].bitcast(F32), -1.0)
            eng.memset(kc_cat[:, :, :].bitcast(F32), -1.0).then_inc(s_one, 1)
            eng.memset(v_cat[:, :, :, :].rearrange("p t h c -> p (t h c)"), 0.0)
            eng.memset(vc_cat[:, :, :].rearrange("p h c -> p (h c)"), 0.0).then_inc(s_one, 1)
            eng.wait_ge(s_one, 2)
            eng.memset(v_cat[:, :, :, HD:HD + 1], 1.0)
            eng.memset(vc_cat[:, :, HD:HD + 1], 1.0).then_inc(s_one, 1)
            emit_with_weights("dve", eng, wait_weights)

        @block.tensor
        def _(eng):
            eng.wait_ge(s_one, 3)
            emit_with_weights("pe", eng, wait_weights)


def kernel(**inputs):
    import concourse.bacc as bacc
    from concourse import mybir
    from concourse.bass_utils import run_bass_kernel_spmd

    nc = bacc.Bacc("TRN2", target_bir_lowering=False, num_devices=1)
    arrays, t = {}, {}
    for name in inputs:
        a = np.ascontiguousarray(inputs[name])
        arrays[f"in_{name}_dram"] = a
        t[name] = nc.dram_tensor(f"in_{name}_dram", a.shape, mybir.dt.from_np(a.dtype), kind="ExternalInput").ap()
    t["out"] = nc.dram_tensor("out_0_dram", (NB, NT, D), mybir.dt.float32, kind="ExternalOutput").ap()
    build(nc, t)
    r = run_bass_kernel_spmd(nc, [arrays], core_ids=[0])
    return r.results[0]["out_0_dram"]
```
